# Optimizing a Trainium2 kernel written in Bass

```python
import numpy as np
import jax
import jax.numpy as jnp

def _softmax(x, axis=-1):
    return jax.nn.softmax(x, axis=axis)

def _gelu(x):
    return jax.nn.gelu(x, approximate=True)

def _silu(x):
    return jax.nn.silu(x)

def _sigmoid(x):
    return jax.nn.sigmoid(x)

def _layernorm(x, axis=-1, eps=1e-05):
    m = jnp.mean(x, axis=axis, keepdims=True)
    v = jnp.var(x, axis=axis, keepdims=True)
    return (x - m) / jnp.sqrt(v + eps)

def _scatter_add(tgt, idx, src, axis=0):
    return tgt.at[idx].add(src)

def _segment_sum(src, seg, n):
    return jax.ops.segment_sum(src, seg, n)
kernel_name = 'mk_perceiver_d1_seqx_r2_2d3ca2'

def setup_inputs(seed: int=0):
    np.random.seed(seed)
    _w = jnp.asarray

    def _rec_inputs():
        import jax
        import jax.numpy as jnp
        _rk = jax.random.key(seed)
        x = -0.0002928 + 1 * jax.random.normal(jax.random.fold_in(_rk, 1), (64, 64, 512), jnp.float32)
        _lenS = 64 - jax.random.randint(jax.random.fold_in(_rk, 7), (64,), 0, max(1, 64 // 4) + 1, jnp.int32)
        _lenS2 = 512 - jax.random.randint(jax.random.fold_in(_rk, 8), (64,), 0, max(1, 512 // 4) + 1, jnp.int32)
        _ctx_1024P = jax.random.normal(jax.random.fold_in(_rk, 11), (64, 16, 512), jnp.float32)
        _ctx_1024c = jax.random.dirichlet(jax.random.fold_in(_rk, 511), 0.3 * jnp.ones((16,), jnp.float32), (64, 512))
        _ctx_1024t = jnp.einsum('bsk,bkd->bsd', _ctx_1024c, _ctx_1024P)
        _ctx_1024t = _ctx_1024t * jax.lax.rsqrt(jnp.mean(jnp.square(_ctx_1024t)) + 1e-12) * 0.953939
        ctx_1024 = -1.39393e-06 + 0.999914 * (_ctx_1024t + 0.3 * jax.random.normal(jax.random.fold_in(_rk, 611), (64, 512, 512), jnp.float32))
        _validS = jnp.arange(64)[None, :] < _lenS[:, None]
        _validS2 = jnp.arange(512)[None, :] < _lenS2[:, None]
        _causal = jnp.tril(jnp.ones((64, 64), dtype=bool))
        mask_1x1xSxS2_bk1 = jnp.broadcast_to(_validS2[0:1, None, None, :], (1, 1, 64, 512))
        return (x, ctx_1024, mask_1x1xSxS2_bk1)
    x, ctx_1024, mask_1x1xSxS2_bk1 = _rec_inputs()

    def _L0_xattn_setup():
        import jax, jax.numpy as jnp
        import numpy as np
        HEADS = 16
        D_MODEL = 512
        D_K = D_MODEL // HEADS
        B, S = (2, 1024)
        key = jax.random.key(seed)
        k = jax.random.split(key, 7)
        Q = jax.random.normal(k[0], (B, S, D_MODEL), dtype=jnp.float32)
        K = jax.random.normal(k[1], (B, S, D_MODEL), dtype=jnp.float32)
        V = jax.random.normal(k[2], (B, S, D_MODEL), dtype=jnp.float32)
        mask = jnp.triu(jnp.ones((S, S), dtype=bool), k=1)[None, None, :, :]
        scale = 1.0 / np.sqrt(D_MODEL)
        W_Q = jax.random.normal(k[3], (D_MODEL, D_MODEL), dtype=jnp.float32) * scale
        W_K = jax.random.normal(k[4], (D_MODEL, D_MODEL), dtype=jnp.float32) * scale
        W_V = jax.random.normal(k[5], (D_MODEL, D_MODEL), dtype=jnp.float32) * scale
        W_O = jax.random.normal(k[6], (D_MODEL, D_MODEL), dtype=jnp.float32) * scale
        return {'Q': Q, 'K': K, 'V': V, 'mask': mask, 'W_Q': W_Q, 'W_K': W_K, 'W_V': W_V, 'W_O': W_O}
    _L0_xattn_all = _L0_xattn_setup()
    _L0_xattn_in = {k: v for k, v in _L0_xattn_all.items() if k in ('W_Q', 'W_K', 'W_V', 'W_O')}
    del _L0_xattn_all

    def _L0_attn_setup():
        import jax, jax.numpy as jnp
        import numpy as np
        EMBED_DIM = 512
        NUM_HEADS = 16
        TOP_K = 64
        key = jax.random.key(seed)
        ks = jax.random.split(key, 9)
        B, S, E = (2, 1024, EMBED_DIM)
        sc = 1.0 / np.sqrt(E)
        inp = {'x': jax.random.normal(ks[0], (B, S, E), dtype=jnp.float32)}
        names = ['Wq', 'bq', 'Wk', 'bk', 'Wv', 'bv', 'Wo', 'bo']
        for i, n in enumerate(names):
            if n.startswith('W'):
                inp[n] = jax.random.normal(ks[i + 1], (E, E), dtype=jnp.float32) * sc
            else:
                inp[n] = jnp.zeros((E,), dtype=jnp.float32)
        return inp
    _L0_attn_all = _L0_attn_setup()
    _L0_attn_in = {k: v for k, v in _L0_attn_all.items() if k in ('Wq', 'bq', 'Wk', 'bk', 'Wv', 'bv', 'Wo', 'bo')}
    del _L0_attn_all

    def _L0_ffn_setup():
        import jax, jax.numpy as jnp
        import numpy as np
        EPS = 1e-05

        def _quantize(W):
            gamma = jnp.mean(jnp.abs(W))
            return jnp.clip(jnp.round(W / (gamma + EPS)), -1.0, 1.0)
        key = jax.random.key(seed)
        k_x, k_w1, k_b1, k_w2, k_b2 = jax.random.split(key, 5)
        n_embd = 512
        d_ff = 4 * n_embd
        B, S = (4, 2048)
        bound1 = 1.0 / np.sqrt(n_embd)
        bound2 = 1.0 / np.sqrt(d_ff)
        x = jax.random.normal(k_x, (B, S, n_embd), dtype=jnp.float32)
        W1 = jax.random.uniform(k_w1, (d_ff, n_embd), jnp.float32, -bound1, bound1)
        b1 = jax.random.uniform(k_b1, (d_ff,), jnp.float32, -bound1, bound1)
        W2 = jax.random.uniform(k_w2, (n_embd, d_ff), jnp.float32, -bound2, bound2)
        b2 = jax.random.uniform(k_b2, (n_embd,), jnp.float32, -bound2, bound2)
        return {'x': x, 'W1': W1, 'b1': b1, 'W2': W2, 'b2': b2}
    _L0_ffn_all = _L0_ffn_setup()
    _L0_ffn_in = {k: v for k, v in _L0_ffn_all.items() if k in ('W1', 'b1', 'W2', 'b2')}
    del _L0_ffn_all
    return {'x': x, 'ctx_1024': ctx_1024, 'mask_1x1xSxS2_bk1': mask_1x1xSxS2_bk1, 'L0_xattn_W_Q': _L0_xattn_in['W_Q'], 'L0_xattn_W_K': _L0_xattn_in['W_K'], 'L0_xattn_W_V': _L0_xattn_in['W_V'], 'L0_xattn_W_O': _L0_xattn_in['W_O'], 'L0_attn_Wq': _L0_attn_in['Wq'], 'L0_attn_bq': _L0_attn_in['bq'], 'L0_attn_Wk': _L0_attn_in['Wk'], 'L0_attn_bk': _L0_attn_in['bk'], 'L0_attn_Wv': _L0_attn_in['Wv'], 'L0_attn_bv': _L0_attn_in['bv'], 'L0_attn_Wo': _L0_attn_in['Wo'], 'L0_attn_bo': _L0_attn_in['bo'], 'L0_ffn_W1': _L0_ffn_in['W1'], 'L0_ffn_b1': _L0_ffn_in['b1'], 'L0_ffn_W2': _L0_ffn_in['W2'], 'L0_ffn_b2': _L0_ffn_in['b2']}

def reference(x, ctx_1024, mask_1x1xSxS2_bk1, L0_xattn_W_Q, L0_xattn_W_K, L0_xattn_W_V, L0_xattn_W_O, L0_attn_Wq, L0_attn_bq, L0_attn_Wk, L0_attn_bk, L0_attn_Wv, L0_attn_bv, L0_attn_Wo, L0_attn_bo, L0_ffn_W1, L0_ffn_b1, L0_ffn_W2, L0_ffn_b2):
    import jax
    import jax.numpy as jnp

    def _L0_xattn_ref(Q, K, V, mask, W_Q, W_K, W_V, W_O):
        import jax, jax.numpy as jnp
        import numpy as np
        HEADS = 16
        D_MODEL = 512
        D_K = D_MODEL // HEADS
        B, S = (2, 1024)
        q = Q @ W_Q.T
        k = K @ W_K.T
        v = V @ W_V.T

        def split(x):
            b, s, _ = x.shape
            return x.reshape(b, s, HEADS, D_K).transpose(0, 2, 1, 3)
        q, k, v = (split(q), split(k), split(v))
        e = jnp.einsum('bhqd,bhkd->bhqk', q, k) / jnp.sqrt(jnp.float32(D_K))
        e = jnp.where(mask, -jnp.inf, e)
        w = jax.nn.softmax(e, axis=-1)
        a = jnp.einsum('bhqk,bhkd->bhqd', w, v)
        b = a.shape[0]
        heads = a.transpose(0, 2, 1, 3).reshape(b, -1, D_MODEL)
        return heads @ W_O.T

    def _L0_attn_ref(x, Wq, bq, Wk, bk, Wv, bv, Wo, bo):
        import jax, jax.numpy as jnp
        import numpy as np
        EMBED_DIM = 512
        NUM_HEADS = 16
        TOP_K = 64
        B, S, E = x.shape
        H = NUM_HEADS
        D = E // H
        k = min(TOP_K, S)

        def proj(W, b):
            return (x @ W.T + b).reshape(B, S, H, D).transpose(0, 2, 1, 3)
        Q, K, V = (proj(Wq, bq), proj(Wk, bk), proj(Wv, bv))
        scores = jnp.einsum('bhqd,bhkd->bhqk', Q, K) / jnp.sqrt(jnp.float32(D))
        _, topi = jax.lax.top_k(scores, k)
        bb = jnp.arange(B)[:, None, None, None]
        hh = jnp.arange(H)[None, :, None, None]
        qq = jnp.arange(S)[None, None, :, None]
        sparse_mask = jnp.zeros_like(scores).at[bb, hh, qq, topi].set(1.0)
        attn = jax.nn.softmax(scores * sparse_mask, axis=-1)
        out = jnp.einsum('bhqk,bhkd->bhqd', attn, V)
        out = out.transpose(0, 2, 1, 3).reshape(B, S, E)
        return out @ Wo.T + bo

    def _L0_ffn_ref(x, W1, b1, W2, b2):
        import jax, jax.numpy as jnp
        import numpy as np
        EPS = 1e-05

        def _quantize(W):
            gamma = jnp.mean(jnp.abs(W))
            return jnp.clip(jnp.round(W / (gamma + EPS)), -1.0, 1.0)
        Wq1 = _quantize(W1)
        Wq2 = _quantize(W2)
        h = jax.nn.relu(jnp.einsum('bsd,fd->bsf', x, Wq1) + b1)
        out = jnp.einsum('bsf,df->bsd', h, Wq2) + b2
        return out
    x = x + _L0_xattn_ref(_layernorm(x, axis=-1), ctx_1024, ctx_1024, mask_1x1xSxS2_bk1, L0_xattn_W_Q, L0_xattn_W_K, L0_xattn_W_V, L0_xattn_W_O)
    x = x + _L0_attn_ref(_layernorm(x, axis=-1), L0_attn_Wq, L0_attn_bq, L0_attn_Wk, L0_attn_bk, L0_attn_Wv, L0_attn_bv, L0_attn_Wo, L0_attn_bo)
    x = x + _L0_ffn_ref(_layernorm(x, axis=-1), L0_ffn_W1, L0_ffn_b1, L0_ffn_W2, L0_ffn_b2)
    return x

_drawn_inputs = setup_inputs


def setup_inputs(seed=0):
    import zlib

    import numpy as np

    out = dict(_drawn_inputs(seed))
    spreads = {'L0_attn_bq': (0.0, 0.753),
     'L0_attn_bk': (0.0, 2.0),
     'L0_attn_bv': (0.0, 0.1),
     'L0_attn_bo': (0.0, 0.1)}
    factors = {'L0_ffn_b1': 44.529, 'L0_ffn_b2': 64.0}
    for name, (base, spread) in spreads.items():
        noise = np.random.default_rng([zlib.crc32(name.encode()), seed]).standard_normal(out[name].shape)
        drawn = base * np.exp(spread * noise) if base else spread * noise
        out[name] = jnp.asarray(drawn.astype(out[name].dtype))
    for name, factor in factors.items():
        out[name] = (out[name] * factor).astype(out[name].dtype)
    return out
```

```python
from collections import namedtuple
from contextlib import ExitStack

import concourse.bass as bass
import concourse.mybir as mybir

F32 = mybir.dt.float32
F32R = mybir.dt.float32r
I32 = mybir.dt.int32
U8 = mybir.dt.uint8
ALU = mybir.AluOpType
ACT = mybir.ActivationFunctionType
AXIS = mybir.AxisListType

P = 128
BATCHES, SEQ, D, KEYS = 64, 64, 512, 512
HEADS = 16
DK = D // HEADS
DC = D // P
PAIRS = HEADS // 2
VW = DK + 1
TOKENS = BATCHES * SEQ
FF = 4 * D
FC = FF // P
KEY_TILES = KEYS // P
SCORE_SCALE = float(DK) ** -0.5
MASKED = -1e30
LN_EPS = 1e-5
QUANT_EPS = 1e-5

Unit = namedtuple("Unit", "half off")


def later(u, n):
    return Unit(u.half, u.off + n)


def parity(u):
    return u.off % 2


def number(u):
    return u.half * 2 + u.off


def total(u, per_unit, k=0):
    return u.half * (2 * per_unit) + (per_unit * u.off + k)


def total_of_parity(u, per_unit, k=0):
    return u.half * per_unit + (per_unit * (u.off // 2) + k)


def wait(eng, sem, value):
    if not (isinstance(value, int) and value <= 0):
        eng.wait_ge(sem, value)


class Banks:

    def __init__(self, prologue, full, last_but_one, last):
        self.prologue = prologue
        self.uses = {"full": full, "last_but_one": last_but_one, "last": last}
        self.first, self.per = len(prologue), len(full)

    def before(self, u, name=None, kind="full"):
        if u is None:
            return self.prologue.index(name)
        fewer = self.per - len(self.uses["last_but_one"]) if kind == "last" else 0
        n = self.uses[kind].index(name) if name else 0
        return self.first + self.per * u.off - fewer + n

    def at(self, u, name, kind="full"):
        j = self.before(u, name, kind)
        earlier = (j + 1 - j % 2) // 2
        return j % 2, earlier if u is None else u.half * self.per + earlier

    def last_but_one_ahead(self, u, kind):
        j = self.before(u, None, kind)
        return j % 2, u.half * self.per + (j + 1 - j % 2) // 2

    def drained(self, bank):
        return (self.first + 1 - bank) // 2


def run_steps(eng, units, step):
    step(Unit(0, 0), "full")
    step(Unit(0, 1), "full")
    with eng.Fori(1, units // 2 - 1) as half:
        step(Unit(half, 0), "full")
        step(Unit(half, 1), "full")
    step(Unit(units // 2 - 1, 0), "last_but_one")
    step(Unit(units // 2 - 1, 1), "last")


def build(nc, x, ctx, mask, w_cross, w_self, bq, bk, bv, bo, w1, b1, w2, b2,
          out,
          only_cross=False):
    x1 = nc.dram_tensor("x1", (TOKENS, D), F32, kind="Internal").ap()
    x2 = nc.dram_tensor("x2", (TOKENS, D), F32, kind="Internal").ap()
    if only_cross:
        x1 = out
    outer = ExitStack()
    with outer:
        def sem(name):
            return outer.enter_context(nc.semaphore(name))

        def sems(name):
            return [sem(f"{name}_{i}") for i in range(2)]

        def sb(stack, name, shape, dt=F32):
            return stack.enter_context(nc.sbuf_tensor(name, shape, dt))

        PJ = [outer.enter_context(nc.psum_tensor(f"project_{i}", [P, 512], F32)) for i in range(2)]
        S = outer.enter_context(nc.psum_tensor("scores", [P, 1024], F32))
        PT = outer.enter_context(nc.psum_tensor("probs_t_psum", [P, 1024], F32))
        PV = outer.enter_context(nc.psum_tensor("attended", [P, 2, 512], F32))
        PV_HEADS = PV[:, :, 0:PAIRS * VW].rearrange("p a (h d) -> p a h d", d=VW)
        YB = [S[:, 0:512], S[:, 512:1024], PT[:, 0:512], PT[:, 512:1024]]
        XB = [PV[:, 0, :], PV[:, 1, :]]

        ident = sb(outer, "ident", [P, P])
        ones = sb(outer, "ones", [P, P])
        minus_half = sb(outer, "minus_half", [P, 1])
        ln_eps = sb(outer, "ln_eps", [P, 1])
        flag_i = sb(outer, "only_last_tile", [1, 2], I32)
        stats = sb(outer, "ln_stats_buf", [P, 4, 6])
        mean_var = sb(outer, "mean_var", [P, 4, 2])
        var_eps = sb(outer, "var_eps", [P, 4, 1])
        rstd = sb(outer, "rstd", [P, 4, 1])
        row_max = sb(outer, "row_max", [P, HEADS])
        sums = sb(outer, "row_sums", [P, 2, HEADS // 2, 1])
        bq_sb = sb(outer, "bq_sb", [P, DC])
        bk_sb = sb(outer, "bk_sb", [P, DC])
        b1_sb = sb(outer, "b1_sb", [P, FC])

        with ExitStack() as st:
            cw_hi = sb(st, "cross_w_hi", [P, 4, DC, D], F32R)
            cw_lo = sb(st, "cross_w_lo", [P, 4, DC, D], F32R)
            ctx_raw = sb(st, "ctx_raw", [P, 2, 4, DC, P])
            ctx_hi = sb(st, "ctx_hi", [P, 2, 4, DC, P], F32R)
            ctx_lo = sb(st, "ctx_lo", [P, 2, 4, DC, P], F32R)
            q_pad = sb(st, "q_pad", [P, DC, 2, 4, 2, SEQ])
            ck_t = sb(st, "cross_k_t", [P, 2, DC, 4, P])
            cv = sb(st, "cross_v", [P, 2, 4, HEADS, VW])
            cx = sb(st, "cross_x", [P, 2, 2, D])
            cxn = sb(st, "cross_x_norm", [P, 2, D])
            cxt_hi = sb(st, "cross_xt_hi", [P, DC, 4 * SEQ], F32R)
            cxt_lo = sb(st, "cross_xt_lo", [P, DC, 4 * SEQ], F32R)
            c_s = sb(st, "cross_scores", [P, 1024])
            c_p = sb(st, "cross_probs", [P, 1024])
            c_pt = sb(st, "cross_probs_t", [P, 1024])
            c_a = sb(st, "cross_a", [P, HEADS, DK])
            cat_hi = sb(st, "cross_at_hi", [P, DC, P], F32R)
            cat_lo = sb(st, "cross_at_lo", [P, DC, P], F32R)
            mask_bias = sb(st, "mask_bias", [P, KEYS])
            counts = sb(st, "mask_counts", [P, 4])
            mask_u8 = c_a.rearrange("p h d -> p (h d)").bitcast(U8)[:, 0:KEYS]
            mask_f = c_pt[:, 0:KEYS]
        with ExitStack() as st:
            sw_hi = sb(st, "self_w_hi", [P, 4, DC, D], F32R)
            sw_lo = sb(st, "self_w_lo", [P, 4, DC, D], F32R)
            sx = sb(st, "self_x", [P, 2, 2, D])
            sres = sb(st, "self_residual", [P, 2, 2, D])
            sxn = sb(st, "self_x_norm", [P, 2, D])
            sxt_hi = sb(st, "self_xt_hi", [P, DC, 4 * SEQ], F32R)
            sxt_lo = sb(st, "self_xt_lo", [P, DC, 4 * SEQ], F32R)
            sq_t = sb(st, "self_q_t", [P, 2, DC, 4, SEQ])
            sk_t = sb(st, "self_k_t", [P, 2, DC, 4, SEQ])
            sv = sb(st, "self_v", [P, 2, 2, HEADS, VW])
            s_s = sb(st, "self_scores", [P, 1024])
            s_p = sb(st, "self_probs", [P, 1024])
            s_pt = sb(st, "self_probs_t", [P, 1024])
            s_a = sb(st, "self_a", [P, HEADS, DK])
            sat_hi = sb(st, "self_at_hi", [P, DC, P], F32R)
            sat_lo = sb(st, "self_at_lo", [P, DC, P], F32R)
            bv_sb = sb(st, "bv_sb", [P, D])
            bo_sb = sb(st, "bo_sb", [P, D])
        with ExitStack() as st:
            w1_q = sb(st, "w1_ternary", [P, DC, FF], F32R)
            w2_q = sb(st, "w2_ternary", [P, FC, D], F32R)
            f_stage = sb(st, "ff_stage", [P, 2, 2048])
            f_neg = sb(st, "ff_negative", [P, 2048])
            abs_sum = sb(st, "abs_sum", [P, 2, 4])
            abs_total = sb(st, "abs_total", [P, 2])
            thresh = sb(st, "thresholds", [P, 2, 2])
            fx = sb(st, "ff_x", [P, 2, 4, D])
            fres = sb(st, "ff_residual", [P, 2, 4, D])
            fxn = sb(st, "ff_x_norm", [P, 2, D])
            fxt_hi = sb(st, "ff_xt_hi", [P, 2, DC, 4 * P], F32R)
            fxt_lo = sb(st, "ff_xt_lo", [P, 2, DC, 4 * P], F32R)
            h_raw = sb(st, "hidden", [P, 2, 512])
            h_hi = sb(st, "hidden_hi", [P, 4, 512], F32R)
            h_lo = sb(st, "hidden_lo", [P, 4, 512], F32R)
            b2_sb = sb(st, "b2_sb", [P, D])

        const_ready = sem("const_ready")
        mask_in = sem("mask_in")
        mask_step = sem("mask_step")
        mask_counted = sem("mask_counted")
        flag_ready = sem("flag_ready")
        w_in = sems("w_in")
        w_hi_ready = sem("w_hi_ready")
        w_lo_ready = sem("w_lo_ready")
        pads_ready = sem("pads_ready")

        class Phase:
            def __init__(self, name):
                s = lambda n: sem(f"{name}_{n}")
                self.x_in = [s(f"x_in_{i}") for i in range(2)]
                self.stats = s("stats")
                self.agg = s("agg")
                self.eps = s("eps")
                self.rstd = s("rstd")
                self.xn = s("xn")
                self.res = s("residual")
                self.pj_full = [s(f"pj_full_{i}") for i in range(2)]
                self.pj_free = [s(f"pj_free_{i}") for i in range(2)]
                self.xt_hi = s("xt_hi")
                self.at_hi = s("at_hi")
                self.s_full = s("s_full")
                self.s_free = s("s_free")
                self.s_max = s("s_max")
                self.s_sub = s("s_sub")
                self.p_ready = s("p_ready")
                self.pt_full = s("pt_full")
                self.pt_ready = s("pt_ready")
                self.pv_done = s("pv_done")
                self.rcp = s("rcp")
                self.a_ready = s("a_ready")
                self.stored = [s(f"stored_{i}") for i in range(2)]

        C = Phase("cross")
        ctx_in = sems("ctx_in")
        ctx_hi_ready = sem("ctx_hi_ready")
        ctx_lo_ready = sem("ctx_lo_ready")
        G = Phase("self")
        self_bias_in = sem("self_bias_in")
        sw_in = sems("sw_in")
        sw_hi_ready = sem("sw_hi_ready")
        sw_lo_ready = sem("sw_lo_ready")
        self_ones = sem("self_ones")
        ff_bias_in = sem("ff_bias_in")
        fw_in = sems("fw_in")
        fw_abs = sem("fw_abs")
        fw_free = sem("fw_free")
        fw_total = sem("fw_total")
        fw_thresh = sem("fw_thresh")
        fw_neg = sem("fw_neg")
        fw_ready = sem("fw_ready")
        fx_in = sems("fx_in")
        f_stats, f_agg, f_eps, f_rstd, f_xn, f_res = (
            sem("f_stats"), sem("f_agg"), sem("f_eps"), sem("f_rstd"), sem("f_xn"), sem("f_res"))
        xb_full, xb_free, fxt_hi_ready = sem("xb_full"), sem("xb_free"), sem("fxt_hi_ready")
        h_full, h_relu, h_hi_ready, h_lo_ready = (
            sem("h_full"), sem("h_relu"), sem("h_hi_ready"), sem("h_lo_ready"))
        y_m = sem("y_m")
        y_full = [sem(f"y_full_{t}") for t in range(4)]
        y_new = [sem(f"y_new_{t}") for t in range(4)]
        cross_done, self_done = sem("cross_done"), sem("self_done")
        f_stored = sems("f_stored")

        def split_products(e, out_ap, pairs, before_last=None):
            n = 0
            last = None
            for s_hi, s_lo, m_hi, m_lo in pairs:
                for a, b in ((s_hi, m_hi), (s_hi, m_lo), (s_lo, m_hi)):
                    if before_last and n == 3 * len(pairs) - 1:
                        before_last()
                    last = nc.tensor.matmul(out_ap, a, b, start=(n == 0),
                                            stop=(n == 3 * len(pairs) - 1))
                    n += 1
            return last

        class Cross:
            def __init__(self, kt):
                self.kt, self.b = kt, 4 // kt
                self.units = BATCHES // self.b
                self.tokens = self.b * SEQ
                self.nt = max(1, self.b // 2)
                self.tp = min(P, self.tokens)
                two = self.nt == 2
                full = (["K0", "K1", "K2", "K3", "X0"] + ["X1"] * two + ["V0", "V1"] + ["A0"] * two
                        + ["V2"] + ["O0"] * two
                        + ["V3", "Q0", f"A{self.nt - 1}", "Q1", f"O{self.nt - 1}"])
                self.banks = Banks(
                    [f"K{i}" for i in range(4)] + [f"X{t}" for t in range(self.nt)]
                    + [f"V{i}" for i in range(4)] + ["Q0", "Q1"],
                    full, full, [n for n in full if n[0] in "AO"])
                self.x = x.rearrange("(u t p) d -> u t p d", t=self.nt, p=self.tp)
                self.x1 = x1.rearrange("(u t p) d -> u t p d", t=self.nt, p=self.tp)
                self.ctx = (ctx.rearrange("(u b) k p n -> u b k p n", b=self.b)[:, :, 3]
                            if kt == 1 else ctx)
                self.tile_of = (lambda q: q // 2) if two else (lambda q: 0)

        def cross_sync(e, K):
            def load_ctx(v):
                wait(e, ctx_lo_ready, total(v, 1, -1))
                for j in range(4):
                    e.dma_start(ctx_raw[:, parity(v), j, :, :].rearrange("p c k -> p (c k)"),
                                K.ctx[number(v), j]).then_inc(ctx_in[parity(v)], 16)

            def load_x(v):
                for t in range(K.nt):
                    e.dma_start(cx[0:K.tp, parity(v), t, :], K.x[number(v), t]) \
                        .then_inc(C.x_in[parity(v)], 16)

            def step(u, kind):
                more, ahead = kind != "last", kind == "full"
                if ahead:
                    load_ctx(later(u, 2))
                for t in range(K.nt):
                    bank, before = K.banks.at(u, f"O{t}", kind)
                    wait(e, C.pj_free[bank], before + 1)
                    e.dma_start(K.x1[number(u), t], cx[0:K.tp, parity(u), t, :]) \
                        .then_inc(C.stored[parity(u)], 16)
                if ahead:
                    wait(e, C.stored[parity(u)], total_of_parity(u, 16 * K.nt, 16 * K.nt))
                    load_x(later(u, 2))

            for n in range(2):
                load_ctx(Unit(0, n))
                load_x(Unit(0, n))
            run_steps(e, K.units, step)
            for i in range(2):
                e.wait_ge(C.stored[i], 16 * K.nt * K.units // 2)
            e.nop().then_inc(cross_done, 1)

        def cross_pe(e, K):
            def begin(u, name, kind="full"):
                bank, before = K.banks.at(u, name, kind)
                wait(e, C.pj_free[bank], before)
                return bank

            def k_proj(u, v, m):
                bank = begin(u, f"K{m}")
                if m == 0:
                    wait(e, ctx_lo_ready, total(v, 1, 1))
                w = slice(m * P, m * P + P)
                split_products(e, PJ[bank][:], [
                    (cw_hi[:, 1, c, w], cw_lo[:, 1, c, w],
                     ctx_hi[:, parity(v), :, c, :], ctx_lo[:, parity(v), :, c, :])
                    for c in range(DC)]).then_inc(C.pj_full[bank], 1)

            def v_proj(u, v, j):
                bank = begin(u, f"V{j}")
                split_products(e, PJ[bank][:], [
                    (ctx_hi[:, parity(v), j, c, :], ctx_lo[:, parity(v), j, c, :],
                     cw_hi[:, 2, c, :], cw_lo[:, 2, c, :])
                    for c in range(DC)]).then_inc(C.pj_full[bank], 1)

            def x_transpose(u, v, t):
                bank = begin(u, f"X{t}")
                wait(e, C.xn, total(v, K.nt, t + 1))
                for c in range(DC):
                    last = nc.tensor.transpose(PJ[bank][:, c * P:c * P + P],
                                               cxn[:, t, c * P:c * P + P], ident[:])
                last.then_inc(C.pj_full[bank], 1)

            def q_proj(u, n):
                bank = begin(u, f"Q{n}")
                if n == 0:
                    for t in range(K.nt):
                        b, before = K.banks.at(u, f"X{t}")
                        wait(e, C.pj_free[b], before + 1)
                for i in range(2):
                    w = slice((2 * n + i) * P, (2 * n + i + 1) * P)
                    last = split_products(e, PJ[bank][:, 256 * i:256 * i + K.tokens], [
                        (cw_hi[:, 0, c, w], cw_lo[:, 0, c, w],
                         cxt_hi[:, c, 0:K.tokens], cxt_lo[:, c, 0:K.tokens]) for c in range(DC)])
                last.then_inc(C.pj_full[bank], 1)

            def scores(u, q):
                wait(e, C.s_free, total(u, 4, q))
                n = K.kt * P
                for i in range(PAIRS // K.kt):
                    pair = i if K.kt == 1 else q * (PAIRS // K.kt) + i
                    batch = q if K.kt == 1 else 0
                    keys = (ck_t[:, parity(u), pair // 2, q, :] if K.kt == 1 else
                            ck_t[:, parity(u), pair // 2, :, :].rearrange("p j k -> p (j k)"))
                    last = nc.tensor.matmul(
                        S[:, i * n:(i + 1) * n],
                        q_pad[:, pair // 2, pair % 2, batch, :, :].rearrange("p a s -> p (a s)"),
                        keys, start=True, stop=True)
                last.then_inc(C.s_full, 1)

            def transposes(u, q):
                wait(e, C.pt_ready, total(u, 4, q))
                wait(e, C.p_ready, total(u, 4, q + 1))
                for i in range(8):
                    last = nc.tensor.transpose(PT[:, i * P:i * P + P], c_p[:, i * P:i * P + P],
                                               ident[:])
                last.then_inc(C.pt_full, 1)

            def attend(u, q):
                t = K.tile_of(q)
                if q == 0 or t != K.tile_of(q - 1):
                    wait(e, C.a_ready, total(u, K.nt, t))
                wait(e, C.pt_ready, total(u, 4, q + 1))
                row = SEQ * (q % 2) if K.kt == 1 else 0
                for i in range(HEADS // K.kt):
                    head = i if K.kt == 1 else q * (HEADS // K.kt) + i
                    for k in range(K.kt):
                        block = (i // 2) * K.kt + k
                        at = block * P + SEQ * (head % 2)
                        last = nc.tensor.matmul(
                            PV_HEADS[row:row + SEQ, head // 8, head % 8, :], c_pt[:, at:at + SEQ],
                            cv[:, parity(u), q if K.kt == 1 else k, head, :],
                            start=(k == 0), stop=(k == K.kt - 1))
                last.then_inc(C.pv_done, 1)

            def a_transpose(u, t, kind):
                bank = begin(u, f"A{t}", kind)
                wait(e, C.a_ready, total(u, K.nt, t + 1))
                a = c_a[:, :, :].rearrange("p h d -> p (h d)")
                for c in range(DC):
                    last = nc.tensor.transpose(PJ[bank][:, c * P:c * P + P],
                                               a[:, c * P:c * P + P], ident[:])
                last.then_inc(C.pj_full[bank], 1)

            def o_proj(u, t, kind):
                bank = begin(u, f"O{t}", kind)
                b, before = K.banks.at(u, f"A{t}", kind)
                wait(e, C.pj_free[b], before + 1)
                split_products(e, PJ[bank][0:K.tp, :], [
                    (cat_hi[:, c, 0:K.tp], cat_lo[:, c, 0:K.tp], cw_hi[:, 3, c, :], cw_lo[:, 3, c, :])
                    for c in range(DC)]).then_inc(C.pj_full[bank], 1)

            def step(u, kind):
                more, ahead = kind != "last", kind == "full"
                v = later(u, 1)
                bank, before = K.banks.last_but_one_ahead(u, kind)
                wait(e, C.pj_free[bank], before)
                scores(u, 0)
                if more:
                    k_proj(u, v, 0)
                    k_proj(u, v, 1)
                scores(u, 1)
                transposes(u, 0)
                if more:
                    k_proj(u, v, 2)
                attend(u, 0)
                scores(u, 2)
                transposes(u, 1)
                if more:
                    k_proj(u, v, 3)
                attend(u, 1)
                if more:
                    x_transpose(u, v, 0)
                scores(u, 3)
                transposes(u, 2)
                if more:
                    if K.nt == 2:
                        x_transpose(u, v, 1)
                    v_proj(u, v, 0)
                attend(u, 2)
                if more:
                    v_proj(u, v, 1)
                if K.nt == 2:
                    a_transpose(u, 0, kind)
                if more:
                    v_proj(u, v, 2)
                if K.nt == 2:
                    o_proj(u, 0, kind)
                transposes(u, 3)
                if more:
                    v_proj(u, v, 3)
                attend(u, 3)
                if more:
                    q_proj(u, 0)
                a_transpose(u, K.nt - 1, kind)
                if more:
                    q_proj(u, 1)
                o_proj(u, K.nt - 1, kind)

            first = Unit(0, 0)
            wait(e, w_lo_ready, 4)
            wait(e, pads_ready, 4)
            for m in range(4):
                k_proj(None, first, m)
            for t in range(K.nt):
                x_transpose(None, first, t)
            for j in range(4):
                v_proj(None, first, j)
            q_proj(None, 0)
            q_proj(None, 1)
            for bank in range(2):
                wait(e, C.pj_free[bank], K.banks.drained(bank))
            run_steps(e, K.units, step)

        def cross_act(e, K):
            def full(u, name, kind="full"):
                bank, before = K.banks.at(u, name, kind)
                wait(e, C.pj_full[bank], before + 1)
                return bank

            def keys_out(u, v, m):
                bank = full(u, f"K{m}")
                nc.scalar.activation(ck_t[:, parity(v), m, :, :].rearrange("p j k -> p (j k)"),
                                     PJ[bank][:], ACT.Copy).then_inc(C.pj_free[bank], 1)

            def x_hi(u, v, t):
                bank = full(u, f"X{t}")
                nc.scalar.activation(
                    cxt_hi[:, :, t * P:t * P + K.tp],
                    PJ[bank][:].rearrange("p (c s) -> p c s", c=DC)[:, :, 0:K.tp],
                    ACT.Copy).then_inc(C.xt_hi, 1)

            def a_hi(u, t, kind):
                bank = full(u, f"A{t}", kind)
                nc.scalar.activation(
                    cat_hi[:, :, 0:K.tp],
                    PJ[bank][:].rearrange("p (c s) -> p c s", c=DC)[:, :, 0:K.tp],
                    ACT.Copy).then_inc(C.at_hi, 1)

            def queries_out(u, n):
                bank = full(u, f"Q{n}")
                for r in range(4):
                    rows = slice(DK * r, DK * r + DK)
                    for i in range(2):
                        src = PJ[bank][rows, 256 * i:256 * i + K.tokens] \
                            .rearrange("p (b s) -> p b s", s=SEQ)
                        last = nc.scalar.activation(
                            q_pad[rows, 2 * n + i, r // 2, 0:K.b, r % 2, :], src, ACT.Copy)
                last.then_inc(C.pj_free[bank], 1)

            def exponentials(u, q):
                wait(e, C.s_sub, total(u, 4, q + 1))
                nc.scalar.activation(c_p[:], c_s[:], ACT.Exp, scale=SCORE_SCALE) \
                    .then_inc(C.p_ready, 1)

            def probs_t_out(u, q):
                wait(e, C.pt_full, total(u, 4, q + 1))
                wait(e, C.pv_done, total(u, 4, q))
                nc.scalar.activation(c_pt[:], PT[:], ACT.Copy).then_inc(C.pt_ready, 1)

            def split_ctx(v):
                wait(e, ctx_in[parity(v)], total_of_parity(v, 64, 64))
                nc.scalar.activation(ctx_hi[:, parity(v)].rearrange("p j c k -> p (j c k)"),
                                     ctx_raw[:, parity(v)].rearrange("p j c k -> p (j c k)"),
                                     ACT.Copy).then_inc(ctx_hi_ready, 1)

            def step(u, kind):
                more, ahead = kind != "last", kind == "full"
                v = later(u, 1)
                if more:
                    keys_out(u, v, 0)
                exponentials(u, 0)
                if more:
                    keys_out(u, v, 1)
                probs_t_out(u, 0)
                if more:
                    keys_out(u, v, 2)
                exponentials(u, 1)
                probs_t_out(u, 1)
                if more:
                    keys_out(u, v, 3)
                exponentials(u, 2)
                if more:
                    x_hi(u, v, 0)
                probs_t_out(u, 2)
                if more and K.nt == 2:
                    x_hi(u, v, 1)
                exponentials(u, 3)
                if ahead:
                    split_ctx(later(u, 2))
                if K.nt == 2:
                    a_hi(u, 0, kind)
                probs_t_out(u, 3)
                if more:
                    queries_out(u, 0)
                a_hi(u, K.nt - 1, kind)
                if more:
                    queries_out(u, 1)

            first = Unit(0, 0)
            split_ctx(first)
            split_ctx(later(first, 1))
            for m in range(4):
                keys_out(None, first, m)
            for t in range(K.nt):
                x_hi(None, first, t)
            wait(e, pads_ready, 4)
            queries_out(None, 0)
            queries_out(None, 1)
            run_steps(e, K.units, step)

        def cross_dve(e, K):
            def full(u, name, kind="full"):
                bank, before = K.banks.at(u, name, kind)
                wait(e, C.pj_full[bank], before + 1)
                return bank

            def ln_statistics(v):
                wait(e, C.x_in[parity(v)], total_of_parity(v, 16 * K.nt, 16 * K.nt))
                for t in range(K.nt):
                    nc.vector.bn_stats(stats[0:K.tp, t, :], cx[0:K.tp, parity(v), t, :]) \
                        .then_inc(C.stats, 1)

            def ln_normalise(v):
                for t in range(K.nt):
                    nc.vector.bn_aggr(mean_var[0:K.tp, t, :], stats[0:K.tp, t, :]) \
                        .then_inc(C.agg, 1)
                for t in range(K.nt):
                    wait(e, C.rstd, total(v, K.nt, t + 1))
                    nc.vector.tensor_scalar(cxn[0:K.tp, t, :], cx[0:K.tp, parity(v), t, :],
                                            mean_var[0:K.tp, t, 0:1], rstd[0:K.tp, t, :],
                                            ALU.subtract, ALU.mult).then_inc(C.xn, 1)

            def x_lo(u, v, t):
                bank = full(u, f"X{t}")
                wait(e, C.xt_hi, total(v, K.nt, t + 1))
                nc.vector.tensor_tensor(
                    cxt_lo[:, :, t * P:t * P + K.tp],
                    PJ[bank][:].rearrange("p (c s) -> p c s", c=DC)[:, :, 0:K.tp],
                    cxt_hi[:, :, t * P:t * P + K.tp].bitcast(F32),
                    ALU.subtract).then_inc(C.pj_free[bank], 1)

            def a_lo(u, t, kind):
                bank = full(u, f"A{t}", kind)
                wait(e, C.at_hi, total(u, K.nt, t + 1))
                nc.vector.tensor_tensor(
                    cat_lo[:, :, 0:K.tp],
                    PJ[bank][:].rearrange("p (c s) -> p c s", c=DC)[:, :, 0:K.tp],
                    cat_hi[:, :, 0:K.tp].bitcast(F32), ALU.subtract).then_inc(C.pj_free[bank], 1)

            def values_out(u, v, j):
                bank = full(u, f"V{j}")
                nc.vector.tensor_copy(cv[:, parity(v), j, :, 0:DK],
                                      PJ[bank][:].rearrange("p (h d) -> p h d", d=DK)) \
                    .then_inc(C.pj_free[bank], 1)

            def softmax(u, q):
                groups = PAIRS // K.kt
                rows = lambda a: a[:].rearrange("p (g k) -> p g k", g=groups)
                n = K.kt * P
                wait(e, C.s_full, total(u, 4, q + 1))
                wait(e, C.p_ready, total(u, 4, q))
                nc.vector.tensor_tensor(
                    rows(c_s), rows(S),
                    mask_bias[:, KEYS - n:KEYS].unsqueeze(1).to_broadcast([P, groups, n]),
                    ALU.add).then_inc(C.s_free, 1)
                wait(e, C.s_free, total(u, 4, q + 1))
                nc.vector.reduce_max(row_max[:, 0:groups], rows(c_s), AXIS.X).then_inc(C.s_max, 1)
                wait(e, C.s_max, total(u, 4, q + 1))
                nc.vector.tensor_tensor(rows(c_s), rows(c_s),
                                        row_max[:, 0:groups].unsqueeze(2).to_broadcast([P, groups, n]),
                                        ALU.subtract).then_inc(C.s_sub, 1)

            def normalise(u, t):
                wait(e, C.pv_done, total(u, 4, 4 // K.nt * (t + 1)))
                nc.vector.reciprocal(sums[0:K.tp, :, :, :], PV_HEADS[0:K.tp, :, :, DK:VW]) \
                    .then_inc(C.rcp, 1)
                wait(e, C.rcp, total(u, K.nt, t + 1))
                nc.vector.tensor_tensor(
                    c_a[0:K.tp].rearrange("p (a h) d -> p a h d", a=2),
                    PV_HEADS[0:K.tp, :, :, 0:DK],
                    sums[0:K.tp].to_broadcast([K.tp, 2, HEADS // 2, DK]),
                    ALU.mult).then_inc(C.a_ready, 1)

            def residual(u, t, kind):
                bank = full(u, f"O{t}", kind)
                nc.vector.tensor_tensor(cx[0:K.tp, parity(u), t, :], PJ[bank][0:K.tp, :],
                                        cx[0:K.tp, parity(u), t, :], ALU.add) \
                    .then_inc(C.pj_free[bank], 1)

            def split_ctx(v):
                wait(e, ctx_hi_ready, total(v, 1, 1))
                flat = lambda a: a[:, parity(v)].rearrange("p j c k -> p (j c k)")
                nc.vector.tensor_tensor(flat(ctx_lo), flat(ctx_raw), flat(ctx_hi).bitcast(F32),
                                        ALU.subtract).then_inc(ctx_lo_ready, 1)

            def step(u, kind):
                more, ahead = kind != "last", kind == "full"
                v = later(u, 1)
                softmax(u, 0)
                if more:
                    ln_statistics(v)
                    wait(e, C.stats, total(v, K.nt, K.nt))
                softmax(u, 1)
                if more:
                    ln_normalise(v)
                softmax(u, 2)
                if K.nt == 2:
                    normalise(u, 0)
                if more:
                    x_lo(u, v, 0)
                softmax(u, 3)
                if more:
                    if K.nt == 2:
                        x_lo(u, v, 1)
                    values_out(u, v, 0)
                    values_out(u, v, 1)
                if K.nt == 2:
                    a_lo(u, 0, kind)
                if ahead:
                    split_ctx(later(u, 2))
                if more:
                    values_out(u, v, 2)
                if K.nt == 2:
                    residual(u, 0, kind)
                if more:
                    values_out(u, v, 3)
                normalise(u, K.nt - 1)
                a_lo(u, K.nt - 1, kind)
                residual(u, K.nt - 1, kind)

            first = Unit(0, 0)
            split_ctx(first)
            split_ctx(later(first, 1))
            ln_statistics(first)
            wait(e, C.stats, K.nt)
            ln_normalise(first)
            for t in range(K.nt):
                x_lo(None, first, t)
            wait(e, pads_ready, 4)
            for j in range(4):
                values_out(None, first, j)
            run_steps(e, K.units, step)

        def rstd_of(e, agg, eps, done, v, per, rows):
            for t in range(per):
                wait(e, agg, total(v, per, t + 1))
                e.tensor_tensor(var_eps[0:rows, t, :], mean_var[0:rows, t, 1:2], ln_eps[0:rows, :],
                                ALU.add).then_inc(eps, 1)
                wait(e, eps, total(v, per, t + 1))
                e.tensor_tensor(rstd[0:rows, t, :], var_eps[0:rows, t, :], minus_half[0:rows, :],
                                ALU.pow).then_inc(done, 1)

        def cross_pool(e, K):
            def step(u, kind):
                more, ahead = kind != "last", kind == "full"
                if more:
                    rstd_of(e, C.agg, C.eps, C.rstd, later(u, 1), K.nt, K.tp)

            rstd_of(e, C.agg, C.eps, C.rstd, Unit(0, 0), K.nt, K.tp)
            run_steps(e, K.units, step)

        def s_stage(n):
            return (sq_t, sk_t)[n % 2][:].rearrange("p a c b s -> p (a c b s)")

        def cv_stage(n):
            return cv[:, n % 2].rearrange("p j h d -> p (j h d)")[:, 0:DC * D]

        LAST_TILE, ALL_TILES = Cross(1), Cross(KEY_TILES)

        block = outer.enter_context(nc.Block())

        S_UNITS, NT = TOKENS // (4 * SEQ), 2
        s_full_uses = ["Q0", "Q1", "K0", "A0", "K1", "O0", "V0", "V1", "A1", "X0", "X1", "O1"]
        SB = Banks(["X0", "X1", "Q0", "Q1", "K0", "K1", "V0", "V1", "Y0", "Y1"], s_full_uses,
                   [n for n in s_full_uses if n[0] != "X"], [n for n in s_full_uses if n[0] in "AO"])
        s_x1 = x1.rearrange("(u t p) d -> u t p d", t=NT, p=P)
        s_x2 = x2.rearrange("(u t p) d -> u t p d", t=NT, p=P)
        SLOT = [(pair % 2) * 4 + pair // 2 for pair in range(PAIRS)]

        def self_sync(e):
            def load_x(v):
                wait(e, G.xn, total(v, NT, -NT))
                wait(e, G.res, total(v, NT, -NT))
                for t in range(NT):
                    e.dma_start(sx[:, parity(v), t, :], s_x1[number(v), t]) \
                        .then_inc(G.x_in[parity(v)], 16)

            def step(u, kind):
                if kind == "full":
                    load_x(later(u, 2))
                for t in range(NT):
                    bank, before = SB.at(u, f"O{t}", kind)
                    wait(e, G.pj_free[bank], before + 1)
                    e.dma_start(s_x2[number(u), t], sres[:, parity(u), t, :]) \
                        .then_inc(G.stored[parity(u)], 16)

            e.wait_ge(cross_done, 1)
            for n in range(4):
                wait(e, sw_lo_ready, n - 1)
                e.dma_start(s_stage(n), w_self[n]).then_inc(sw_in[n % 2], 16)
            for n in range(2):
                load_x(Unit(0, n))
            for dst, src in ((bq_sb, bq), (bk_sb, bk)):
                e.dma_start(dst[:], src).then_inc(self_bias_in, 16)
            for dst, src in ((bv_sb, bv), (bo_sb, bo)):
                e.dma_start(dst[:], src.unsqueeze(0).to_broadcast([P, D])) \
                    .then_inc(self_bias_in, 16)
            run_steps(e, S_UNITS, step)
            for i in range(2):
                e.wait_ge(G.stored[i], 16 * NT * S_UNITS // 2)
            e.nop().then_inc(self_done, 1)

        def self_pe(e):
            def begin(u, name, kind="full"):
                bank, before = SB.at(u, name, kind)
                wait(e, G.pj_free[bank], before)
                return bank

            def x_transpose(u, v, t, name=None):
                bank = begin(u, name or f"X{t}")
                wait(e, G.xn, total(v, NT, t + 1))
                for c in range(DC):
                    last = nc.tensor.transpose(PJ[bank][:, c * P:c * P + P],
                                               sxn[:, t, c * P:c * P + P], ident[:])
                last.then_inc(G.pj_full[bank], 1)

            def qk_proj(u, name, w, kind="full", before_last=None):
                bank = begin(u, name, kind)
                n = int(name[1])
                for i in range(2):
                    cols = slice((2 * n + i) * P, (2 * n + i + 1) * P)
                    last = split_products(e, PJ[bank][:, 256 * i:256 * i + 256], [
                        (sw_hi[:, w, c, cols], sw_lo[:, w, c, cols], sxt_hi[:, c, :], sxt_lo[:, c, :])
                        for c in range(DC)], before_last if i else None)
                last.then_inc(G.pj_full[bank], 1)

            def v_proj(u, t, kind="full", before_last=None):
                bank = begin(u, f"V{t}", kind)
                rows = slice(t * P, t * P + P)
                split_products(e, PJ[bank][:], [
                    (sxt_hi[:, c, rows], sxt_lo[:, c, rows], sw_hi[:, 2, c, :], sw_lo[:, 2, c, :])
                    for c in range(DC)], before_last).then_inc(G.pj_full[bank], 1)

            def scores(u, t):
                wait(e, G.s_free, total(u, NT, t))
                for r in (0, 2, 1, 3):
                    rows, half = slice(DK * r, DK * r + DK), SEQ * (r % 2)
                    for c in range(DC):
                        slot = SLOT[2 * c + r // 2]
                        for b in range(2):
                            col = slot * P + b * SEQ
                            last = nc.tensor.matmul(S[half:half + SEQ, col:col + SEQ],
                                                    sq_t[rows, parity(u), c, 2 * t + b, :],
                                                    sk_t[rows, parity(u), c, 2 * t + b, :],
                                                    start=True, stop=True)
                last.then_inc(G.s_full, 1)

            def transposes(u, t):
                wait(e, G.pt_ready, total(u, NT, t))
                wait(e, G.p_ready, total(u, NT, t + 1))
                for i in range(8):
                    last = nc.tensor.transpose(PT[:, i * P:i * P + P], s_p[:, i * P:i * P + P],
                                               ident[:])
                last.then_inc(G.pt_full, 1)

            def attend_waits(u, t):
                wait(e, G.a_ready, total(u, NT, t))
                wait(e, G.pt_ready, total(u, NT, t + 1))

            def attend(u, t):
                for b in range(2):
                    rows = slice(SEQ * b, SEQ * b + SEQ)
                    for head in range(HEADS):
                        at = SLOT[head // 2] * P + SEQ * (head % 2)
                        last = nc.tensor.matmul(PV_HEADS[rows, head // 8, head % 8, :],
                                                s_pt[rows, at:at + SEQ], sv[rows, parity(u), t, head, :],
                                                start=True, stop=True)
                last.then_inc(G.pv_done, 1)

            def a_transpose(u, t, kind):
                bank = begin(u, f"A{t}", kind)
                wait(e, G.a_ready, total(u, NT, t + 1))
                a = s_a[:].rearrange("p h d -> p (h d)")
                for c in range(DC):
                    last = nc.tensor.transpose(PJ[bank][:, c * P:c * P + P], a[:, c * P:c * P + P],
                                               ident[:])
                last.then_inc(G.pj_full[bank], 1)

            def o_proj(u, t, kind):
                bank = begin(u, f"O{t}", kind)
                b, before = SB.at(u, f"A{t}", kind)
                wait(e, G.pj_free[b], before + 1)
                split_products(e, PJ[bank][:], [
                    (sat_hi[:, c, :], sat_lo[:, c, :], sw_hi[:, 3, c, :], sw_lo[:, 3, c, :])
                    for c in range(DC)]).then_inc(G.pj_full[bank], 1)

            def step(u, kind):
                more = kind != "last"
                scores(u, 0)
                if more:
                    qk_proj(u, "Q0", 0, kind)
                scores(u, 1)
                transposes(u, 0)
                if more:
                    qk_proj(u, "Q1", 0, kind, lambda: attend_waits(u, 0))
                else:
                    attend_waits(u, 0)
                attend(u, 0)
                if more:
                    qk_proj(u, "K0", 1, kind)
                a_transpose(u, 0, kind)
                if more:
                    qk_proj(u, "K1", 1, kind)
                o_proj(u, 0, kind)
                transposes(u, 1)
                if more:
                    v_proj(u, 0, kind, lambda: attend_waits(u, 1))
                else:
                    attend_waits(u, 1)
                attend(u, 1)
                if more:
                    v_proj(u, 1, kind)
                a_transpose(u, 1, kind)
                if kind == "full":
                    x_transpose(u, later(u, 2), 0)
                    x_transpose(u, later(u, 2), 1)
                o_proj(u, 1, kind)

            e.wait_ge(sw_lo_ready, 4)
            e.wait_ge(self_ones, 1)
            for t in range(NT):
                x_transpose(None, Unit(0, 0), t)
            for bank in range(2):
                e.wait_ge(G.pj_free[bank], 1)
            for n in range(2):
                qk_proj(None, f"Q{n}", 0)
            for n in range(2):
                qk_proj(None, f"K{n}", 1)
            for t in range(NT):
                v_proj(None, t)
            for t in range(NT):
                x_transpose(None, Unit(0, 1), t, f"Y{t}")
            for bank in range(2):
                e.wait_ge(G.pj_free[bank], SB.drained(bank))
            run_steps(e, S_UNITS, step)

        def self_act(e):
            def full(u, name, kind="full"):
                bank, before = SB.at(u, name, kind)
                wait(e, G.pj_full[bank], before + 1)
                return bank

            def x_hi(u, v, t, name=None):
                bank = full(u, name or f"X{t}")
                nc.scalar.activation(sxt_hi[:, :, t * P:t * P + P],
                                     PJ[bank][:].rearrange("p (c s) -> p c s", c=DC),
                                     ACT.Copy).then_inc(G.xt_hi, 1)

            def a_hi(u, t, kind):
                bank = full(u, f"A{t}", kind)
                nc.scalar.activation(sat_hi[:].rearrange("p c s -> p (c s)"), PJ[bank][:],
                                     ACT.Copy).then_inc(G.at_hi, 1)

            def qk_out(u, v, name, kind="full"):
                bank = full(u, name, kind)
                n = int(name[1])
                dst, bias = (sq_t, bq_sb) if name[0] == "Q" else (sk_t, bk_sb)
                for i in range(2):
                    last = nc.scalar.activation(
                        dst[:, parity(v), 2 * n + i, :, :].rearrange("p b s -> p (b s)"),
                        PJ[bank][:, 256 * i:256 * i + 256], ACT.Identity,
                        bias=bias[:, 2 * n + i:2 * n + i + 1])
                last.then_inc(G.pj_free[bank], 1)

            def exponentials(u, t):
                wait(e, G.s_free, total(u, NT, t + 1))
                nc.scalar.activation(s_p[:], s_s[:], ACT.Exp, scale=SCORE_SCALE) \
                    .then_inc(G.p_ready, 1)

            def probs_t_out(u, t):
                wait(e, G.pt_full, total(u, NT, t + 1))
                wait(e, G.pv_done, total(u, NT, t))
                nc.scalar.activation(s_pt[:], PT[:], ACT.Copy).then_inc(G.pt_ready, 1)

            def step(u, kind):
                v, more = later(u, 1), kind != "last"
                exponentials(u, 0)
                if more:
                    qk_out(u, v, "Q0", kind)
                probs_t_out(u, 0)
                exponentials(u, 1)
                if more:
                    qk_out(u, v, "Q1", kind)
                    qk_out(u, v, "K0", kind)
                a_hi(u, 0, kind)
                if more:
                    qk_out(u, v, "K1", kind)
                probs_t_out(u, 1)
                a_hi(u, 1, kind)
                if kind == "full":
                    x_hi(u, later(u, 2), 0)
                    x_hi(u, later(u, 2), 1)

            e.wait_ge(cross_done, 1)
            for n in range(4):
                e.wait_ge(sw_in[n % 2], 16 * (n // 2 + 1))
                nc.scalar.activation(sw_hi[:, n].rearrange("p c d -> p (c d)"), s_stage(n),
                                     ACT.Copy).then_inc(sw_hi_ready, 1)
            e.wait_ge(self_bias_in, 64)
            e.wait_ge(sw_lo_ready, 4)
            for t in range(NT):
                x_hi(None, Unit(0, 0), t)
            for name in ("Q0", "Q1", "K0", "K1"):
                qk_out(None, Unit(0, 0), name)
            for t in range(NT):
                x_hi(None, Unit(0, 1), t, f"Y{t}")
            run_steps(e, S_UNITS, step)

        def self_dve(e):
            def full(u, name, kind="full"):
                bank, before = SB.at(u, name, kind)
                wait(e, G.pj_full[bank], before + 1)
                return bank

            def ln_statistics(v):
                wait(e, G.x_in[parity(v)], total_of_parity(v, 16 * NT, 16 * NT))
                for t in range(NT):
                    nc.vector.bn_stats(stats[:, t, :], sx[:, parity(v), t, :]).then_inc(G.stats, 1)

            def ln_normalise(v):
                for t in range(NT):
                    nc.vector.bn_aggr(mean_var[:, t, :], stats[:, t, :]).then_inc(G.agg, 1)
                for t in range(NT):
                    wait(e, G.rstd, total(v, NT, t + 1))
                    nc.vector.tensor_scalar(sxn[:, t, :], sx[:, parity(v), t, :],
                                            mean_var[:, t, 0:1], rstd[:, t, :],
                                            ALU.subtract, ALU.mult).then_inc(G.xn, 1)

            def x_lo(u, v, t, name=None):
                bank = full(u, name or f"X{t}")
                wait(e, G.xt_hi, total(v, NT, t + 1))
                nc.vector.tensor_tensor(sxt_lo[:, :, t * P:t * P + P],
                                        PJ[bank][:].rearrange("p (c s) -> p c s", c=DC),
                                        sxt_hi[:, :, t * P:t * P + P].bitcast(F32),
                                        ALU.subtract).then_inc(G.pj_free[bank], 1)

            def a_lo(u, t, kind):
                bank = full(u, f"A{t}", kind)
                wait(e, G.at_hi, total(u, NT, t + 1))
                nc.vector.tensor_tensor(sat_lo[:].rearrange("p c s -> p (c s)"), PJ[bank][:],
                                        sat_hi[:].rearrange("p c s -> p (c s)").bitcast(F32),
                                        ALU.subtract).then_inc(G.pj_free[bank], 1)

            def values_out(u, v, t, kind="full"):
                bank = full(u, f"V{t}", kind)
                nc.vector.tensor_tensor(sv[:, parity(v), t, :, 0:DK],
                                        PJ[bank][:].rearrange("p (h d) -> p h d", d=DK),
                                        bv_sb[:].rearrange("p (h d) -> p h d", d=DK),
                                        ALU.add).then_inc(G.pj_free[bank], 1)

            def softmax(u, t):
                rows = lambda a: a[:].rearrange("p (g k) -> p g k", g=HEADS)
                wait(e, G.s_full, total(u, NT, t + 1))
                nc.vector.reduce_max(row_max[:], rows(S), AXIS.X).then_inc(G.s_max, 1)
                wait(e, G.s_max, total(u, NT, t + 1))
                wait(e, G.p_ready, total(u, NT, t))
                nc.vector.tensor_tensor(rows(s_s), rows(S),
                                        row_max[:].unsqueeze(2).to_broadcast([P, HEADS, SEQ]),
                                        ALU.subtract).then_inc(G.s_free, 1)

            def normalise(u, t):
                wait(e, G.pv_done, total(u, NT, t + 1))
                nc.vector.reciprocal(sums[:], PV_HEADS[:, :, :, DK:VW]).then_inc(G.rcp, 1)
                wait(e, G.rcp, total(u, NT, t + 1))
                nc.vector.tensor_tensor(s_a[:].rearrange("p (a h) d -> p a h d", a=2),
                                        PV_HEADS[:, :, :, 0:DK],
                                        sums[:].to_broadcast([P, 2, HEADS // 2, DK]),
                                        ALU.mult).then_inc(G.a_ready, 1)

            def residual(u, t, kind):
                bank = full(u, f"O{t}", kind)
                if t == 0:
                    wait(e, G.res, total(u, NT, NT))
                nc.vector.tensor_tensor(sres[:, parity(u), t, :], PJ[bank][:],
                                        sres[:, parity(u), t, :], ALU.add) \
                    .then_inc(G.pj_free[bank], 1)

            def step(u, kind):
                v, more, w = later(u, 1), kind != "last", later(u, 2)
                softmax(u, 0)
                if kind == "full":
                    ln_statistics(w)
                    wait(e, G.stats, total(w, NT, NT))
                softmax(u, 1)
                if kind == "full":
                    ln_normalise(w)
                normalise(u, 0)
                a_lo(u, 0, kind)
                residual(u, 0, kind)
                if more:
                    values_out(u, v, 0, kind)
                normalise(u, 1)
                if more:
                    values_out(u, v, 1, kind)
                a_lo(u, 1, kind)
                if kind == "full":
                    x_lo(u, w, 0)
                    x_lo(u, w, 1)
                residual(u, 1, kind)

            e.wait_ge(cross_done, 1)
            for n in range(4):
                e.wait_ge(sw_hi_ready, n + 1)
                nc.vector.tensor_tensor(sw_lo[:, n].rearrange("p c d -> p (c d)"), s_stage(n),
                                        sw_hi[:, n].rearrange("p c d -> p (c d)").bitcast(F32),
                                        ALU.subtract).then_inc(sw_lo_ready, 1)
            e.wait_ge(self_bias_in, 64)
            e.wait_ge(self_ones, 1)
            for n in range(2):
                v = Unit(0, n)
                ln_statistics(v)
                e.wait_ge(G.stats, NT * (n + 1))
                if n == 1:
                    for bank in range(2):
                        e.wait_ge(G.pj_full[bank], 1)
                ln_normalise(v)
                for t in range(NT):
                    x_lo(None, v, t, f"{'XY'[n]}{t}")
                if n == 0:
                    for t in range(NT):
                        values_out(None, v, t)
            run_steps(e, S_UNITS, step)

        def self_pool(e):
            def residuals(v):
                wait(e, G.x_in[parity(v)], total_of_parity(v, 16 * NT, 16 * NT))
                wait(e, G.stored[parity(v)], total_of_parity(v, 16 * NT))
                for t in range(NT):
                    e.tensor_tensor(sres[:, parity(v), t, :], sx[:, parity(v), t, :], bo_sb[:],
                                    ALU.add).then_inc(G.res, 1)

            def step(u, kind):
                if kind != "last":
                    residuals(later(u, 1))
                if kind == "full":
                    rstd_of(e, G.agg, G.eps, G.rstd, later(u, 2), NT, P)

            e.wait_ge(cross_done, 1)
            e.memset(sv[:, :, :, :, DK:VW].rearrange("p a t h o -> p (a t) (h o)"), 1.0) \
                .then_inc(self_ones, 1)
            rstd_of(e, G.agg, G.eps, G.rstd, Unit(0, 0), NT, P)
            e.wait_ge(self_bias_in, 64)
            residuals(Unit(0, 0))
            rstd_of(e, G.agg, G.eps, G.rstd, Unit(0, 1), NT, P)
            run_steps(e, S_UNITS, step)

        F_UNITS, FT, LEAD = TOKENS // (4 * P), 4, 2
        f_x2 = x2.rearrange("(u t p) d -> u t p d", t=FT, p=P)
        f_out = out.rearrange("(u t p) d -> u t p d", t=FT, p=P)
        W_PIECES = 4
        PIECE = DC * FF // W_PIECES

        def ternary_pieces():
            flat = (w1_q[:].rearrange("p c f -> p (c f)"), w2_q[:].rearrange("p c d -> p (c d)"))
            for n in range(2 * W_PIECES):
                w, cols = n // W_PIECES, slice(n % W_PIECES * PIECE, (n % W_PIECES + 1) * PIECE)
                yield n, (w1, w2)[w][:, cols], flat[w][:, cols]

        def ff_sync(e):
            def step(u, kind):
                if kind == "full":
                    w = later(u, 2)
                    wait(e, f_xn, total(u, FT, FT))
                    wait(e, f_res, total(u, FT, FT))
                    for t in range(FT):
                        e.dma_start(fx[:, parity(w), t, :], f_x2[number(w), t]) \
                            .then_inc(fx_in[parity(w)], 16)
                for t in range(FT):
                    wait(e, y_new[t], total(u, 1, 1))
                    e.dma_start(f_out[number(u), t], fres[:, parity(u), t, :]) \
                        .then_inc(f_stored[parity(u)], 16)

            e.wait_ge(self_done, 1)
            e.dma_start(b1_sb[:], b1).then_inc(ff_bias_in, 16)
            e.dma_start(b2_sb[:], b2.unsqueeze(0).to_broadcast([P, D])).then_inc(ff_bias_in, 16)
            for n in range(2):
                for t in range(FT):
                    e.dma_start(fx[:, n, t, :], f_x2[n, t]).then_inc(fx_in[n], 16)
            for again in range(2):
                for n, src, _ in ternary_pieces():
                    at = again * 2 * W_PIECES + n
                    wait(e, fw_free, min(at - 1, 2 * W_PIECES))
                    wait(e, fw_ready, at - 2 * W_PIECES - 1)
                    e.dma_start(f_stage[:, at % 2, :], src).then_inc(fw_in[at % 2], 16)
            run_steps(e, F_UNITS, step)
            for i in range(2):
                e.wait_ge(f_stored[i], 16 * FT * F_UNITS // 2)

        def ff_pe(e):
            def x_transpose(v, t):
                wait(e, xb_free, total(v, FT, t - 1))
                wait(e, f_xn, total(v, FT, t + 1))
                for c in range(DC):
                    last = nc.tensor.transpose(XB[t % 2][:, c * P:c * P + P],
                                               fxn[:, t % 2, c * P:c * P + P], ident[:])
                last.then_inc(xb_full, 1)

            def hidden(v, m):
                wait(e, h_relu, total(v, FC, m - 1))
                if m == 0:
                    wait(e, xb_free, total(v, FT, FT))
                cols = slice(m * P, m * P + P)
                for c in range(DC):
                    for x_t in (fxt_hi, fxt_lo):
                        last = nc.tensor.matmul(PJ[m % 2][:], w1_q[:, c, cols],
                                                x_t[:, parity(v), c, :],
                                                start=(c == 0 and x_t is fxt_hi),
                                                stop=(c == DC - 1 and x_t is fxt_lo))
                last.then_inc(h_full, 1)

            def contract(u, m):
                wait(e, h_lo_ready, total(u, FC, m + 1))
                for t in range(FT):
                    if m == 0:
                        wait(e, y_new[t], total(u, 1))
                    rows = slice(t * P, t * P + P)
                    nc.tensor.matmul(YB[t], h_hi[:, m % 4, rows], w2_q[:, m, :],
                                     start=(m == 0), stop=False)
                    last = nc.tensor.matmul(YB[t], h_lo[:, m % 4, rows], w2_q[:, m, :],
                                            start=False, stop=(m == FC - 1))
                    if m == FC - 1:
                        last.then_inc(y_full[t], 1)
                    elif t == FT - 1:
                        last.then_inc(y_m, 1)

            def step(u, kind):
                v, more = later(u, 1), kind != "last"
                for m in range(FC):
                    if m + LEAD < FC:
                        hidden(u, m + LEAD)
                    elif more:
                        hidden(v, m + LEAD - FC)
                    contract(u, m)
                    if more and m in (3, 5, 7, 9):
                        x_transpose(v, (m - 3) // 2)

            e.wait_ge(self_done, 1)
            e.wait_ge(fw_abs, 1)
            nc.tensor.matmul(XB[0][:, 0:2], ones[:], abs_total[:], start=True, stop=True) \
                .then_inc(fw_total, 1)
            e.wait_ge(fw_thresh, 1)
            for t in range(FT):
                x_transpose(Unit(0, 0), t)
            e.wait_ge(fw_ready, 2 * W_PIECES)
            for m in range(LEAD):
                hidden(Unit(0, 0), m)
            run_steps(e, F_UNITS, step)

        def ff_act(e):
            def x_hi(v, t):
                wait(e, xb_full, total(v, FT, t + 1))
                nc.scalar.activation(fxt_hi[:, parity(v), :, t * P:t * P + P],
                                     XB[t % 2].rearrange("p (c s) -> p c s", c=DC),
                                     ACT.Copy).then_inc(fxt_hi_ready, 1)

            def relu(v, m):
                wait(e, h_full, total(v, FC, m + 1))
                wait(e, h_lo_ready, total(v, FC, m - 1))
                nc.scalar.activation(h_raw[:, m % 2, :], PJ[m % 2][:], ACT.Relu,
                                     bias=b1_sb[:, m:m + 1]).then_inc(h_relu, 1)

            def step(u, kind):
                v, more = later(u, 1), kind != "last"
                for m in range(FC):
                    if m + LEAD < FC:
                        relu(u, m + LEAD)
                    elif more:
                        relu(v, m + LEAD - FC)
                    if more and m in (3, 5, 7, 9):
                        x_hi(v, (m - 3) // 2)

            e.wait_ge(self_done, 1)
            e.wait_ge(ff_bias_in, 32)
            for n, _, _ in ternary_pieces():
                e.wait_ge(fw_in[n % 2], 16 * (n // 2 + 1))
                if n:
                    e.wait_ge(fw_free, n)
                nc.scalar.activation(f_neg[:], f_stage[:, n % 2, :], ACT.Abs,
                                     accum_out=abs_sum[:, n // W_PIECES, n % W_PIECES:
                                                       n % W_PIECES + 1]).then_inc(fw_free, 1)
            for t in range(FT):
                x_hi(Unit(0, 0), t)
            for m in range(LEAD):
                relu(Unit(0, 0), m)
            run_steps(e, F_UNITS, step)

        def ff_dve(e):
            def ln_statistics(v):
                wait(e, fx_in[parity(v)], total_of_parity(v, 16 * FT, 16 * FT))
                for t in range(FT):
                    nc.vector.bn_stats(stats[:, t, :], fx[:, parity(v), t, :]).then_inc(f_stats, 1)

            def ln_aggregate():
                for t in range(FT):
                    nc.vector.bn_aggr(mean_var[:, t, :], stats[:, t, :]).then_inc(f_agg, 1)

            def ln_normalise(v, t):
                wait(e, f_rstd, total(v, FT, t + 1))
                wait(e, xb_full, total(v, FT, t - 1))
                nc.vector.tensor_scalar(fxn[:, t % 2, :], fx[:, parity(v), t, :],
                                        mean_var[:, t, 0:1], rstd[:, t, :],
                                        ALU.subtract, ALU.mult).then_inc(f_xn, 1)

            def x_lo(v, t):
                wait(e, fxt_hi_ready, total(v, FT, t + 1))
                nc.vector.tensor_tensor(fxt_lo[:, parity(v), :, t * P:t * P + P],
                                        XB[t % 2].rearrange("p (c s) -> p c s", c=DC),
                                        fxt_hi[:, parity(v), :, t * P:t * P + P].bitcast(F32),
                                        ALU.subtract).then_inc(xb_free, 1)

            def split_hidden(v, m):
                wait(e, h_relu, total(v, FC, m + 1))
                nc.vector.tensor_copy(h_hi[:, m % 4, :], h_raw[:, m % 2, :]).then_inc(h_hi_ready, 1)
                wait(e, h_hi_ready, total(v, FC, m + 1))
                nc.vector.tensor_tensor(h_lo[:, m % 4, :], h_raw[:, m % 2, :],
                                        h_hi[:, m % 4, :].bitcast(F32),
                                        ALU.subtract).then_inc(h_lo_ready, 1)

            def step(u, kind):
                v, more = later(u, 1), kind != "last"
                for m in range(FC):
                    if more and m == 1:
                        wait(e, f_stats, total(v, FT, FT))
                    if m + LEAD < FC:
                        split_hidden(u, m + LEAD)
                    elif more:
                        split_hidden(v, m + LEAD - FC)
                    if more:
                        if m == 0:
                            ln_statistics(v)
                        if m == 1:
                            ln_aggregate()
                        if m in (2, 4, 6, 8):
                            ln_normalise(v, (m - 2) // 2)
                        if m in (3, 5, 7, 9):
                            x_lo(v, (m - 3) // 2)
                for t in range(FT):
                    wait(e, y_full[t], total(u, 1, 1))
                    if t == 0:
                        wait(e, f_res, total(u, FT, FT))
                    nc.vector.tensor_tensor(fres[:, parity(u), t, :], YB[t],
                                            fres[:, parity(u), t, :], ALU.add) \
                        .then_inc(y_new[t], 1)

            e.wait_ge(self_done, 1)
            e.wait_ge(fw_free, 2 * W_PIECES)
            nc.vector.reduce_sum(abs_total[:], abs_sum[:], AXIS.X).then_inc(fw_abs, 1)
            e.wait_ge(fw_total, 1)
            nc.vector.tensor_scalar(thresh[:, 0, :], XB[0][:, 0:2], 0.5 / (D * FF), 0.5 * QUANT_EPS,
                                    ALU.mult, ALU.add).then_inc(fw_thresh, 1)
            e.wait_ge(fw_thresh, 1)
            nc.vector.tensor_scalar(thresh[:, 1, :], thresh[:, 0, :], -1.0, None, ALU.mult) \
                .then_inc(fw_thresh, 1)
            e.wait_ge(fw_thresh, 2)
            first = Unit(0, 0)
            ln_statistics(first)
            e.wait_ge(f_stats, FT)
            ln_aggregate()
            for t in range(FT):
                ln_normalise(first, t)
                x_lo_after = t - 1
                if x_lo_after >= 0:
                    x_lo(first, x_lo_after)
            x_lo(first, FT - 1)
            for n, _, dst in ternary_pieces():
                at, w = 2 * W_PIECES + n, n // W_PIECES
                e.wait_ge(fw_in[at % 2], 16 * (at // 2 + 1))
                if n:
                    e.wait_ge(fw_ready, n)
                nc.vector.tensor_scalar(f_neg[:], f_stage[:, at % 2, :], thresh[:, 1, w:w + 1], None,
                                        ALU.is_lt).then_inc(fw_neg, 1)
                e.wait_ge(fw_neg, n + 1)
                nc.vector.scalar_tensor_tensor(dst, f_stage[:, at % 2, :], thresh[:, 0, w:w + 1],
                                               f_neg[:], ALU.is_gt, ALU.subtract) \
                    .then_inc(fw_ready, 1)
            for m in range(LEAD):
                split_hidden(first, m)
            run_steps(e, F_UNITS, step)

        def ff_pool(e):
            def residuals(v):
                wait(e, fx_in[parity(v)], total_of_parity(v, 16 * FT, 16 * FT))
                wait(e, f_stored[parity(v)], total_of_parity(v, 16 * FT))
                for t in range(FT):
                    e.tensor_tensor(fres[:, parity(v), t, :], fx[:, parity(v), t, :], b2_sb[:],
                                    ALU.add).then_inc(f_res, 1)

            def step(u, kind):
                if kind != "last":
                    rstd_of(e, f_agg, f_eps, f_rstd, later(u, 1), FT, P)
                    residuals(later(u, 1))

            e.wait_ge(self_done, 1)
            e.wait_ge(ff_bias_in, 32)
            rstd_of(e, f_agg, f_eps, f_rstd, Unit(0, 0), FT, P)
            residuals(Unit(0, 0))
            run_steps(e, F_UNITS, step)

        def choose(e, program):
            e.wait_ge(flag_ready, 1)
            only_last = e.value_load(flag_i[0:1, 0:1], min_val=0, max_val=1)
            with e.If(only_last):
                program(e, LAST_TILE)
                e.nop()
            with e.Else():
                program(e, ALL_TILES)
                e.nop()

        @block.sync
        def _(e):
            m = mask.rearrange("a b s k -> (a b s) k")
            for half in range(2):
                e.dma_start(mask_u8[SEQ * half:SEQ * half + SEQ, :], m).then_inc(mask_in, 16)
            for n in range(4):
                wait(e, w_lo_ready, n - 1)
                e.dma_start(cv_stage(n), w_cross[n]).then_inc(w_in[n % 2], 16)
            choose(e, cross_sync)
            if not only_cross:
                self_sync(e)
                ff_sync(e)

        @block.gpsimd
        def _(e):
            e.memset(ident[:], 0.0).then_inc(const_ready, 1)
            e.memset(ones[:], 1.0).then_inc(const_ready, 1)
            e.memset(minus_half[:], -0.5).then_inc(const_ready, 1)
            e.memset(ln_eps[:], LN_EPS).then_inc(const_ready, 1)
            e.wait_ge(const_ready, 4)
            e.affine_select(out=ident[:], in_=ident[:], compare_op=ALU.not_equal, fill=1.0, base=0,
                            pattern=[[-1, P]], channel_multiplier=1).then_inc(const_ready, 1)
            e.memset(q_pad[:].rearrange("p c a b h s -> p (c a b h s)"), 0.0).then_inc(pads_ready, 1)
            e.memset(cxn[:].rearrange("p t d -> p (t d)"), 0.0).then_inc(pads_ready, 1)
            e.wait_ge(mask_step, 1)
            e.memset(c_a[:].rearrange("p h d -> p (h d)"), 0.0).then_inc(pads_ready, 1)
            e.wait_ge(w_lo_ready, 4)
            e.memset(cv[:, :, :, :, DK:VW].rearrange("p a j h o -> p (a j) (h o)"), 1.0) \
                .then_inc(pads_ready, 1)
            choose(e, cross_pool)
            if not only_cross:
                self_pool(e)
                ff_pool(e)

        @block.scalar
        def _(e):
            for n in range(4):
                e.wait_ge(w_in[n % 2], 16 * (n // 2 + 1))
                nc.scalar.activation(cw_hi[:, n].rearrange("p c d -> p (c d)"), cv_stage(n),
                                     ACT.Copy).then_inc(w_hi_ready, 1)
            choose(e, cross_act)
            if not only_cross:
                self_act(e)
                ff_act(e)

        @block.vector
        def _(e):
            e.wait_ge(mask_in, 32)
            nc.vector.tensor_copy(mask_f, mask_u8).then_inc(mask_step, 1)
            e.wait_ge(mask_step, 1)
            nc.vector.reduce_sum(counts[:, 0:1], mask_f, AXIS.X)
            nc.vector.reduce_sum(counts[:, 1:2], mask_f[:, 0:KEYS - P], AXIS.X).then_inc(mask_step, 1)
            e.wait_ge(mask_step, 2)
            nc.vector.tensor_scalar(counts[:, 2:3], counts[:, 0:1], -1.0, float(KEYS),
                                    ALU.mult, ALU.add).then_inc(mask_step, 1)
            e.wait_ge(mask_step, 3)
            nc.vector.reciprocal(counts[:, 3:4], counts[:, 2:3]).then_inc(mask_step, 1)
            e.wait_ge(mask_step, 4)
            nc.vector.tensor_scalar(counts[:, 2:3], counts[:, 3:4], 0.0, None, ALU.mult) \
                .then_inc(mask_step, 1)
            e.wait_ge(mask_step, 5)
            nc.vector.tensor_scalar(mask_bias[:], mask_f, MASKED, counts[:, 2:3],
                                    ALU.mult, ALU.add).then_inc(mask_step, 1)
            e.wait_ge(mask_counted, 1)
            nc.vector.tensor_scalar(flag_i[0:1, 0:1], S[0:1, 0:1], float(P * (KEYS - P)), None,
                                    ALU.is_ge).then_inc(flag_ready, 1)
            for n in range(4):
                e.wait_ge(w_hi_ready, n + 1)
                nc.vector.tensor_tensor(cw_lo[:, n].rearrange("p c d -> p (c d)"), cv_stage(n),
                                        cw_hi[:, n].rearrange("p c d -> p (c d)").bitcast(F32),
                                        ALU.subtract).then_inc(w_lo_ready, 1)
            e.wait_ge(mask_step, 6)
            e.wait_ge(pads_ready, 4)
            choose(e, cross_dve)
            if not only_cross:
                self_dve(e)
                ff_dve(e)

        @block.tensor
        def _(e):
            e.wait_ge(const_ready, 5)
            e.wait_ge(mask_step, 2)
            nc.tensor.matmul(S[0:1, 0:2], counts[:, 1:2], ones[:, 0:2], start=True, stop=True) \
                .then_inc(mask_counted, 1)
            e.wait_ge(flag_ready, 1)
            choose(e, cross_pe)
            if not only_cross:
                self_pe(e)
                ff_pe(e)


def tiled(w):
    import numpy as np
    t = np.ascontiguousarray(w.T)
    return np.ascontiguousarray(t.reshape(t.shape[0] // 128, 128, t.shape[1]).transpose(1, 0, 2)) \
        .reshape(128, -1)


def kernel(x, ctx_1024, mask_1x1xSxS2_bk1, L0_xattn_W_Q, L0_xattn_W_K, L0_xattn_W_V, L0_xattn_W_O,
           L0_attn_Wq, L0_attn_bq, L0_attn_Wk, L0_attn_bk, L0_attn_Wv, L0_attn_bv, L0_attn_Wo,
           L0_attn_bo, L0_ffn_W1, L0_ffn_b1, L0_ffn_W2, L0_ffn_b2):
    import numpy as np
    import concourse.bacc as bacc
    from concourse.bass_utils import run_bass_kernel_spmd

    a = np.asarray
    ctx = np.ascontiguousarray(a(ctx_1024).reshape(BATCHES, KEY_TILES, P, DC, P)
                               .transpose(0, 1, 4, 3, 2)).reshape(BATCHES, KEY_TILES, P, DC * P)
    arrays = {
        "x": a(x).reshape(TOKENS, D),
        "ctx": ctx,
        "mask": a(mask_1x1xSxS2_bk1),
        "w_cross": np.stack([tiled(a(w)) for w in
                             (L0_xattn_W_Q, L0_xattn_W_K, L0_xattn_W_V, L0_xattn_W_O)]),
        "w_self": np.stack([tiled(a(w)) for w in
                            (L0_attn_Wq, L0_attn_Wk, L0_attn_Wv, L0_attn_Wo)]),
        "bq": np.ascontiguousarray(a(L0_attn_bq).reshape(DC, P).T),
        "bk": np.ascontiguousarray(a(L0_attn_bk).reshape(DC, P).T),
        "bv": a(L0_attn_bv),
        "bo": a(L0_attn_bo),
        "w1": tiled(a(L0_ffn_W1)),
        "b1": np.ascontiguousarray(a(L0_ffn_b1).reshape(FC, P).T),
        "w2": tiled(a(L0_ffn_W2)),
        "b2": a(L0_ffn_b2),
    }
    nc = bacc.Bacc("TRN2", target_bir_lowering=False, num_devices=1)
    args = [nc.dram_tensor(f"in_{n}", v.shape, mybir.dt.from_np(v.dtype), kind="ExternalInput").ap()
            for n, v in arrays.items()]
    out = nc.dram_tensor("out", (TOKENS, D), F32, kind="ExternalOutput").ap()
    build(nc, *args, out)
    result = run_bass_kernel_spmd(nc, [{f"in_{n}": v for n, v in arrays.items()}], core_ids=[0])
    return np.asarray(result.results[0]["out"]).reshape(BATCHES, SEQ, D)
```

```python
from collections import namedtuple
from contextlib import ExitStack

import concourse.bass as bass
import concourse.mybir as mybir

F32 = mybir.dt.float32
F32R = mybir.dt.float32r
I32 = mybir.dt.int32
U8 = mybir.dt.uint8
ALU = mybir.AluOpType
ACT = mybir.ActivationFunctionType
AXIS = mybir.AxisListType

P = 128
BATCHES, SEQ, D, KEYS = 64, 64, 512, 512
HEADS = 16
DK = D // HEADS
DC = D // P
PAIRS = HEADS // 2
VW = DK + 1
TOKENS = BATCHES * SEQ
FF = 4 * D
FC = FF // P
KEY_TILES = KEYS // P
SCORE_SCALE = float(DK) ** -0.5
MASKED = -1e30
LN_EPS = 1e-5
QUANT_EPS = 1e-5

Unit = namedtuple("Unit", "half off")


def later(u, n):
    return Unit(u.half, u.off + n)


def parity(u):
    return u.off % 2


def number(u):
    return u.half * 2 + u.off


def is_unit(u, n):
    return isinstance(u.half, int) and number(u) == n


def total(u, per_unit, k=0):
    return u.half * (2 * per_unit) + (per_unit * u.off + k)


def total_of_parity(u, per_unit, k=0):
    return u.half * per_unit + (per_unit * (u.off // 2) + k)


def wait(eng, sem, value):
    if not (isinstance(value, int) and value <= 0):
        eng.wait_ge(sem, value)


class Banks:

    def __init__(self, prologue, full, last_but_one, last):
        self.prologue = prologue
        self.uses = {"full": full, "last_but_one": last_but_one, "last": last}
        self.first, self.per = len(prologue), len(full)

    def before(self, u, name=None, kind="full"):
        if u is None:
            return self.prologue.index(name)
        fewer = self.per - len(self.uses["last_but_one"]) if kind == "last" else 0
        n = self.uses[kind].index(name) if name else 0
        return self.first + self.per * u.off - fewer + n

    def at(self, u, name, kind="full"):
        j = self.before(u, name, kind)
        earlier = (j + 1 - j % 2) // 2
        return j % 2, earlier if u is None else u.half * self.per + earlier

    def drained(self, bank):
        return (self.first + 1 - bank) // 2


def run_steps(eng, units, step):
    step(Unit(0, 0), "full")
    step(Unit(0, 1), "full")
    with eng.Fori(1, units // 2 - 1) as half:
        step(Unit(half, 0), "full")
        step(Unit(half, 1), "full")
    step(Unit(units // 2 - 1, 0), "last_but_one")
    step(Unit(units // 2 - 1, 1), "last")


def build(nc, x, ctx, mask, w_cross, w_self, bq, bk, bv, bo, w1, b1, w2, b2,
          out,
          only_cross=False):
    x1 = nc.dram_tensor("x1", (TOKENS, D), F32, kind="Internal").ap()
    x2 = nc.dram_tensor("x2", (TOKENS, D), F32, kind="Internal").ap()
    if only_cross:
        x1 = out
    outer = ExitStack()
    with outer:
        def sem(name):
            return outer.enter_context(nc.semaphore(name))

        def sems(name):
            return [sem(f"{name}_{i}") for i in range(2)]

        def sb(stack, name, shape, dt=F32):
            return stack.enter_context(nc.sbuf_tensor(name, shape, dt))

        PJ = [outer.enter_context(nc.psum_tensor(f"project_{i}", [P, 512], F32)) for i in range(2)]
        S = outer.enter_context(nc.psum_tensor("scores", [P, 1024], F32))
        PT = outer.enter_context(nc.psum_tensor("probs_t_psum", [P, 1024], F32))
        PV = outer.enter_context(nc.psum_tensor("attended", [P, 2, 512], F32))
        PV_HEADS = PV[:, :, 0:PAIRS * VW].rearrange("p a (h d) -> p a h d", d=VW)
        YB = [S[:, 0:512], S[:, 512:1024], PT[:, 0:512], PT[:, 512:1024]]
        XB = [PV[:, 0, :], PV[:, 1, :]]

        ident = sb(outer, "ident", [P, P])
        ones = sb(outer, "ones", [P, P])
        minus_half = sb(outer, "minus_half", [P, 1])
        ln_eps = sb(outer, "ln_eps", [P, 1])
        flag_i = sb(outer, "only_last_tile", [1, 2], I32)
        stats = sb(outer, "ln_stats_buf", [P, 4, 6])
        mean_var = sb(outer, "mean_var", [P, 4, 2])
        var_eps = sb(outer, "var_eps", [P, 4, 1])
        rstd = sb(outer, "rstd", [P, 4, 1])
        abs_sum = sb(outer, "abs_sum", [P, 2, FC])
        abs_total = sb(outer, "abs_total", [P, 2])
        thresh = sb(outer, "thresholds", [P, 2, 2])
        row_max = sb(outer, "row_max", [P, HEADS])
        sums = sb(outer, "row_sums", [P, 2, HEADS // 2, 1])
        bq_sb = sb(outer, "bq_sb", [P, DC])
        bk_sb = sb(outer, "bk_sb", [P, DC])
        b1_sb = sb(outer, "b1_sb", [P, FC])

        with ExitStack() as st:
            q_pad = sb(st, "q_pad", [P, DC, 2, 4, 2, SEQ])
            ck_t = sb(st, "cross_k_t", [P, 2, DC, 4, P])
            cx = sb(st, "cross_x", [P, 2, 2, D])
            cxn = sb(st, "cross_x_norm", [P, 2, D])
            cxt_hi = sb(st, "cross_xt_hi", [P, DC, 4 * SEQ], F32R)
            cxt_lo = sb(st, "cross_xt_lo", [P, DC, 4 * SEQ], F32R)
            c_sp = sb(st, "cross_scores_probs", [P, 2048])
            c_s, c_p = c_sp[:, 0:1024], c_sp[:, 1024:2048]
            c_pt = sb(st, "cross_probs_t", [P, 1024])
            cw_hi = sb(st, "cross_w_hi", [P, 4, DC, D], F32R)
            cw_lo = sb(st, "cross_w_lo", [P, 4, DC, D], F32R)
            ctx_raw = sb(st, "ctx_raw", [P, 2, 4, DC, P])
            ctx_hi = sb(st, "ctx_hi", [P, 2, 4, DC, P], F32R)
            ctx_lo = sb(st, "ctx_lo", [P, 2, 4, DC, P], F32R)
            cv = sb(st, "cross_v", [P, 2, 4, HEADS, VW])
            c_a = sb(st, "cross_a", [P, HEADS, DK])
            cat_hi = sb(st, "cross_at_hi", [P, DC, P], F32R)
            cat_lo = sb(st, "cross_at_lo", [P, DC, P], F32R)
            mask_bias = sb(st, "mask_bias", [P, KEYS])
            counts = sb(st, "mask_counts", [P, 4])
            mask_u8 = c_a.rearrange("p h d -> p (h d)").bitcast(U8)[:, 0:KEYS]
            mask_f = c_pt[:, 0:KEYS]
        with ExitStack() as st:
            w_raw = sb(st, "ff_w_raw", [P, 2, FC, 512])
        f_weights = ExitStack()
        outer.enter_context(f_weights)
        w1_q = sb(f_weights, "w1_ternary", [P, DC, FF], F32R)
        w2_q = sb(f_weights, "w2_ternary", [P, FC, D], F32R)
        with ExitStack() as st:
            sw_hi = sb(st, "self_w_hi", [P, 4, DC, D], F32R)
            sw_lo = sb(st, "self_w_lo", [P, 4, DC, D], F32R)
            sq_t = sb(st, "self_q_t", [P, 2, DC, 4, SEQ])
            sk_t = sb(st, "self_k_t", [P, 2, DC, 4, SEQ])
            sres = sb(st, "self_residual", [P, 2, 2, D])
            sv = sb(st, "self_v", [P, 2, 2, HEADS, VW])
            sx = sb(st, "self_x", [P, 2, 2, D])
            sxn = sb(st, "self_x_norm", [P, 2, D])
            bv_sb = sb(st, "bv_sb", [P, D])
            bo_sb = sb(st, "bo_sb", [P, D])
            sxt_hi = sb(st, "self_xt_hi", [P, DC, 4 * SEQ], F32R)
            sxt_lo = sb(st, "self_xt_lo", [P, DC, 4 * SEQ], F32R)
            s_s = sb(st, "self_scores", [P, 1024])
            s_p = sb(st, "self_probs", [P, 1024])
            s_pt = sb(st, "self_probs_t", [P, 1024])
            s_a = sb(st, "self_a", [P, HEADS, DK])
            sat_hi = sb(st, "self_at_hi", [P, DC, P], F32R)
            sat_lo = sb(st, "self_at_lo", [P, DC, P], F32R)
            f_scratch = sb(st, "ff_weight_scratch", [P, 512])
            s_stages = [sq_t[:].rearrange("p a c b s -> p (a c b s)"),
                        sk_t[:].rearrange("p a c b s -> p (a c b s)"),
                        sv[:].rearrange("p a t h d -> p (a t h d)")[:, 0:DC * D],
                        sres[:].rearrange("p a t d -> p (a t d)")]
        with ExitStack() as st:
            fx = sb(st, "ff_x", [P, 2, 4, D])
            fxn = sb(st, "ff_x_norm", [P, 2, D])
            b2_sb = sb(st, "b2_sb", [P, D])
            sb(st, "ff_gap", [P, D])
            h_hi = sb(st, "hidden_hi", [P, 4, 512], F32R)
            fxt_0 = sb(st, "ff_xt_0", [P, 2, DC, 4 * P], F32R)
            fres = sb(st, "ff_residual", [P, 2, 4, D])
            h_lo = sb(st, "hidden_lo", [P, 4, 512], F32R)
            h_raw = sb(st, "hidden", [P, 2, 512])
            fxt_1 = sb(st, "ff_xt_1", [P, 2, DC, 4 * P], F32R)
            fxt_hi = [t[:, 0] for t in (fxt_0, fxt_1)]
            fxt_lo = [t[:, 1] for t in (fxt_0, fxt_1)]

        const_ready = sem("const_ready")
        mask_in = sem("mask_in")
        mask_step = sem("mask_step")
        mask_counted = sem("mask_counted")
        flag_ready = sem("flag_ready")
        w_in = [sem(f"w_in_{n}") for n in range(4)]
        w_hi_ready = sem("w_hi_ready")
        w_lo_ready = sem("w_lo_ready")
        pads_ready = sem("pads_ready")

        class Phase:
            def __init__(self, name):
                s = lambda n: sem(f"{name}_{n}")
                self.x_in = [s(f"x_in_{i}") for i in range(2)]
                self.stats = s("stats")
                self.agg = s("agg")
                self.eps = s("eps")
                self.rstd = s("rstd")
                self.xn = s("xn")
                self.res = s("residual")
                self.pj_full = [s(f"pj_full_{i}") for i in range(2)]
                self.pj_free = [s(f"pj_free_{i}") for i in range(2)]
                self.xt_hi = s("xt_hi")
                self.at_hi = s("at_hi")
                self.s_full = s("s_full")
                self.s_free = s("s_free")
                self.s_max = s("s_max")
                self.s_sub = s("s_sub")
                self.p_ready = s("p_ready")
                self.pt_full = s("pt_full")
                self.pt_ready = s("pt_ready")
                self.pv_done = s("pv_done")
                self.rcp = s("rcp")
                self.a_ready = s("a_ready")
                self.stored = [s(f"stored_{i}") for i in range(2)]

        C = Phase("cross")
        ctx_in = sems("ctx_in")
        ctx_hi_ready = sem("ctx_hi_ready")
        ctx_lo_ready = sem("ctx_lo_ready")
        G = Phase("self")
        cross_w_used = sem("cross_w_used")
        self_bias_in = sem("self_bias_in")
        sw_in = [sem(f"sw_in_{n}") for n in range(4)]
        sw_hi_ready = sem("sw_hi_ready")
        sw_lo_ready = sem("sw_lo_ready")
        self_ones = sem("self_ones")
        ff_bias_in = sem("ff_bias_in")
        fw_in = sems("fw_in")
        fw_summed = sem("fw_summed")
        fw_abs = sem("fw_abs")
        fw_total = sem("fw_total")
        fw_thresh = sem("fw_thresh")
        fw_neg = sem("fw_neg")
        fw_ready = sem("fw_ready")
        fx_in = sems("fx_in")
        f_stats, f_agg, f_eps, f_rstd, f_xn, f_res = (
            sem("f_stats"), sem("f_agg"), sem("f_eps"), sem("f_rstd"), sem("f_xn"), sem("f_res"))
        xb_full, xb_free, fxt_hi_ready = sem("xb_full"), sem("xb_free"), sem("fxt_hi_ready")
        h_full, h_relu, h_hi_ready, h_lo_ready = (
            sem("h_full"), sem("h_relu"), sem("h_hi_ready"), sem("h_lo_ready"))
        y_m = sem("y_m")
        y_full = [sem(f"y_full_{t}") for t in range(4)]
        y_new = [sem(f"y_new_{t}") for t in range(4)]
        f_stored = sems("f_stored")

        def split_products(e, out_ap, pairs, before_last=None):
            n = 0
            last = None
            for s_hi, s_lo, m_hi, m_lo in pairs:
                for a, b in ((s_hi, m_hi), (s_hi, m_lo), (s_lo, m_hi)):
                    if before_last and n == 3 * len(pairs) - 1:
                        before_last()
                    last = nc.tensor.matmul(out_ap, a, b, start=(n == 0),
                                            stop=(n == 3 * len(pairs) - 1))
                    n += 1
            return last

        W_ORDER = (1, 0, 2, 3)
        c_stages = [cv[:, 0].rearrange("p j h d -> p (j h d)")[:, 0:DC * D],
                    cv[:, 1].rearrange("p j h d -> p (j h d)")[:, 0:DC * D],
                    ck_t[:, 1].rearrange("p c j k -> p (c j k)"), c_sp[:]]
        flat_w = lambda t, n: t[:, n].rearrange("p c d -> p (c d)")

        def load_cross_w(e, n):
            e.dma_start(c_stages[n], w_cross[W_ORDER[n]]).then_inc(w_in[n], 16)

        def cross_w_hi(e, n):
            e.wait_ge(w_in[n], 16)
            nc.scalar.activation(flat_w(cw_hi, W_ORDER[n]), c_stages[n], ACT.Copy) \
                .then_inc(w_hi_ready, 1)

        def cross_w_lo(e, n):
            e.wait_ge(w_hi_ready, n + 1)
            nc.vector.tensor_tensor(flat_w(cw_lo, W_ORDER[n]), c_stages[n],
                                    flat_w(cw_hi, W_ORDER[n]).bitcast(F32), ALU.subtract) \
                .then_inc(w_lo_ready, 1)

        def load_self_w(e, n):
            e.dma_start(s_stages[n], w_self[n]).then_inc(sw_in[n], 16)

        def self_w_hi(e, n):
            e.wait_ge(sw_in[n], 16)
            nc.scalar.activation(flat_w(sw_hi, n), s_stages[n], ACT.Copy).then_inc(sw_hi_ready, 1)

        def self_w_lo(e, n):
            e.wait_ge(sw_hi_ready, n + 1)
            nc.vector.tensor_tensor(flat_w(sw_lo, n), s_stages[n],
                                    flat_w(sw_hi, n).bitcast(F32), ALU.subtract) \
                .then_inc(sw_lo_ready, 1)

        S_UNITS, NT = TOKENS // (4 * SEQ), 2
        s_x1 = x1.rearrange("(u t p) d -> u t p d", t=NT, p=P)
        s_x2 = x2.rearrange("(u t p) d -> u t p d", t=NT, p=P)

        def load_self_x(e, v):
            wait(e, G.xn, total(v, NT, -NT))
            wait(e, G.res, total(v, NT, -NT))
            for t in range(NT):
                e.dma_start(sx[:, parity(v), t, :], s_x1[number(v), t]) \
                    .then_inc(G.x_in[parity(v)], 16)

        def self_ln_statistics(e, v):
            wait(e, G.x_in[parity(v)], total_of_parity(v, 16 * NT, 16 * NT))
            for t in range(NT):
                nc.vector.bn_stats(stats[:, t, :], sx[:, parity(v), t, :]).then_inc(G.stats, 1)

        def self_ln_normalise(e, v):
            for t in range(NT):
                nc.vector.bn_aggr(mean_var[:, t, :], stats[:, t, :]).then_inc(G.agg, 1)
            for t in range(NT):
                wait(e, G.rstd, total(v, NT, t + 1))
                nc.vector.tensor_scalar(sxn[:, t, :], sx[:, parity(v), t, :],
                                        mean_var[:, t, 0:1], rstd[:, t, :],
                                        ALU.subtract, ALU.mult).then_inc(G.xn, 1)

        class Cross:
            def __init__(self, kt):
                self.kt, self.b = kt, 4 // kt
                self.units = BATCHES // self.b
                self.tokens = self.b * SEQ
                self.nt = max(1, self.b // 2)
                self.tp = min(P, self.tokens)
                two = self.nt == 2
                full = (["K0", "K1", "K2", "K3", "X0"] + ["X1"] * two + ["V0", "V1"] + ["A0"] * two
                        + ["V2"] + ["O0"] * two
                        + ["Q0", "Q1", "V3", f"A{self.nt - 1}", f"O{self.nt - 1}"])
                self.banks = Banks(
                    [f"K{i}" for i in range(4)] + [f"X{t}" for t in range(self.nt)]
                    + ["Q0", "Q1"] + [f"V{i}" for i in range(4)],
                    full, full, [n for n in full if n[0] in "AO"])
                self.x = x.rearrange("(u t p) d -> u t p d", t=self.nt, p=self.tp)
                self.x1 = x1.rearrange("(u t p) d -> u t p d", t=self.nt, p=self.tp)
                self.ctx = (ctx.rearrange("(u b) k p n -> u b k p n", b=self.b)[:, :, 3]
                            if kt == 1 else ctx)
                self.tile_of = (lambda q: q // 2) if two else (lambda q: 0)

        def cross_sync(e, K):
            def load_ctx(v):
                wait(e, ctx_lo_ready, total(v, 1, -1))
                for j in range(4):
                    e.dma_start(ctx_raw[:, parity(v), j, :, :].rearrange("p c k -> p (c k)"),
                                K.ctx[number(v), j]).then_inc(ctx_in[parity(v)], 16)

            def load_x(v):
                for t in range(K.nt):
                    e.dma_start(cx[0:K.tp, parity(v), t, :], K.x[number(v), t]) \
                        .then_inc(C.x_in[parity(v)], 16)

            def step(u, kind):
                more, ahead = kind != "last", kind == "full"
                if ahead:
                    load_ctx(later(u, 2))
                elif more:
                    wait(e, ctx_lo_ready, total(u, 1, 2))
                    load_self_w(e, 0)
                    load_self_w(e, 1)
                else:
                    bank, before = K.banks.at(later(u, -1), "V3", "last_but_one")
                    e.wait_ge(C.pj_free[bank], before + 1)
                    load_self_w(e, 2)
                    for i in range(2):
                        e.wait_ge(C.stored[i], 16 * K.nt * (K.units // 2 - 1))
                    load_self_x(e, Unit(0, 0))
                    load_self_w(e, 3)
                    load_self_x(e, Unit(0, 1))
                    for dst, src in ((bq_sb, bq), (bk_sb, bk), (b1_sb, b1)):
                        e.dma_start(dst[:], src).then_inc(self_bias_in, 16)
                    for dst, src in ((bv_sb, bv), (bo_sb, bo)):
                        e.dma_start(dst[:], src.unsqueeze(0).to_broadcast([P, D])) \
                            .then_inc(self_bias_in, 16)
                for t in range(K.nt):
                    bank, before = K.banks.at(u, f"O{t}", kind)
                    wait(e, C.pj_free[bank], before + 1)
                    e.dma_start(K.x1[number(u), t], cx[0:K.tp, parity(u), t, :]) \
                        .then_inc(C.stored[parity(u)], 16)
                if ahead:
                    wait(e, C.stored[parity(u)], total_of_parity(u, 16 * K.nt, 16 * K.nt))
                    load_x(later(u, 2))

            load_ctx(Unit(0, 0))
            load_x(Unit(0, 0))
            for n in range(1, 4):
                load_cross_w(e, n)
            load_ctx(Unit(0, 1))
            load_x(Unit(0, 1))
            run_steps(e, K.units, step)
            for i in range(2):
                e.wait_ge(C.stored[i], 16 * K.nt * K.units // 2)

        def cross_pe(e, K):
            def begin(u, name, kind="full"):
                bank, before = K.banks.at(u, name, kind)
                wait(e, C.pj_free[bank], before)
                return bank

            def k_proj(u, v, m):
                bank = begin(u, f"K{m}")
                if m == 0:
                    wait(e, ctx_lo_ready, total(v, 1, 1))
                w = slice(m * P, m * P + P)
                split_products(e, PJ[bank][:], [
                    (cw_hi[:, 1, c, w], cw_lo[:, 1, c, w],
                     ctx_hi[:, parity(v), :, c, :], ctx_lo[:, parity(v), :, c, :])
                    for c in range(DC)]).then_inc(C.pj_full[bank], 1)

            def v_proj(u, v, j):
                bank = begin(u, f"V{j}")
                split_products(e, PJ[bank][:], [
                    (ctx_hi[:, parity(v), j, c, :], ctx_lo[:, parity(v), j, c, :],
                     cw_hi[:, 2, c, :], cw_lo[:, 2, c, :])
                    for c in range(DC)]).then_inc(C.pj_full[bank], 1)

            def x_transpose(u, v, t):
                bank = begin(u, f"X{t}")
                wait(e, C.xn, total(v, K.nt, t + 1))
                for c in range(DC):
                    last = nc.tensor.transpose(PJ[bank][:, c * P:c * P + P],
                                               cxn[:, t, c * P:c * P + P], ident[:])
                last.then_inc(C.pj_full[bank], 1)

            def q_proj(u, n):
                bank = begin(u, f"Q{n}")
                if n == 0:
                    for t in range(K.nt):
                        b, before = K.banks.at(u, f"X{t}")
                        wait(e, C.pj_free[b], before + 1)
                for i in range(2):
                    w = slice((2 * n + i) * P, (2 * n + i + 1) * P)
                    last = split_products(e, PJ[bank][:, 256 * i:256 * i + K.tokens], [
                        (cw_hi[:, 0, c, w], cw_lo[:, 0, c, w],
                         cxt_hi[:, c, 0:K.tokens], cxt_lo[:, c, 0:K.tokens]) for c in range(DC)])
                last.then_inc(C.pj_full[bank], 1)

            def scores(u, q):
                wait(e, C.s_free, total(u, 4, q))
                n = K.kt * P
                for i in range(PAIRS // K.kt):
                    pair = i if K.kt == 1 else q * (PAIRS // K.kt) + i
                    batch = q if K.kt == 1 else 0
                    keys = (ck_t[:, parity(u), pair // 2, q, :] if K.kt == 1 else
                            ck_t[:, parity(u), pair // 2, :, :].rearrange("p j k -> p (j k)"))
                    last = nc.tensor.matmul(
                        S[:, i * n:(i + 1) * n],
                        q_pad[:, pair // 2, pair % 2, batch, :, :].rearrange("p a s -> p (a s)"),
                        keys, start=True, stop=True)
                last.then_inc(C.s_full, 1)

            def transposes(u, q):
                wait(e, C.pt_ready, total(u, 4, q))
                wait(e, C.p_ready, total(u, 4, q + 1))
                for i in range(8):
                    last = nc.tensor.transpose(PT[:, i * P:i * P + P], c_p[:, i * P:i * P + P],
                                               ident[:])
                last.then_inc(C.pt_full, 1)

            def attend(u, q):
                t = K.tile_of(q)
                if q == 0 or t != K.tile_of(q - 1):
                    wait(e, C.a_ready, total(u, K.nt, t))
                wait(e, C.pt_ready, total(u, 4, q + 1))
                row = SEQ * (q % 2) if K.kt == 1 else 0
                for i in range(HEADS // K.kt):
                    head = i if K.kt == 1 else q * (HEADS // K.kt) + i
                    for k in range(K.kt):
                        block = (i // 2) * K.kt + k
                        at = block * P + SEQ * (head % 2)
                        last = nc.tensor.matmul(
                            PV_HEADS[row:row + SEQ, head // 8, head % 8, :], c_pt[:, at:at + SEQ],
                            cv[:, parity(u), q if K.kt == 1 else k, head, :],
                            start=(k == 0), stop=(k == K.kt - 1))
                last.then_inc(C.pv_done, 1)

            def a_transpose(u, t, kind):
                bank = begin(u, f"A{t}", kind)
                wait(e, C.a_ready, total(u, K.nt, t + 1))
                a = c_a[:, :, :].rearrange("p h d -> p (h d)")
                for c in range(DC):
                    last = nc.tensor.transpose(PJ[bank][:, c * P:c * P + P],
                                               a[:, c * P:c * P + P], ident[:])
                last.then_inc(C.pj_full[bank], 1)

            def o_proj(u, t, kind):
                bank = begin(u, f"O{t}", kind)
                b, before = K.banks.at(u, f"A{t}", kind)
                wait(e, C.pj_free[b], before + 1)
                split_products(e, PJ[bank][0:K.tp, :], [
                    (cat_hi[:, c, 0:K.tp], cat_lo[:, c, 0:K.tp], cw_hi[:, 3, c, :], cw_lo[:, 3, c, :])
                    for c in range(DC)]).then_inc(C.pj_full[bank], 1)

            def step(u, kind):
                more, ahead = kind != "last", kind == "full"
                v = later(u, 1)
                scores(u, 0)
                if is_unit(u, 0):
                    e.wait_ge(w_lo_ready, 4)
                else:
                    o_proj(later(u, -1), K.nt - 1, "last_but_one" if kind == "last" else "full")
                if more:
                    k_proj(u, v, 0)
                scores(u, 1)
                transposes(u, 0)
                if more:
                    k_proj(u, v, 1)
                    attend(u, 0)
                    k_proj(u, v, 2)
                    scores(u, 2)
                else:
                    scores(u, 2)
                    attend(u, 0)
                transposes(u, 1)
                if more:
                    k_proj(u, v, 3)
                    attend(u, 1)
                    for t in range(K.nt):
                        x_transpose(u, v, t)
                    scores(u, 3)
                else:
                    scores(u, 3)
                    attend(u, 1)
                transposes(u, 2)
                if more:
                    v_proj(u, v, 0)
                    v_proj(u, v, 1)
                attend(u, 2)
                if K.nt == 2:
                    a_transpose(u, 0, kind)
                if more:
                    v_proj(u, v, 2)
                if K.nt == 2:
                    o_proj(u, 0, kind)
                transposes(u, 3)
                if more:
                    q_proj(u, 0)
                attend(u, 3)
                if more:
                    q_proj(u, 1)
                    v_proj(u, v, 3)
                a_transpose(u, K.nt - 1, kind)
                if not more:
                    o_proj(u, K.nt - 1, kind)

            first = Unit(0, 0)
            e.wait_ge(w_lo_ready, 1)
            for m in range(4):
                k_proj(None, first, m)
            e.wait_ge(pads_ready, 3)
            for t in range(K.nt):
                x_transpose(None, first, t)
            e.wait_ge(w_lo_ready, 2)
            q_proj(None, 0)
            q_proj(None, 1)
            e.wait_ge(w_lo_ready, 3)
            for j in range(4):
                v_proj(None, first, j)
            run_steps(e, K.units, step)
            last = Unit(K.units // 2 - 1, 1)
            for name in ("A", "O"):
                bank, before = K.banks.at(last, f"{name}{K.nt - 1}", "last")
                e.wait_ge(C.pj_free[bank], before + 1)
            e.nop().then_inc(cross_w_used, 1)

        def cross_act(e, K):
            def full(u, name, kind="full"):
                bank, before = K.banks.at(u, name, kind)
                wait(e, C.pj_full[bank], before + 1)
                return bank

            def keys_out(u, v, m):
                bank = full(u, f"K{m}")
                nc.scalar.activation(ck_t[:, parity(v), m, :, :].rearrange("p j k -> p (j k)"),
                                     PJ[bank][:], ACT.Copy).then_inc(C.pj_free[bank], 1)

            def x_hi(u, v, t):
                bank = full(u, f"X{t}")
                nc.scalar.activation(
                    cxt_hi[:, :, t * P:t * P + K.tp],
                    PJ[bank][:].rearrange("p (c s) -> p c s", c=DC)[:, :, 0:K.tp],
                    ACT.Copy).then_inc(C.xt_hi, 1)

            def a_hi(u, t, kind):
                bank = full(u, f"A{t}", kind)
                nc.scalar.activation(
                    cat_hi[:, :, 0:K.tp],
                    PJ[bank][:].rearrange("p (c s) -> p c s", c=DC)[:, :, 0:K.tp],
                    ACT.Copy).then_inc(C.at_hi, 1)

            def queries_out(u, n):
                bank = full(u, f"Q{n}")
                chunks = PJ[bank][:].rearrange("p (i b s) -> p i b s", i=2, s=SEQ)
                for r in range(4):
                    rows = slice(DK * r, DK * r + DK)
                    last = nc.scalar.activation(
                        q_pad[rows, 2 * n:2 * n + 2, r // 2, 0:K.b, r % 2, :],
                        chunks[rows, :, 0:K.b, :], ACT.Copy)
                last.then_inc(C.pj_free[bank], 1)

            def exponentials(u, q):
                wait(e, C.s_sub, total(u, 4, q + 1))
                nc.scalar.activation(c_p[:], c_s[:], ACT.Exp, scale=SCORE_SCALE) \
                    .then_inc(C.p_ready, 1)

            def probs_t_out(u, q):
                wait(e, C.pt_full, total(u, 4, q + 1))
                wait(e, C.pv_done, total(u, 4, q))
                nc.scalar.activation(c_pt[:], PT[:], ACT.Copy).then_inc(C.pt_ready, 1)

            def split_ctx(v):
                wait(e, ctx_in[parity(v)], total_of_parity(v, 64, 64))
                nc.scalar.activation(ctx_hi[:, parity(v)].rearrange("p j c k -> p (j c k)"),
                                     ctx_raw[:, parity(v)].rearrange("p j c k -> p (j c k)"),
                                     ACT.Copy).then_inc(ctx_hi_ready, 1)

            def step(u, kind):
                more, ahead = kind != "last", kind == "full"
                v = later(u, 1)
                if more:
                    keys_out(u, v, 0)
                exponentials(u, 0)
                probs_t_out(u, 0)
                if more:
                    keys_out(u, v, 1)
                else:
                    self_w_hi(e, 0)
                exponentials(u, 1)
                if more:
                    keys_out(u, v, 2)
                probs_t_out(u, 1)
                if more:
                    keys_out(u, v, 3)
                else:
                    self_w_hi(e, 1)
                exponentials(u, 2)
                if more:
                    for t in range(K.nt):
                        x_hi(u, v, t)
                probs_t_out(u, 2)
                exponentials(u, 3)
                if ahead:
                    split_ctx(later(u, 2))
                if K.nt == 2:
                    a_hi(u, 0, kind)
                if not more:
                    self_w_hi(e, 2)
                probs_t_out(u, 3)
                if more:
                    queries_out(u, 0)
                    queries_out(u, 1)
                a_hi(u, K.nt - 1, kind)

            first = Unit(0, 0)
            split_ctx(first)
            cross_w_hi(e, 1)
            keys_out(None, first, 0)
            keys_out(None, first, 1)
            cross_w_hi(e, 2)
            keys_out(None, first, 2)
            keys_out(None, first, 3)
            for t in range(K.nt):
                x_hi(None, first, t)
            e.wait_ge(pads_ready, 1)
            queries_out(None, 0)
            cross_w_hi(e, 3)
            queries_out(None, 1)
            split_ctx(later(first, 1))
            run_steps(e, K.units, step)

        def cross_dve(e, K):
            def full(u, name, kind="full"):
                bank, before = K.banks.at(u, name, kind)
                wait(e, C.pj_full[bank], before + 1)
                return bank

            def ln_statistics(v):
                wait(e, C.x_in[parity(v)], total_of_parity(v, 16 * K.nt, 16 * K.nt))
                for t in range(K.nt):
                    nc.vector.bn_stats(stats[0:K.tp, t, :], cx[0:K.tp, parity(v), t, :]) \
                        .then_inc(C.stats, 1)

            def ln_normalise(v):
                for t in range(K.nt):
                    nc.vector.bn_aggr(mean_var[0:K.tp, t, :], stats[0:K.tp, t, :]) \
                        .then_inc(C.agg, 1)
                for t in range(K.nt):
                    wait(e, C.rstd, total(v, K.nt, t + 1))
                    nc.vector.tensor_scalar(cxn[0:K.tp, t, :], cx[0:K.tp, parity(v), t, :],
                                            mean_var[0:K.tp, t, 0:1], rstd[0:K.tp, t, :],
                                            ALU.subtract, ALU.mult).then_inc(C.xn, 1)

            def x_lo(u, v, t):
                bank = full(u, f"X{t}")
                wait(e, C.xt_hi, total(v, K.nt, t + 1))
                nc.vector.tensor_tensor(
                    cxt_lo[:, :, t * P:t * P + K.tp],
                    PJ[bank][:].rearrange("p (c s) -> p c s", c=DC)[:, :, 0:K.tp],
                    cxt_hi[:, :, t * P:t * P + K.tp].bitcast(F32),
                    ALU.subtract).then_inc(C.pj_free[bank], 1)

            def a_lo(u, t, kind):
                bank = full(u, f"A{t}", kind)
                wait(e, C.at_hi, total(u, K.nt, t + 1))
                nc.vector.tensor_tensor(
                    cat_lo[:, :, 0:K.tp],
                    PJ[bank][:].rearrange("p (c s) -> p c s", c=DC)[:, :, 0:K.tp],
                    cat_hi[:, :, 0:K.tp].bitcast(F32), ALU.subtract).then_inc(C.pj_free[bank], 1)

            def values_out(u, v, j):
                bank = full(u, f"V{j}")
                nc.vector.tensor_copy(cv[:, parity(v), j, :, 0:DK],
                                      PJ[bank][:].rearrange("p (h d) -> p h d", d=DK)) \
                    .then_inc(C.pj_free[bank], 1)

            def softmax(u, q):
                groups = PAIRS // K.kt
                rows = lambda a: a[:].rearrange("p (g k) -> p g k", g=groups)
                n = K.kt * P
                wait(e, C.s_full, total(u, 4, q + 1))
                wait(e, C.p_ready, total(u, 4, q))
                nc.vector.tensor_tensor(
                    rows(c_s), rows(S),
                    mask_bias[:, KEYS - n:KEYS].unsqueeze(1).to_broadcast([P, groups, n]),
                    ALU.add).then_inc(C.s_free, 1)
                wait(e, C.s_free, total(u, 4, q + 1))
                nc.vector.reduce_max(row_max[:, 0:groups], rows(c_s), AXIS.X).then_inc(C.s_max, 1)
                wait(e, C.s_max, total(u, 4, q + 1))
                nc.vector.tensor_tensor(rows(c_s), rows(c_s),
                                        row_max[:, 0:groups].unsqueeze(2).to_broadcast([P, groups, n]),
                                        ALU.subtract).then_inc(C.s_sub, 1)

            def normalise(u, t):
                wait(e, C.pv_done, total(u, 4, 4 // K.nt * (t + 1)))
                nc.vector.reciprocal(sums[0:K.tp, :, :, :], PV_HEADS[0:K.tp, :, :, DK:VW]) \
                    .then_inc(C.rcp, 1)
                wait(e, C.rcp, total(u, K.nt, t + 1))
                nc.vector.tensor_tensor(
                    c_a[0:K.tp].rearrange("p (a h) d -> p a h d", a=2),
                    PV_HEADS[0:K.tp, :, :, 0:DK],
                    sums[0:K.tp].to_broadcast([K.tp, 2, HEADS // 2, DK]),
                    ALU.mult).then_inc(C.a_ready, 1)

            def residual(u, t, kind):
                bank = full(u, f"O{t}", kind)
                nc.vector.tensor_tensor(cx[0:K.tp, parity(u), t, :], PJ[bank][0:K.tp, :],
                                        cx[0:K.tp, parity(u), t, :], ALU.add) \
                    .then_inc(C.pj_free[bank], 1)

            def split_ctx(v):
                wait(e, ctx_hi_ready, total(v, 1, 1))
                flat = lambda a: a[:, parity(v)].rearrange("p j c k -> p (j c k)")
                nc.vector.tensor_tensor(flat(ctx_lo), flat(ctx_raw), flat(ctx_hi).bitcast(F32),
                                        ALU.subtract).then_inc(ctx_lo_ready, 1)

            def step(u, kind):
                more, ahead = kind != "last", kind == "full"
                v = later(u, 1)
                softmax(u, 0)
                if not is_unit(u, 0):
                    residual(later(u, -1), K.nt - 1, "last_but_one" if kind == "last" else "full")
                if more:
                    ln_statistics(v)
                    wait(e, C.stats, total(v, K.nt, K.nt))
                softmax(u, 1)
                if more:
                    ln_normalise(v)
                else:
                    self_w_lo(e, 0)
                softmax(u, 2)
                if K.nt == 2:
                    normalise(u, 0)
                if more:
                    for t in range(K.nt):
                        x_lo(u, v, t)
                softmax(u, 3)
                if more:
                    values_out(u, v, 0)
                    values_out(u, v, 1)
                if K.nt == 2:
                    a_lo(u, 0, kind)
                if ahead:
                    split_ctx(later(u, 2))
                if more:
                    values_out(u, v, 2)
                else:
                    self_w_lo(e, 1)
                if K.nt == 2:
                    residual(u, 0, kind)
                if not more:
                    self_ln_statistics(e, Unit(0, 0))
                    e.wait_ge(G.stats, NT)
                    self_ln_normalise(e, Unit(0, 0))
                normalise(u, K.nt - 1)
                if more:
                    values_out(u, v, 3)
                a_lo(u, K.nt - 1, kind)
                if not more:
                    self_w_lo(e, 2)
                    residual(u, K.nt - 1, kind)

            first = Unit(0, 0)
            split_ctx(first)
            ln_statistics(first)
            e.wait_ge(C.stats, K.nt)
            cross_w_lo(e, 1)
            e.wait_ge(pads_ready, 3)
            ln_normalise(first)
            cross_w_lo(e, 2)
            for t in range(K.nt):
                x_lo(None, first, t)
            e.wait_ge(pads_ready, 4)
            values_out(None, first, 0)
            values_out(None, first, 1)
            cross_w_lo(e, 3)
            values_out(None, first, 2)
            values_out(None, first, 3)
            split_ctx(later(first, 1))
            e.wait_ge(w_lo_ready, 4)
            run_steps(e, K.units, step)

        def rstd_of(e, agg, eps, done, v, per, rows):
            for t in range(per):
                wait(e, agg, total(v, per, t + 1))
                e.tensor_tensor(var_eps[0:rows, t, :], mean_var[0:rows, t, 1:2], ln_eps[0:rows, :],
                                ALU.add).then_inc(eps, 1)
                wait(e, eps, total(v, per, t + 1))
                e.tensor_tensor(rstd[0:rows, t, :], var_eps[0:rows, t, :], minus_half[0:rows, :],
                                ALU.pow).then_inc(done, 1)

        def cross_pool(e, K):
            def step(u, kind):
                more, ahead = kind != "last", kind == "full"
                if more:
                    rstd_of(e, C.agg, C.eps, C.rstd, later(u, 1), K.nt, K.tp)

            rstd_of(e, C.agg, C.eps, C.rstd, Unit(0, 0), K.nt, K.tp)
            run_steps(e, K.units, step)

        F_UNITS, FT, LEAD = TOKENS // (4 * P), 4, 2
        f_x2 = x2.rearrange("(u t p) d -> u t p d", t=FT, p=P)
        f_out = out.rearrange("(u t p) d -> u t p d", t=FT, p=P)
        W_SUMS = PV[:, 0, 384:386]
        flat_q = [t[:].rearrange("p a b -> p (a b)").rearrange("p (k n) -> p k n", n=512)
                  for t in (w1_q, w2_q)]

        def ff_ln_statistics(e, v):
            wait(e, fx_in[parity(v)], total_of_parity(v, 16 * FT, 16 * FT))
            for t in range(FT):
                nc.vector.bn_stats(stats[:, t, :], fx[:, parity(v), t, :]).then_inc(f_stats, 1)

        def ff_ln_aggregate(e):
            for t in range(FT):
                nc.vector.bn_aggr(mean_var[:, t, :], stats[:, t, :]).then_inc(f_agg, 1)

        def ff_ln_normalise(e, v, t):
            wait(e, f_rstd, total(v, FT, t + 1))
            wait(e, xb_full, total(v, FT, t - 1))
            nc.vector.tensor_scalar(fxn[:, t % 2, :], fx[:, parity(v), t, :],
                                    mean_var[:, t, 0:1], rstd[:, t, :],
                                    ALU.subtract, ALU.mult).then_inc(f_xn, 1)

        def ff_x_transpose(e, v, t):
            wait(e, xb_free, total(v, FT, t - 1))
            wait(e, f_xn, total(v, FT, t + 1))
            for c in range(DC):
                last = nc.tensor.transpose(XB[t % 2][:, c * P:c * P + P],
                                           fxn[:, t % 2, c * P:c * P + P], ident[:])
            last.then_inc(xb_full, 1)

        def ff_x_hi(e, v, t):
            wait(e, xb_full, total(v, FT, t + 1))
            nc.scalar.activation(fxt_hi[parity(v)][:, :, t * P:t * P + P],
                                 XB[t % 2].rearrange("p (c s) -> p c s", c=DC),
                                 ACT.Copy).then_inc(fxt_hi_ready, 1)

        def ff_x_lo(e, v, t):
            wait(e, fxt_hi_ready, total(v, FT, t + 1))
            nc.vector.tensor_tensor(fxt_lo[parity(v)][:, :, t * P:t * P + P],
                                    XB[t % 2].rearrange("p (c s) -> p c s", c=DC),
                                    fxt_hi[parity(v)][:, :, t * P:t * P + P].bitcast(F32),
                                    ALU.subtract).then_inc(xb_free, 1)

        LAST_TILE, ALL_TILES = Cross(1), Cross(KEY_TILES)

        block = outer.enter_context(nc.Block())

        s_full_uses = ["Q0", "Q1", "K0", "A0", "K1", "V0", "V1", "X0", "O0", "X1", "A1", "O1"]
        SB = Banks(["X0", "X1", "Q0", "Q1", "K0", "K1", "V0", "V1", "Y0", "Y1"], s_full_uses,
                   [n for n in s_full_uses if n[0] != "X"], [n for n in s_full_uses if n[0] in "AO"])
        SLOT = [(pair % 2) * 4 + pair // 2 for pair in range(PAIRS)]

        def self_sync(e):
            def step(u, kind):
                if kind == "full":
                    load_self_x(e, later(u, 2))
                elif kind == "last":
                    bank, before = SB.at(later(u, -1), "V1", "last_but_one")
                    wait(e, G.pj_free[bank], before + 1)
                    for i in range(2):
                        e.wait_ge(G.stored[i], 16 * NT * (S_UNITS // 2 - 1))
                    e.dma_start(b2_sb[:], b2.unsqueeze(0).to_broadcast([P, D])) \
                        .then_inc(ff_bias_in, 16)
                    for n in range(2):
                        for t in range(FT):
                            e.dma_start(fx[:, n, t, :], f_x2[n, t]).then_inc(fx_in[n], 16)
                for t in range(NT):
                    bank, before = SB.at(u, f"O{t}", kind)
                    wait(e, G.pj_free[bank], before + 1)
                    e.dma_start(s_x2[number(u), t], sres[:, parity(u), t, :]) \
                        .then_inc(G.stored[parity(u)], 16)

            for n, src in enumerate((w1, w2)):
                e.dma_start(w_raw[:, n].rearrange("p k n -> p (k n)"), src).then_inc(fw_in[n], 16)
            run_steps(e, S_UNITS, step)
            for i in range(2):
                e.wait_ge(G.stored[i], 16 * NT * S_UNITS // 2)

        def self_pe(e):
            def begin(u, name, kind="full"):
                bank, before = SB.at(u, name, kind)
                wait(e, G.pj_free[bank], before)
                return bank

            def x_transpose(u, v, t, name=None):
                bank = begin(u, name or f"X{t}")
                wait(e, G.xn, total(v, NT, t + 1))
                for c in range(DC):
                    last = nc.tensor.transpose(PJ[bank][:, c * P:c * P + P],
                                               sxn[:, t, c * P:c * P + P], ident[:])
                last.then_inc(G.pj_full[bank], 1)

            def qk_proj(u, name, w, kind="full", before_last=None):
                bank = begin(u, name, kind)
                n = int(name[1])
                for i in range(2):
                    cols = slice((2 * n + i) * P, (2 * n + i + 1) * P)
                    last = split_products(e, PJ[bank][:, 256 * i:256 * i + 256], [
                        (sw_hi[:, w, c, cols], sw_lo[:, w, c, cols], sxt_hi[:, c, :], sxt_lo[:, c, :])
                        for c in range(DC)], before_last if i else None)
                last.then_inc(G.pj_full[bank], 1)

            def v_proj(u, t, kind="full", before_last=None):
                bank = begin(u, f"V{t}", kind)
                rows = slice(t * P, t * P + P)
                split_products(e, PJ[bank][:], [
                    (sxt_hi[:, c, rows], sxt_lo[:, c, rows], sw_hi[:, 2, c, :], sw_lo[:, 2, c, :])
                    for c in range(DC)], before_last).then_inc(G.pj_full[bank], 1)

            def scores(u, t):
                wait(e, G.s_free, total(u, NT, t))
                for r in (0, 2, 1, 3):
                    rows, half = slice(DK * r, DK * r + DK), SEQ * (r % 2)
                    for c in range(DC):
                        slot = SLOT[2 * c + r // 2]
                        for b in range(2):
                            col = slot * P + b * SEQ
                            last = nc.tensor.matmul(S[half:half + SEQ, col:col + SEQ],
                                                    sq_t[rows, parity(u), c, 2 * t + b, :],
                                                    sk_t[rows, parity(u), c, 2 * t + b, :],
                                                    start=True, stop=True)
                last.then_inc(G.s_full, 1)

            def transposes(u, t):
                wait(e, G.pt_ready, total(u, NT, t))
                wait(e, G.p_ready, total(u, NT, t + 1))
                for i in range(8):
                    last = nc.tensor.transpose(PT[:, i * P:i * P + P], s_p[:, i * P:i * P + P],
                                               ident[:])
                last.then_inc(G.pt_full, 1)

            def attend_waits(u, t):
                wait(e, G.a_ready, total(u, NT, t))
                wait(e, G.pt_ready, total(u, NT, t + 1))

            def attend(u, t):
                for b in range(2):
                    rows = slice(SEQ * b, SEQ * b + SEQ)
                    for head in range(HEADS):
                        at = SLOT[head // 2] * P + SEQ * (head % 2)
                        last = nc.tensor.matmul(PV_HEADS[rows, head // 8, head % 8, :],
                                                s_pt[rows, at:at + SEQ], sv[rows, parity(u), t, head, :],
                                                start=True, stop=True)
                last.then_inc(G.pv_done, 1)

            def a_transpose(u, t, kind):
                bank = begin(u, f"A{t}", kind)
                wait(e, G.a_ready, total(u, NT, t + 1))
                a = s_a[:].rearrange("p h d -> p (h d)")
                for c in range(DC):
                    last = nc.tensor.transpose(PJ[bank][:, c * P:c * P + P], a[:, c * P:c * P + P],
                                               ident[:])
                last.then_inc(G.pj_full[bank], 1)

            def o_proj(u, t, kind):
                bank = begin(u, f"O{t}", kind)
                b, before = SB.at(u, f"A{t}", kind)
                wait(e, G.pj_free[b], before + 1)
                split_products(e, PJ[bank][:], [
                    (sat_hi[:, c, :], sat_lo[:, c, :], sw_hi[:, 3, c, :], sw_lo[:, 3, c, :])
                    for c in range(DC)]).then_inc(G.pj_full[bank], 1)

            def step(u, kind):
                more = kind != "last"
                scores(u, 0)
                if is_unit(u, 0):
                    e.wait_ge(sw_lo_ready, 4)
                    e.wait_ge(self_ones, 1)
                    for bank in range(2):
                        e.wait_ge(G.pj_free[bank], SB.drained(bank))
                else:
                    o_proj(later(u, -1), 1, "last_but_one" if kind == "last" else "full")
                if more:
                    qk_proj(u, "Q0", 0, kind)
                scores(u, 1)
                transposes(u, 0)
                if more:
                    qk_proj(u, "Q1", 0, kind, lambda: attend_waits(u, 0))
                else:
                    attend_waits(u, 0)
                attend(u, 0)
                if more:
                    qk_proj(u, "K0", 1, kind)
                transposes(u, 1)
                a_transpose(u, 0, kind)
                if more:
                    qk_proj(u, "K1", 1, kind)
                    v_proj(u, 0, kind)
                    v_proj(u, 1, kind, lambda: attend_waits(u, 1))
                else:
                    attend_waits(u, 1)
                if kind == "full":
                    x_transpose(u, later(u, 2), 0)
                attend(u, 1)
                o_proj(u, 0, kind)
                if kind == "full":
                    x_transpose(u, later(u, 2), 1)
                a_transpose(u, 1, kind)
                if is_unit(u, 1):
                    e.wait_ge(fw_abs, 1)
                    nc.tensor.matmul(W_SUMS, ones[:], abs_total[:], start=True, stop=True) \
                        .then_inc(fw_total, 1)
                if kind == "last":
                    for t in range(2):
                        ff_x_transpose(e, Unit(0, 0), t)
                    o_proj(u, 1, kind)

            for t in range(NT):
                x_transpose(None, Unit(0, 0), t)
            e.wait_ge(sw_lo_ready, 3)
            for bank in range(2):
                e.wait_ge(G.pj_free[bank], 1)
            for n in range(2):
                qk_proj(None, f"Q{n}", 0)
            for n in range(2):
                qk_proj(None, f"K{n}", 1)
            for t in range(NT):
                v_proj(None, t)
            for t in range(NT):
                x_transpose(None, Unit(0, 1), t, f"Y{t}")
            run_steps(e, S_UNITS, step)

        def self_act(e):
            def full(u, name, kind="full"):
                bank, before = SB.at(u, name, kind)
                wait(e, G.pj_full[bank], before + 1)
                return bank

            def x_hi(u, v, t, name=None):
                bank = full(u, name or f"X{t}")
                nc.scalar.activation(sxt_hi[:, :, t * P:t * P + P],
                                     PJ[bank][:].rearrange("p (c s) -> p c s", c=DC),
                                     ACT.Copy).then_inc(G.xt_hi, 1)

            def a_hi(u, t, kind):
                bank = full(u, f"A{t}", kind)
                nc.scalar.activation(sat_hi[:].rearrange("p c s -> p (c s)"), PJ[bank][:],
                                     ACT.Copy).then_inc(G.at_hi, 1)

            def qk_out(u, v, name, kind="full"):
                bank = full(u, name, kind)
                n = int(name[1])
                dst, bias = (sq_t, bq_sb) if name[0] == "Q" else (sk_t, bk_sb)
                for i in range(2):
                    last = nc.scalar.activation(
                        dst[:, parity(v), 2 * n + i, :, :].rearrange("p b s -> p (b s)"),
                        PJ[bank][:, 256 * i:256 * i + 256], ACT.Identity,
                        bias=bias[:, 2 * n + i:2 * n + i + 1])
                last.then_inc(G.pj_free[bank], 1)

            def exponentials(u, t):
                wait(e, G.s_free, total(u, NT, t + 1))
                nc.scalar.activation(s_p[:], s_s[:], ACT.Exp, scale=SCORE_SCALE) \
                    .then_inc(G.p_ready, 1)

            def probs_t_out(u, t):
                wait(e, G.pt_full, total(u, NT, t + 1))
                wait(e, G.pv_done, total(u, NT, t))
                nc.scalar.activation(s_pt[:], PT[:], ACT.Copy).then_inc(G.pt_ready, 1)

            def magnitudes(u, first, last):
                if not (is_unit(u, 0) or is_unit(u, 1)):
                    return
                w = u.off
                if first == 0:
                    e.wait_ge(fw_in[w], 16)
                for n in range(first, last):
                    wait(e, fw_summed, w * FC + n)
                    nc.scalar.activation(f_scratch[:], w_raw[:, w, n, :], ACT.Abs,
                                         accum_out=abs_sum[:, w, n:n + 1]).then_inc(fw_summed, 1)

            def step(u, kind):
                v, more = later(u, 1), kind != "last"
                exponentials(u, 0)
                magnitudes(u, 0, 3)
                if more:
                    qk_out(u, v, "Q0", kind)
                magnitudes(u, 3, 6)
                probs_t_out(u, 0)
                exponentials(u, 1)
                if more:
                    qk_out(u, v, "Q1", kind)
                magnitudes(u, 6, 9)
                if more:
                    qk_out(u, v, "K0", kind)
                probs_t_out(u, 1)
                a_hi(u, 0, kind)
                magnitudes(u, 9, 12)
                if more:
                    qk_out(u, v, "K1", kind)
                magnitudes(u, 12, 16)
                if kind == "full":
                    x_hi(u, later(u, 2), 0)
                    x_hi(u, later(u, 2), 1)
                a_hi(u, 1, kind)
                if kind == "last":
                    for t in range(2):
                        ff_x_hi(e, Unit(0, 0), t)

            e.wait_ge(self_bias_in, 80)
            e.wait_ge(sw_lo_ready, 3)
            for t in range(NT):
                x_hi(None, Unit(0, 0), t)
            qk_out(None, Unit(0, 0), "Q0")
            e.wait_ge(cross_w_used, 1)
            self_w_hi(e, 3)
            for name in ("Q1", "K0", "K1"):
                qk_out(None, Unit(0, 0), name)
            for t in range(NT):
                x_hi(None, Unit(0, 1), t, f"Y{t}")
            run_steps(e, S_UNITS, step)

        def self_dve(e):
            def full(u, name, kind="full"):
                bank, before = SB.at(u, name, kind)
                wait(e, G.pj_full[bank], before + 1)
                return bank

            def x_lo(u, v, t, name=None):
                bank = full(u, name or f"X{t}")
                wait(e, G.xt_hi, total(v, NT, t + 1))
                nc.vector.tensor_tensor(sxt_lo[:, :, t * P:t * P + P],
                                        PJ[bank][:].rearrange("p (c s) -> p c s", c=DC),
                                        sxt_hi[:, :, t * P:t * P + P].bitcast(F32),
                                        ALU.subtract).then_inc(G.pj_free[bank], 1)

            def a_lo(u, t, kind):
                bank = full(u, f"A{t}", kind)
                wait(e, G.at_hi, total(u, NT, t + 1))
                nc.vector.tensor_tensor(sat_lo[:].rearrange("p c s -> p (c s)"), PJ[bank][:],
                                        sat_hi[:].rearrange("p c s -> p (c s)").bitcast(F32),
                                        ALU.subtract).then_inc(G.pj_free[bank], 1)

            def values_out(u, v, t, kind="full"):
                bank = full(u, f"V{t}", kind)
                nc.vector.tensor_tensor(sv[:, parity(v), t, :, 0:DK],
                                        PJ[bank][:].rearrange("p (h d) -> p h d", d=DK),
                                        bv_sb[:].rearrange("p (h d) -> p h d", d=DK),
                                        ALU.add).then_inc(G.pj_free[bank], 1)

            def softmax(u, t):
                rows = lambda a: a[:].rearrange("p (g k) -> p g k", g=HEADS)
                wait(e, G.s_full, total(u, NT, t + 1))
                nc.vector.reduce_max(row_max[:], rows(S), AXIS.X).then_inc(G.s_max, 1)
                wait(e, G.s_max, total(u, NT, t + 1))
                wait(e, G.p_ready, total(u, NT, t))
                nc.vector.tensor_tensor(rows(s_s), rows(S),
                                        row_max[:].unsqueeze(2).to_broadcast([P, HEADS, SEQ]),
                                        ALU.subtract).then_inc(G.s_free, 1)

            def normalise(u, t):
                wait(e, G.pv_done, total(u, NT, t + 1))
                nc.vector.reciprocal(sums[:], PV_HEADS[:, :, :, DK:VW]).then_inc(G.rcp, 1)
                wait(e, G.rcp, total(u, NT, t + 1))
                nc.vector.tensor_tensor(s_a[:].rearrange("p (a h) d -> p a h d", a=2),
                                        PV_HEADS[:, :, :, 0:DK],
                                        sums[:].to_broadcast([P, 2, HEADS // 2, DK]),
                                        ALU.mult).then_inc(G.a_ready, 1)

            def residual(u, t, kind):
                bank = full(u, f"O{t}", kind)
                if t == 0:
                    wait(e, G.res, total(u, NT, NT))
                nc.vector.tensor_tensor(sres[:, parity(u), t, :], PJ[bank][:],
                                        sres[:, parity(u), t, :], ALU.add) \
                    .then_inc(G.pj_free[bank], 1)

            def ternary(k, waits):
                for w in range(2):
                    wait(e, fw_ready, waits(w))
                    nc.vector.tensor_scalar(f_scratch[:], w_raw[:, w, k, :], thresh[:, 1, w:w + 1],
                                            None, ALU.is_lt).then_inc(fw_neg, 1)
                    wait(e, fw_neg, waits(w + 1))
                    nc.vector.scalar_tensor_tensor(flat_q[w][:, k, :], w_raw[:, w, k, :],
                                                   thresh[:, 0, w:w + 1],
                                                   f_scratch[:], ALU.is_gt, ALU.subtract) \
                        .then_inc(fw_ready, 1)

            def make_ternary(k):
                ternary(k, lambda n: 2 * k + n)

            def step(u, kind):
                v, more, w = later(u, 1), kind != "last", later(u, 2)
                softmax(u, 0)
                if not is_unit(u, 0):
                    residual(later(u, -1), 1, "last_but_one" if kind == "last" else "full")
                if kind == "full":
                    self_ln_statistics(e, w)
                    wait(e, G.stats, total(w, NT, NT))
                elif kind == "last_but_one":
                    make_ternary(S_UNITS - 4)
                    make_ternary(S_UNITS - 3)
                softmax(u, 1)
                if kind == "full":
                    self_ln_normalise(e, w)
                elif kind == "last_but_one":
                    make_ternary(S_UNITS - 2)
                elif kind == "last":
                    ff_ln_statistics(e, Unit(0, 0))
                    e.wait_ge(f_stats, FT)
                    ff_ln_aggregate(e)
                normalise(u, 0)
                if kind == "full" and not (isinstance(u.half, int)):
                    ternary(number(u) - 2, lambda n: total(u, 2, n - 4))
                if kind == "last":
                    for t in range(2):
                        ff_ln_normalise(e, Unit(0, 0), t)
                a_lo(u, 0, kind)
                if kind == "last_but_one":
                    make_ternary(S_UNITS - 1)
                if more:
                    values_out(u, v, 0, kind)
                    values_out(u, v, 1, kind)
                if kind == "full":
                    x_lo(u, w, 0)
                normalise(u, 1)
                residual(u, 0, kind)
                if kind == "full":
                    x_lo(u, w, 1)
                a_lo(u, 1, kind)
                if is_unit(u, 1):
                    e.wait_ge(fw_summed, 2 * FC)
                    nc.vector.reduce_sum(abs_total[:], abs_sum[:], AXIS.X).then_inc(fw_abs, 1)
                    e.wait_ge(fw_total, 1)
                    nc.vector.tensor_scalar(thresh[:, 0, :], W_SUMS, 0.5 / (D * FF),
                                            0.5 * QUANT_EPS, ALU.mult, ALU.add) \
                        .then_inc(fw_thresh, 1)
                    e.wait_ge(fw_thresh, 1)
                    nc.vector.tensor_scalar(thresh[:, 1, :], thresh[:, 0, :], -1.0, None, ALU.mult) \
                        .then_inc(fw_thresh, 1)
                    e.wait_ge(fw_thresh, 2)
                if kind == "last":
                    for t in range(2):
                        ff_x_lo(e, Unit(0, 0), t)
                    residual(u, 1, kind)

            for t in range(NT):
                x_lo(None, Unit(0, 0), t)
            self_ln_statistics(e, Unit(0, 1))
            e.wait_ge(G.stats, 2 * NT)
            self_ln_normalise(e, Unit(0, 1))
            self_w_lo(e, 3)
            e.wait_ge(self_bias_in, 80)
            e.wait_ge(self_ones, 1)
            for t in range(NT):
                values_out(None, Unit(0, 0), t)
            for t in range(NT):
                x_lo(None, Unit(0, 1), t, f"Y{t}")
            run_steps(e, S_UNITS, step)

        def self_pool(e):
            def residuals(v):
                wait(e, G.x_in[parity(v)], total_of_parity(v, 16 * NT, 16 * NT))
                wait(e, G.stored[parity(v)], total_of_parity(v, 16 * NT))
                for t in range(NT):
                    e.tensor_tensor(sres[:, parity(v), t, :], sx[:, parity(v), t, :], bo_sb[:],
                                    ALU.add).then_inc(G.res, 1)

            def step(u, kind):
                if kind != "last":
                    residuals(later(u, 1))
                if kind == "full":
                    rstd_of(e, G.agg, G.eps, G.rstd, later(u, 2), NT, P)

            rstd_of(e, G.agg, G.eps, G.rstd, Unit(0, 0), NT, P)
            e.wait_ge(sw_lo_ready, 3)
            e.memset(sv[:, :, :, :, DK:VW].rearrange("p a t h o -> p (a t) (h o)"), 1.0) \
                .then_inc(self_ones, 1)
            rstd_of(e, G.agg, G.eps, G.rstd, Unit(0, 1), NT, P)
            e.wait_ge(self_bias_in, 80)
            e.wait_ge(sw_lo_ready, 4)
            residuals(Unit(0, 0))
            run_steps(e, S_UNITS, step)


        def ff_sync(e):
            def step(u, kind):
                if kind == "full":
                    w = later(u, 2)
                    wait(e, f_xn, total(u, FT, FT))
                    wait(e, f_res, total(u, FT, FT))
                    for t in range(FT):
                        e.dma_start(fx[:, parity(w), t, :], f_x2[number(w), t]) \
                            .then_inc(fx_in[parity(w)], 16)
                for t in range(FT):
                    wait(e, y_new[t], total(u, 1, 1))
                    e.dma_start(f_out[number(u), t], fres[:, parity(u), t, :]) \
                        .then_inc(f_stored[parity(u)], 16)

            run_steps(e, F_UNITS, step)
            for i in range(2):
                e.wait_ge(f_stored[i], 16 * FT * F_UNITS // 2)

        def ff_pe(e):
            def hidden(v, m):
                wait(e, h_relu, total(v, FC, m - 1))
                if m == 0:
                    wait(e, xb_free, total(v, FT, FT))
                cols = slice(m * P, m * P + P)
                for c in range(DC):
                    for x_t in (fxt_hi, fxt_lo):
                        last = nc.tensor.matmul(PJ[m % 2][:], w1_q[:, c, cols],
                                                x_t[parity(v)][:, c, :],
                                                start=(c == 0 and x_t is fxt_hi),
                                                stop=(c == DC - 1 and x_t is fxt_lo))
                last.then_inc(h_full, 1)

            def contract(u, m):
                wait(e, h_lo_ready, total(u, FC, m + 1))
                for t in range(FT):
                    if m == 0:
                        wait(e, y_new[t], total(u, 1))
                    rows = slice(t * P, t * P + P)
                    nc.tensor.matmul(YB[t], h_hi[:, m % 4, rows], w2_q[:, m, :],
                                     start=(m == 0), stop=False)
                    last = nc.tensor.matmul(YB[t], h_lo[:, m % 4, rows], w2_q[:, m, :],
                                            start=False, stop=(m == FC - 1))
                    if m == FC - 1:
                        last.then_inc(y_full[t], 1)
                    elif t == FT - 1:
                        last.then_inc(y_m, 1)

            def step(u, kind):
                v, more = later(u, 1), kind != "last"
                for m in range(FC):
                    if m + LEAD < FC:
                        hidden(u, m + LEAD)
                    elif more:
                        hidden(v, m + LEAD - FC)
                    contract(u, m)
                    if more and m in (3, 5, 7, 9):
                        ff_x_transpose(e, v, (m - 3) // 2)

            for t in range(2, FT):
                ff_x_transpose(e, Unit(0, 0), t)
            e.wait_ge(fw_ready, 2 * FC)
            bank, before = SB.at(Unit(S_UNITS // 2 - 1, 1), "O1", "last")
            e.wait_ge(G.pj_free[bank], before + 1)
            for m in range(LEAD):
                hidden(Unit(0, 0), m)
            run_steps(e, F_UNITS, step)

        def ff_act(e):
            def relu(v, m):
                wait(e, h_full, total(v, FC, m + 1))
                wait(e, h_lo_ready, total(v, FC, m - 1))
                nc.scalar.activation(h_raw[:, m % 2, :], PJ[m % 2][:], ACT.Relu,
                                     bias=b1_sb[:, m:m + 1]).then_inc(h_relu, 1)

            def step(u, kind):
                v, more = later(u, 1), kind != "last"
                for m in range(FC):
                    if m + LEAD < FC:
                        relu(u, m + LEAD)
                    elif more:
                        relu(v, m + LEAD - FC)
                    if more and m in (3, 5, 7, 9):
                        ff_x_hi(e, v, (m - 3) // 2)

            for t in range(2, FT):
                ff_x_hi(e, Unit(0, 0), t)
            for m in range(LEAD):
                relu(Unit(0, 0), m)
            for i in range(2):
                e.wait_ge(G.stored[i], 16 * NT * S_UNITS // 2)
            run_steps(e, F_UNITS, step)

        def ff_dve(e):
            def split_hidden(v, m):
                wait(e, h_relu, total(v, FC, m + 1))
                nc.vector.tensor_copy(h_hi[:, m % 4, :], h_raw[:, m % 2, :]).then_inc(h_hi_ready, 1)
                wait(e, h_hi_ready, total(v, FC, m + 1))
                nc.vector.tensor_tensor(h_lo[:, m % 4, :], h_raw[:, m % 2, :],
                                        h_hi[:, m % 4, :].bitcast(F32),
                                        ALU.subtract).then_inc(h_lo_ready, 1)

            def step(u, kind):
                v, more = later(u, 1), kind != "last"
                for m in range(FC):
                    if more and m == 1:
                        wait(e, f_stats, total(v, FT, FT))
                    if m + LEAD < FC:
                        split_hidden(u, m + LEAD)
                    elif more:
                        split_hidden(v, m + LEAD - FC)
                    if more:
                        if m == 0:
                            ff_ln_statistics(e, v)
                        if m == 1:
                            ff_ln_aggregate(e)
                        if m in (2, 4, 6, 8):
                            ff_ln_normalise(e, v, (m - 2) // 2)
                        if m in (3, 5, 7, 9):
                            ff_x_lo(e, v, (m - 3) // 2)
                for t in range(FT):
                    wait(e, y_full[t], total(u, 1, 1))
                    if t == 0:
                        wait(e, f_res, total(u, FT, FT))
                    nc.vector.tensor_tensor(fres[:, parity(u), t, :], YB[t],
                                            fres[:, parity(u), t, :], ALU.add) \
                        .then_inc(y_new[t], 1)

            first = Unit(0, 0)
            for t in range(2, FT):
                ff_ln_normalise(e, first, t)
                ff_x_lo(e, first, t)
            for m in range(LEAD):
                split_hidden(first, m)
            run_steps(e, F_UNITS, step)

        def ff_pool(e):
            def residuals(v):
                wait(e, fx_in[parity(v)], total_of_parity(v, 16 * FT, 16 * FT))
                wait(e, f_stored[parity(v)], total_of_parity(v, 16 * FT))
                for t in range(FT):
                    e.tensor_tensor(fres[:, parity(v), t, :], fx[:, parity(v), t, :], b2_sb[:],
                                    ALU.add).then_inc(f_res, 1)

            def step(u, kind):
                if kind != "last":
                    rstd_of(e, f_agg, f_eps, f_rstd, later(u, 1), FT, P)
                    residuals(later(u, 1))

            rstd_of(e, f_agg, f_eps, f_rstd, Unit(0, 0), FT, P)
            e.wait_ge(ff_bias_in, 16)
            residuals(Unit(0, 0))
            run_steps(e, F_UNITS, step)

        def choose(e, program):
            e.wait_ge(flag_ready, 1)
            only_last = e.value_load(flag_i[0:1, 0:1], min_val=0, max_val=1)
            with e.If(only_last):
                program(e, LAST_TILE)
                e.nop()
            with e.Else():
                program(e, ALL_TILES)
                e.nop()

        @block.sync
        def _(e):
            m = mask.rearrange("a b s k -> (a b s) k")
            for half in range(2):
                e.dma_start(mask_u8[SEQ * half:SEQ * half + SEQ, :], m).then_inc(mask_in, 16)
            load_cross_w(e, 0)
            choose(e, cross_sync)
            if not only_cross:
                self_sync(e)
                ff_sync(e)

        @block.gpsimd
        def _(e):
            e.memset(ident[:], 0.0).then_inc(const_ready, 1)
            e.memset(ones[:], 1.0).then_inc(const_ready, 1)
            e.memset(minus_half[:], -0.5).then_inc(const_ready, 1)
            e.memset(ln_eps[:], LN_EPS).then_inc(const_ready, 1)
            e.wait_ge(const_ready, 4)
            e.affine_select(out=ident[:], in_=ident[:], compare_op=ALU.not_equal, fill=1.0, base=0,
                            pattern=[[-1, P]], channel_multiplier=1).then_inc(const_ready, 1)
            e.memset(q_pad[:].rearrange("p c a b h s -> p (c a b h s)"), 0.0).then_inc(pads_ready, 1)
            e.memset(cxn[:].rearrange("p t d -> p (t d)"), 0.0).then_inc(pads_ready, 1)
            e.wait_ge(mask_step, 1)
            e.memset(c_a[:].rearrange("p h d -> p (h d)"), 0.0).then_inc(pads_ready, 1)
            e.wait_ge(w_lo_ready, 2)
            e.memset(cv[:, :, :, :, DK:VW].rearrange("p a j h o -> p (a j) (h o)"), 1.0) \
                .then_inc(pads_ready, 1)
            choose(e, cross_pool)
            if not only_cross:
                self_pool(e)
                ff_pool(e)

        @block.scalar
        def _(e):
            cross_w_hi(e, 0)
            choose(e, cross_act)
            if not only_cross:
                self_act(e)
                ff_act(e)

        @block.vector
        def _(e):
            e.wait_ge(mask_in, 32)
            nc.vector.tensor_copy(mask_f, mask_u8).then_inc(mask_step, 1)
            e.wait_ge(mask_step, 1)
            nc.vector.reduce_sum(counts[:, 0:1], mask_f, AXIS.X)
            nc.vector.reduce_sum(counts[:, 1:2], mask_f[:, 0:KEYS - P], AXIS.X).then_inc(mask_step, 1)
            e.wait_ge(mask_step, 2)
            nc.vector.tensor_scalar(counts[:, 2:3], counts[:, 0:1], -1.0, float(KEYS),
                                    ALU.mult, ALU.add).then_inc(mask_step, 1)
            e.wait_ge(mask_step, 3)
            nc.vector.reciprocal(counts[:, 3:4], counts[:, 2:3]).then_inc(mask_step, 1)
            e.wait_ge(mask_step, 4)
            nc.vector.tensor_scalar(counts[:, 2:3], counts[:, 3:4], 0.0, None, ALU.mult) \
                .then_inc(mask_step, 1)
            e.wait_ge(mask_step, 5)
            nc.vector.tensor_scalar(mask_bias[:], mask_f, MASKED, counts[:, 2:3],
                                    ALU.mult, ALU.add).then_inc(mask_step, 1)
            e.wait_ge(mask_counted, 1)
            nc.vector.tensor_scalar(flag_i[0:1, 0:1], S[0:1, 0:1], float(P * (KEYS - P)), None,
                                    ALU.is_ge).then_inc(flag_ready, 1)
            cross_w_lo(e, 0)
            e.wait_ge(mask_step, 6)
            choose(e, cross_dve)
            if not only_cross:
                self_dve(e)
                ff_dve(e)

        @block.tensor
        def _(e):
            e.wait_ge(const_ready, 5)
            e.wait_ge(mask_step, 2)
            nc.tensor.matmul(S[0:1, 0:2], counts[:, 1:2], ones[:, 0:2], start=True, stop=True) \
                .then_inc(mask_counted, 1)
            e.wait_ge(flag_ready, 1)
            choose(e, cross_pe)
            if not only_cross:
                self_pe(e)
                ff_pe(e)


def tiled(w):
    import numpy as np
    t = np.ascontiguousarray(w.T)
    return np.ascontiguousarray(t.reshape(t.shape[0] // 128, 128, t.shape[1]).transpose(1, 0, 2)) \
        .reshape(128, -1)


def kernel(x, ctx_1024, mask_1x1xSxS2_bk1, L0_xattn_W_Q, L0_xattn_W_K, L0_xattn_W_V, L0_xattn_W_O,
           L0_attn_Wq, L0_attn_bq, L0_attn_Wk, L0_attn_bk, L0_attn_Wv, L0_attn_bv, L0_attn_Wo,
           L0_attn_bo, L0_ffn_W1, L0_ffn_b1, L0_ffn_W2, L0_ffn_b2):
    import numpy as np
    import concourse.bacc as bacc
    from concourse.bass_utils import run_bass_kernel_spmd

    a = np.asarray
    ctx = np.ascontiguousarray(a(ctx_1024).reshape(BATCHES, KEY_TILES, P, DC, P)
                               .transpose(0, 1, 4, 3, 2)).reshape(BATCHES, KEY_TILES, P, DC * P)
    arrays = {
        "x": a(x).reshape(TOKENS, D),
        "ctx": ctx,
        "mask": a(mask_1x1xSxS2_bk1),
        "w_cross": np.stack([tiled(a(w)) for w in
                             (L0_xattn_W_Q, L0_xattn_W_K, L0_xattn_W_V, L0_xattn_W_O)]),
        "w_self": np.stack([tiled(a(w)) for w in
                            (L0_attn_Wq, L0_attn_Wk, L0_attn_Wv, L0_attn_Wo)]),
        "bq": np.ascontiguousarray(a(L0_attn_bq).reshape(DC, P).T),
        "bk": np.ascontiguousarray(a(L0_attn_bk).reshape(DC, P).T),
        "bv": a(L0_attn_bv),
        "bo": a(L0_attn_bo),
        "w1": tiled(a(L0_ffn_W1)),
        "b1": np.ascontiguousarray(a(L0_ffn_b1).reshape(FC, P).T),
        "w2": tiled(a(L0_ffn_W2)),
        "b2": a(L0_ffn_b2),
    }
    nc = bacc.Bacc("TRN2", target_bir_lowering=False, num_devices=1)
    args = [nc.dram_tensor(f"in_{n}", v.shape, mybir.dt.from_np(v.dtype), kind="ExternalInput").ap()
            for n, v in arrays.items()]
    out = nc.dram_tensor("out", (TOKENS, D), F32, kind="ExternalOutput").ap()
    build(nc, *args, out)
    result = run_bass_kernel_spmd(nc, [{f"in_{n}": v for n, v in arrays.items()}], core_ids=[0])
    return np.asarray(result.results[0]["out"]).reshape(BATCHES, SEQ, D)
```

```python
from collections import namedtuple
from contextlib import ExitStack

import concourse.bass as bass
import concourse.mybir as mybir

F32 = mybir.dt.float32
F32R = mybir.dt.float32r
I32 = mybir.dt.int32
U8 = mybir.dt.uint8
ALU = mybir.AluOpType
ACT = mybir.ActivationFunctionType
AXIS = mybir.AxisListType

P = 128
BATCHES, SEQ, D, KEYS = 64, 64, 512, 512
HEADS = 16
DK = D // HEADS
DC = D // P
PAIRS = HEADS // 2
TOKENS = BATCHES * SEQ
FF = 4 * D
FC = FF // P
KEY_TILES = KEYS // P
SCORE_SCALE = float(DK) ** -0.5
MASKED = -1e30
LN_EPS = 1e-5
QUANT_EPS = 1e-5

Unit = namedtuple("Unit", "half off")


def later(u, n):
    return Unit(u.half, u.off + n)


def parity(u):
    return u.off % 2


def number(u):
    return u.half * 2 + u.off


def is_unit(u, n):
    return isinstance(u.half, int) and number(u) == n


def total(u, per_unit, k=0):
    return u.half * (2 * per_unit) + (per_unit * u.off + k)


def total_of_parity(u, per_unit, k=0):
    return u.half * per_unit + (per_unit * (u.off // 2) + k)


def wait(eng, sem, value):
    if not (isinstance(value, int) and value <= 0):
        eng.wait_ge(sem, value)


class Banks:

    def __init__(self, prologue, full, last_but_one, last):
        self.prologue = prologue
        self.uses = {"full": full, "last_but_one": last_but_one, "last": last}
        self.first, self.per = len(prologue), len(full)

    def before(self, u, name=None, kind="full"):
        if u is None:
            return self.prologue.index(name)
        fewer = self.per - len(self.uses["last_but_one"]) if kind == "last" else 0
        n = self.uses[kind].index(name) if name else 0
        return self.first + self.per * u.off - fewer + n

    def at(self, u, name, kind="full"):
        j = self.before(u, name, kind)
        earlier = (j + 1 - j % 2) // 2
        return j % 2, earlier if u is None else u.half * self.per + earlier

    def drained(self, bank, units=0):
        n = self.first
        if units:
            n += self.per * (units - 2) + len(self.uses["last_but_one"]) + len(self.uses["last"])
        return (n + 1 - bank) // 2


def run_steps(eng, units, step):
    step(Unit(0, 0), "full")
    step(Unit(0, 1), "full")
    with eng.Fori(1, units // 2 - 1) as half:
        step(Unit(half, 0), "full")
        step(Unit(half, 1), "full")
    step(Unit(units // 2 - 1, 0), "last_but_one")
    step(Unit(units // 2 - 1, 1), "last")


def build(nc, x, ctx, mask, w_cross, w_self, bq, bk, bv, bo, w1, b1, w2, b2,
          out):
    x1 = nc.dram_tensor("x1", (TOKENS, D), F32, kind="Internal").ap()
    x2 = nc.dram_tensor("x2", (TOKENS, D), F32, kind="Internal").ap()
    outer = ExitStack()
    with outer:
        def sem(name):
            return outer.enter_context(nc.semaphore(name))

        def sems(name):
            return [sem(f"{name}_{i}") for i in range(2)]

        def sb(stack, name, shape, dt=F32):
            return stack.enter_context(nc.sbuf_tensor(name, shape, dt))

        PJ = [outer.enter_context(nc.psum_tensor(f"project_{i}", [P, 512], F32)) for i in range(2)]
        S = outer.enter_context(nc.psum_tensor("scores", [P, 1024], F32))
        PT = outer.enter_context(nc.psum_tensor("probs_t_psum", [P, 1024], F32))
        PV = outer.enter_context(nc.psum_tensor("attended_t", [P, 2, 512], F32))
        YB = [S[:, 0:512], S[:, 512:1024], PT[:, 0:512], PT[:, 512:1024]]
        XB = [PV[:, 0, :], PV[:, 1, :]]

        ident = sb(outer, "ident", [P, P])
        ones = sb(outer, "ones", [P, P])
        minus_half = sb(outer, "minus_half", [P, 1])
        ln_eps = sb(outer, "ln_eps", [P, 1])
        flag_i = sb(outer, "only_last_tile", [1, 2], I32)
        stats = sb(outer, "ln_stats_buf", [P, 4, 6])
        stats_seen = sb(outer, "stats_seen", [1, 1])
        mean_var = sb(outer, "mean_var", [P, 4, 2])
        var_eps = sb(outer, "var_eps", [P, 4, 1])
        rstd = sb(outer, "rstd", [P, 4, 1])
        abs_sum = sb(outer, "abs_sum", [P, 2, FC])
        abs_total = sb(outer, "abs_total", [P, 2])
        thresh = sb(outer, "thresholds", [P, 2, 2])
        row_max = sb(outer, "row_max", [P, HEADS])
        exp_bias = sb(outer, "exp_bias", [P, 2, HEADS])
        row_sum = sb(outer, "row_sum", [P, HEADS])
        row_scale = sb(outer, "row_scale", [P, HEADS])
        bq_sb = sb(outer, "bq_sb", [P, DC])
        bk_sb = sb(outer, "bk_sb", [P, DC])
        b1_sb = sb(outer, "b1_sb", [P, FC])

        with ExitStack() as st:
            q_pad = sb(st, "q_pad", [P, DC, 2, 4, 2, SEQ])
            ck_t = sb(st, "cross_k_t", [P, 2, DC, 4, P])
            cx = sb(st, "cross_x", [P, 2, 2, D])
            cxn = sb(st, "cross_x_norm", [P, 2, D])
            cxt_hi = sb(st, "cross_xt_hi", [P, DC, 4 * SEQ], F32R)
            cxt_lo = sb(st, "cross_xt_lo", [P, DC, 4 * SEQ], F32R)
            c_sp = sb(st, "cross_scores_probs", [P, 2048])
            c_p = c_sp[:, 1024:2048]
            c_pt = sb(st, "cross_probs_t", [P, 1024])
            cw_hi = sb(st, "cross_w_hi", [P, 4, DC, D], F32R)
            cw_lo = sb(st, "cross_w_lo", [P, 4, DC, D], F32R)
            ctx_raw = sb(st, "ctx_raw", [P, 2, 4, DC, P])
            ctx_hi = sb(st, "ctx_hi", [P, 2, 4, DC, P], F32R)
            ctx_lo = sb(st, "ctx_lo", [P, 2, 4, DC, P], F32R)
            cv = sb(st, "cross_v", [P, 2, 4, D])
            cat_hi = sb(st, "cross_at_hi", [P, DC, P], F32R)
            cat_lo = sb(st, "cross_at_lo", [P, DC, P], F32R)
            mask_bias = sb(st, "mask_bias", [P, KEYS])
            counts = sb(st, "mask_counts", [P, 4])
            c_s2 = sb(st, "cross_scores_2", [P, 1024])
            c_s = [c_sp[:, 0:1024], c_s2[:]]
            mask_u8 = sb(st, "mask_u8", [P, KEYS], U8)
            mask_f = c_pt[:, 0:KEYS]
        with ExitStack() as st:
            w_raw = sb(st, "ff_w_raw", [P, 2, FC, 512])
        f_weights = ExitStack()
        outer.enter_context(f_weights)
        w1_q = sb(f_weights, "w1_ternary", [P, DC, FF], F32R)
        w2_q = sb(f_weights, "w2_ternary", [P, FC, D], F32R)
        with ExitStack() as st:
            sw_hi = sb(st, "self_w_hi", [P, 4, DC, D], F32R)
            sw_lo = sb(st, "self_w_lo", [P, 4, DC, D], F32R)
            sq_t = sb(st, "self_q_t", [P, 2, DC, 4, SEQ])
            sk_t = sb(st, "self_k_t", [P, 2, DC, 4, SEQ])
            sres = sb(st, "self_residual", [P, 2, 2, D])
            sv = sb(st, "self_v", [P, 2, 2, D])
            sx = sb(st, "self_x", [P, 2, 2, D])
            sxn = sb(st, "self_x_norm", [P, 2, D])
            bv_sb = sb(st, "bv_sb", [P, D])
            bo_sb = sb(st, "bo_sb", [P, D])
            sxt_hi = sb(st, "self_xt_hi", [P, DC, 4 * SEQ], F32R)
            sxt_lo = sb(st, "self_xt_lo", [P, DC, 4 * SEQ], F32R)
            s_p = sb(st, "self_probs", [P, 1024])
            s_pt = sb(st, "self_probs_t", [P, 1024])
            sat_hi = sb(st, "self_at_hi", [P, DC, P], F32R)
            sat_lo = sb(st, "self_at_lo", [P, DC, P], F32R)
            f_scratch = sb(st, "ff_weight_scratch", [P, 512])
            s_stages = [sq_t[:].rearrange("p a c b s -> p (a c b s)"),
                        sk_t[:].rearrange("p a c b s -> p (a c b s)"),
                        sv[:].rearrange("p a t d -> p (a t d)"),
                        sres[:].rearrange("p a t d -> p (a t d)")]
        with ExitStack() as st:
            fx = sb(st, "ff_x", [P, 2, 4, D])
            fxn = sb(st, "ff_x_norm", [P, 2, D])
            b2_sb = sb(st, "b2_sb", [P, D])
            sb(st, "ff_gap", [P, D])
            h_hi = sb(st, "hidden_hi", [P, 4, 512], F32R)
            fxt_0 = sb(st, "ff_xt_0", [P, 2, DC, 4 * P], F32R)
            fres = sb(st, "ff_residual", [P, 2, 4, D])
            h_lo = sb(st, "hidden_lo", [P, 4, 512], F32R)
            h_raw = sb(st, "hidden", [P, 2, 512])
            fxt_1 = sb(st, "ff_xt_1", [P, 2, DC, 4 * P], F32R)
            fxt_hi = [t[:, 0] for t in (fxt_0, fxt_1)]
            fxt_lo = [t[:, 1] for t in (fxt_0, fxt_1)]

        const_ready = sem("const_ready")
        mask_in = sem("mask_in")
        mask_step = sem("mask_step")
        mask_counted = sem("mask_counted")
        flag_ready = sem("flag_ready")
        w_in = [sem(f"w_in_{n}") for n in range(4)]
        w_hi_ready = sem("w_hi_ready")
        w_lo_ready = sem("w_lo_ready")
        pads_ready = sem("pads_ready")

        class Phase:
            def __init__(self, name):
                s = lambda n: sem(f"{name}_{n}")
                self.x_in = [s(f"x_in_{i}") for i in range(2)]
                self.stats = s("stats")
                self.agg = s("agg")
                self.eps = s("eps")
                self.rstd = s("rstd")
                self.xn = s("xn")
                self.res = s("residual")
                self.pj_full = [s(f"pj_full_{i}") for i in range(2)]
                self.pj_free = [s(f"pj_free_{i}") for i in range(2)]
                self.xt_hi = s("xt_hi")
                self.at_hi = s("at_hi")
                self.s_full = s("s_full")
                self.s_free = s("s_free")
                self.s_max = s("s_max")
                self.s_bias = s("s_bias")
                self.p_ready = s("p_ready")
                self.p_scale = s("p_scale")
                self.p_norm = s("p_norm")
                self.pt_full = s("pt_full")
                self.pt_ready = s("pt_ready")
                self.pv_done = s("pv_done")
                self.at_lo = s("at_lo")
                self.stored = [s(f"stored_{i}") for i in range(2)]

        C = Phase("cross")
        ctx_in = sems("ctx_in")
        ctx_hi_ready = sem("ctx_hi_ready")
        ctx_lo_ready = sem("ctx_lo_ready")
        G = Phase("self")
        cross_w_used = sem("cross_w_used")
        self_bias_in = sem("self_bias_in")
        sw_in = [sem(f"sw_in_{n}") for n in range(4)]
        sw_hi_ready = sem("sw_hi_ready")
        sw_lo_ready = sem("sw_lo_ready")
        ff_bias_in = sem("ff_bias_in")
        fw_in = sems("fw_in")
        fw_summed = sem("fw_summed")
        fw_abs = sem("fw_abs")
        fw_total = sem("fw_total")
        fw_thresh = sem("fw_thresh")
        fw_neg = sem("fw_neg")
        fw_ready = sem("fw_ready")
        fx_in = sems("fx_in")
        f_stats, f_agg, f_eps, f_rstd, f_xn, f_res = (
            sem("f_stats"), sem("f_agg"), sem("f_eps"), sem("f_rstd"), sem("f_xn"), sem("f_res"))
        xb_full, xb_free, fxt_hi_ready = sem("xb_full"), sem("xb_free"), sem("fxt_hi_ready")
        h_full, h_relu, h_hi_ready, h_lo_ready = (
            sem("h_full"), sem("h_relu"), sem("h_hi_ready"), sem("h_lo_ready"))
        y_m = sem("y_m")
        y_full = [sem(f"y_full_{t}") for t in range(4)]
        y_new = [sem(f"y_new_{t}") for t in range(4)]
        f_stored = sems("f_stored")

        def split_products(e, out_ap, pairs, before_last=None):
            n = 0
            last = None
            for s_hi, s_lo, m_hi, m_lo in pairs:
                for a, b in ((s_hi, m_hi), (s_hi, m_lo), (s_lo, m_hi)):
                    if before_last and n == 3 * len(pairs) - 1:
                        before_last()
                    last = nc.tensor.matmul(out_ap, a, b, start=(n == 0),
                                            stop=(n == 3 * len(pairs) - 1))
                    n += 1
            return last

        W_ORDER = (1, 0, 2, 3)
        c_stages = [cv[:, 0].rearrange("p j d -> p (j d)"), cv[:, 1].rearrange("p j d -> p (j d)"),
                    ck_t[:, 1].rearrange("p c j k -> p (c j k)"), c_sp[:]]
        flat_w = lambda t, n: t[:, n].rearrange("p c d -> p (c d)")

        def load_cross_w(e, n):
            e.dma_start(c_stages[n], w_cross[W_ORDER[n]]).then_inc(w_in[n], 16)

        def cross_w_hi(e, n):
            e.wait_ge(w_in[n], 16)
            nc.scalar.activation(flat_w(cw_hi, W_ORDER[n]), c_stages[n], ACT.Copy) \
                .then_inc(w_hi_ready, 1)

        def cross_w_lo(e, n):
            e.wait_ge(w_hi_ready, n + 1)
            nc.vector.tensor_tensor(flat_w(cw_lo, W_ORDER[n]), c_stages[n],
                                    flat_w(cw_hi, W_ORDER[n]).bitcast(F32), ALU.subtract) \
                .then_inc(w_lo_ready, 1)

        def load_self_w(e, n):
            e.dma_start(s_stages[n], w_self[n]).then_inc(sw_in[n], 16)

        def self_w_hi(e, n):
            e.wait_ge(sw_in[n], 16)
            nc.scalar.activation(flat_w(sw_hi, n), s_stages[n], ACT.Copy).then_inc(sw_hi_ready, 1)

        def self_w_lo(e, n):
            e.wait_ge(sw_hi_ready, n + 1)
            nc.vector.tensor_tensor(flat_w(sw_lo, n), s_stages[n],
                                    flat_w(sw_hi, n).bitcast(F32), ALU.subtract) \
                .then_inc(sw_lo_ready, 1)

        def row_bias(e, ph, n, buf, groups, scores_in):
            nc.vector.reduce_max(row_max[:, 0:groups], scores_in, AXIS.X).then_inc(ph.s_max, 1)
            wait(e, ph.s_max, n(1))
            nc.vector.tensor_scalar(exp_bias[:, buf, 0:groups], row_max[:, 0:groups], -SCORE_SCALE, None,
                                    ALU.mult).then_inc(ph.s_bias, 1)

        def exponentials_of(e, ph, n, buf, groups, scores_in, probs):
            wait(e, ph.s_bias, n(1))
            width = 1024 // groups
            for g in range(groups):
                cols = slice(g * width, g * width + width)
                last = nc.scalar.activation(probs[:, cols], scores_in[:, cols], ACT.Exp,
                                            bias=exp_bias[:, buf, g:g + 1], scale=SCORE_SCALE,
                                            accum_out=row_sum[:, g:g + 1])
            last.then_inc(ph.p_ready, 1)

        def divide_by_sums(e, ph, n, groups, probs):
            wait(e, ph.p_ready, n(1))
            nc.vector.reciprocal(row_scale[:, 0:groups], row_sum[:, 0:groups]) \
                .then_inc(ph.p_scale, 1)
            wait(e, ph.p_scale, n(1))
            width = 1024 // groups
            p = probs.rearrange("p (g k) -> p g k", g=groups)
            nc.vector.tensor_tensor(
                p, p, row_scale[:, 0:groups].unsqueeze(2).to_broadcast([P, groups, width]),
                ALU.mult).then_inc(ph.p_norm, 1)

        S_UNITS, NT = TOKENS // (4 * SEQ), 2
        s_x1 = x1.rearrange("(u t p) d -> u t p d", t=NT, p=P)
        s_x2 = x2.rearrange("(u t p) d -> u t p d", t=NT, p=P)

        def load_self_x(e, v):
            wait(e, G.xn, total(v, NT, -NT))
            wait(e, G.res, total(v, NT, -NT))
            for t in range(NT):
                e.dma_start(sx[:, parity(v), t, :], s_x1[number(v), t]) \
                    .then_inc(G.x_in[parity(v)], 16)

        def self_ln_statistics(e, v):
            wait(e, G.x_in[parity(v)], total_of_parity(v, 16 * NT, 16 * NT))
            for t in range(NT):
                nc.vector.bn_stats(stats[:, t, :], sx[:, parity(v), t, :]).then_inc(G.stats, 1)

        def self_ln_normalise(e, v):
            for t in range(NT):
                nc.vector.bn_aggr(mean_var[:, t, :], stats[:, t, :]).then_inc(G.agg, 1)
            for t in range(NT):
                wait(e, G.rstd, total(v, NT, t + 1))
                nc.vector.tensor_scalar(sxn[:, t, :], sx[:, parity(v), t, :],
                                        mean_var[:, t, 0:1], rstd[:, t, :],
                                        ALU.subtract, ALU.mult).then_inc(G.xn, 1)

        class Cross:
            def __init__(self, kt):
                self.kt, self.b = kt, 4 // kt
                self.units = BATCHES // self.b
                self.tokens = self.b * SEQ
                self.nt = max(1, self.b // 2)
                self.tp = min(P, self.tokens)
                two = self.nt == 2
                full = (["K0", "K1", "K2", "K3", "X0"] + ["X1"] * two + ["V0", "V1", "V2"]
                        + ["O0"] * two + ["Q0", "Q1", "V3", f"O{self.nt - 1}"])
                self.banks = Banks(
                    [f"K{i}" for i in range(4)] + [f"X{t}" for t in range(self.nt)]
                    + ["Q0", "Q1"] + [f"V{i}" for i in range(4)],
                    full, full, [n for n in full if n[0] == "O"])
                self.x = x.rearrange("(u t p) d -> u t p d", t=self.nt, p=self.tp)
                self.x1 = x1.rearrange("(u t p) d -> u t p d", t=self.nt, p=self.tp)
                self.ctx = (ctx.rearrange("(u b) k p n -> u b k p n", b=self.b)[:, :, 3]
                            if kt == 1 else ctx)
                self.attended_t = lambda t: PV[:, t, 0:DC * self.tp].rearrange("p (c s) -> p c s", c=DC)
                self.tile_of = (lambda q: q // 2) if two else (lambda q: 0)

        def cross_sync(e, K):
            def load_ctx(v):
                wait(e, ctx_lo_ready, total(v, 1, -1))
                for j in range(4):
                    e.dma_start(ctx_raw[:, parity(v), j, :, :].rearrange("p c k -> p (c k)"),
                                K.ctx[number(v), j]).then_inc(ctx_in[parity(v)], 16)

            def load_x(v):
                for t in range(K.nt):
                    e.dma_start(cx[0:K.tp, parity(v), t, :], K.x[number(v), t]) \
                        .then_inc(C.x_in[parity(v)], 16)

            def step(u, kind):
                more, ahead = kind != "last", kind == "full"
                if ahead:
                    load_ctx(later(u, 2))
                elif more:
                    wait(e, ctx_lo_ready, total(u, 1, 2))
                    load_self_w(e, 0)
                    load_self_w(e, 1)
                else:
                    bank, before = K.banks.at(later(u, -1), "V3", "last_but_one")
                    e.wait_ge(C.pj_free[bank], before + 1)
                    load_self_w(e, 2)
                    for i in range(2):
                        e.wait_ge(C.stored[i], 16 * K.nt * (K.units // 2 - 1))
                    load_self_x(e, Unit(0, 0))
                    load_self_w(e, 3)
                    load_self_x(e, Unit(0, 1))
                    for dst, src in ((bq_sb, bq), (bk_sb, bk), (b1_sb, b1)):
                        e.dma_start(dst[:], src).then_inc(self_bias_in, 16)
                    for dst, src in ((bv_sb, bv), (bo_sb, bo)):
                        e.dma_start(dst[:], src.unsqueeze(0).to_broadcast([P, D])) \
                            .then_inc(self_bias_in, 16)
                for t in range(K.nt):
                    bank, before = K.banks.at(u, f"O{t}", kind)
                    wait(e, C.pj_free[bank], before + 1)
                    e.dma_start(K.x1[number(u), t], cx[0:K.tp, parity(u), t, :]) \
                        .then_inc(C.stored[parity(u)], 16)
                if ahead:
                    wait(e, C.stored[parity(u)], total_of_parity(u, 16 * K.nt, 16 * K.nt))
                    load_x(later(u, 2))

            load_ctx(Unit(0, 0))
            load_x(Unit(0, 0))
            for n in range(1, 4):
                load_cross_w(e, n)
            load_ctx(Unit(0, 1))
            load_x(Unit(0, 1))
            run_steps(e, K.units, step)
            for i in range(2):
                e.wait_ge(C.stored[i], 16 * K.nt * K.units // 2)

        def cross_pe(e, K):
            def begin(u, name, kind="full"):
                bank, before = K.banks.at(u, name, kind)
                wait(e, C.pj_free[bank], before)
                return bank

            def k_proj(u, v, m):
                bank = begin(u, f"K{m}")
                if m == 0:
                    wait(e, ctx_lo_ready, total(v, 1, 1))
                w = slice(m * P, m * P + P)
                split_products(e, PJ[bank][:], [
                    (cw_hi[:, 1, c, w], cw_lo[:, 1, c, w],
                     ctx_hi[:, parity(v), :, c, :], ctx_lo[:, parity(v), :, c, :])
                    for c in range(DC)]).then_inc(C.pj_full[bank], 1)

            def v_proj(u, v, j):
                bank = begin(u, f"V{j}")
                split_products(e, PJ[bank][:], [
                    (ctx_hi[:, parity(v), j, c, :], ctx_lo[:, parity(v), j, c, :],
                     cw_hi[:, 2, c, :], cw_lo[:, 2, c, :])
                    for c in range(DC)]).then_inc(C.pj_full[bank], 1)

            def x_transpose(u, v, t):
                bank = begin(u, f"X{t}")
                wait(e, C.xn, total(v, K.nt, t + 1))
                for c in range(DC):
                    last = nc.tensor.transpose(PJ[bank][:, c * P:c * P + P],
                                               cxn[:, t, c * P:c * P + P], ident[:])
                last.then_inc(C.pj_full[bank], 1)

            def q_proj(u, n):
                bank = begin(u, f"Q{n}")
                if n == 0:
                    for t in range(K.nt):
                        b, before = K.banks.at(u, f"X{t}")
                        wait(e, C.pj_free[b], before + 1)
                for i in range(2):
                    w = slice((2 * n + i) * P, (2 * n + i + 1) * P)
                    last = split_products(e, PJ[bank][:, 256 * i:256 * i + K.tokens], [
                        (cw_hi[:, 0, c, w], cw_lo[:, 0, c, w],
                         cxt_hi[:, c, 0:K.tokens], cxt_lo[:, c, 0:K.tokens]) for c in range(DC)])
                last.then_inc(C.pj_full[bank], 1)

            def scores(u, q):
                wait(e, C.s_free, total(u, 4, q))
                n = K.kt * P
                for i in range(PAIRS // K.kt):
                    pair = i if K.kt == 1 else q * (PAIRS // K.kt) + i
                    batch = q if K.kt == 1 else 0
                    keys = (ck_t[:, parity(u), pair // 2, q, :] if K.kt == 1 else
                            ck_t[:, parity(u), pair // 2, :, :].rearrange("p j k -> p (j k)"))
                    last = nc.tensor.matmul(
                        S[:, i * n:(i + 1) * n],
                        q_pad[:, pair // 2, pair % 2, batch, :, :].rearrange("p a s -> p (a s)"),
                        keys, start=True, stop=True)
                last.then_inc(C.s_full, 1)

            def transposes(u, q):
                wait(e, C.pt_ready, total(u, 4, q))
                wait(e, C.p_norm, total(u, 4, q + 1))
                for i in range(8):
                    last = nc.tensor.transpose(PT[:, i * P:i * P + P], c_p[:, i * P:i * P + P],
                                               ident[:])
                last.then_inc(C.pt_full, 1)

            def attend(u, q):
                t = K.tile_of(q)
                if q == 0 or t != K.tile_of(q - 1):
                    wait(e, C.at_lo, total(u, K.nt, t + 1 - K.nt))
                wait(e, C.pt_ready, total(u, 4, q + 1))
                for i in range(HEADS // K.kt):
                    head = i if K.kt == 1 else q * (HEADS // K.kt) + i
                    rows = slice(DK * (head % 4), DK * (head % 4) + DK)
                    col = (head // 4) * K.tp + (SEQ * (q % 2) if K.kt == 1 else 0)
                    for k in range(K.kt):
                        at = ((i // 2) * K.kt + k) * P + SEQ * (head % 2)
                        last = nc.tensor.matmul(
                            PV[rows, t, col:col + SEQ],
                            cv[:, parity(u), q if K.kt == 1 else k, DK * head:DK * head + DK],
                            c_pt[:, at:at + SEQ], start=(k == 0), stop=(k == K.kt - 1))
                last.then_inc(C.pv_done, 1)

            def o_proj(u, t, kind):
                bank = begin(u, f"O{t}", kind)
                wait(e, C.at_lo, total(u, K.nt, t + 1))
                split_products(e, PJ[bank][0:K.tp, :], [
                    (cat_hi[:, c, 0:K.tp], cat_lo[:, c, 0:K.tp], cw_hi[:, 3, c, :], cw_lo[:, 3, c, :])
                    for c in range(DC)]).then_inc(C.pj_full[bank], 1)

            def step(u, kind):
                more, ahead = kind != "last", kind == "full"
                v = later(u, 1)
                if is_unit(u, 0):
                    bank, before = K.banks.at(None, "Q1")
                else:
                    bank, before = K.banks.at(later(u, -1), "Q1",
                                              "last_but_one" if kind == "last" else "full")
                e.wait_ge(C.pj_free[bank], before + 1)
                scores(u, 0)
                if is_unit(u, 0):
                    e.wait_ge(w_lo_ready, 4)
                else:
                    o_proj(later(u, -1), K.nt - 1, "last_but_one" if kind == "last" else "full")
                if more:
                    k_proj(u, v, 0)
                scores(u, 1)
                if more:
                    k_proj(u, v, 1)
                    transposes(u, 0)
                    k_proj(u, v, 2)
                    attend(u, 0)
                    scores(u, 2)
                    k_proj(u, v, 3)
                    transposes(u, 1)
                    for t in range(K.nt):
                        x_transpose(u, v, t)
                    scores(u, 3)
                    attend(u, 1)
                    v_proj(u, v, 0)
                    v_proj(u, v, 1)
                    transposes(u, 2)
                    v_proj(u, v, 2)
                else:
                    scores(u, 2)
                    transposes(u, 0)
                    scores(u, 3)
                    attend(u, 0)
                    transposes(u, 1)
                    attend(u, 1)
                    transposes(u, 2)
                attend(u, 2)
                if K.nt == 2:
                    o_proj(u, 0, kind)
                transposes(u, 3)
                if more:
                    q_proj(u, 0)
                attend(u, 3)
                if more:
                    q_proj(u, 1)
                    v_proj(u, v, 3)
                else:
                    o_proj(u, K.nt - 1, kind)

            first = Unit(0, 0)
            e.wait_ge(w_lo_ready, 1)
            for m in range(4):
                k_proj(None, first, m)
            e.wait_ge(pads_ready, 2)
            for t in range(K.nt):
                x_transpose(None, first, t)
            e.wait_ge(w_lo_ready, 2)
            q_proj(None, 0)
            q_proj(None, 1)
            e.wait_ge(w_lo_ready, 3)
            for j in range(4):
                v_proj(None, first, j)
            run_steps(e, K.units, step)
            for bank in range(2):
                e.wait_ge(C.pj_free[bank], K.banks.drained(bank, K.units))
            e.nop().then_inc(cross_w_used, 1)

        def cross_act(e, K):
            def full(u, name, kind="full"):
                bank, before = K.banks.at(u, name, kind)
                wait(e, C.pj_full[bank], before + 1)
                return bank

            def keys_out(u, v, m):
                bank = full(u, f"K{m}")
                nc.scalar.activation(ck_t[:, parity(v), m, :, :].rearrange("p j k -> p (j k)"),
                                     PJ[bank][:], ACT.Copy).then_inc(C.pj_free[bank], 1)

            def x_hi(u, v, t):
                bank = full(u, f"X{t}")
                nc.scalar.activation(
                    cxt_hi[:, :, t * P:t * P + K.tp],
                    PJ[bank][:].rearrange("p (c s) -> p c s", c=DC)[:, :, 0:K.tp],
                    ACT.Copy).then_inc(C.xt_hi, 1)

            def a_hi(u, t):
                wait(e, C.pv_done, total(u, 4, 4 // K.nt * (t + 1)))
                nc.scalar.activation(cat_hi[:, :, 0:K.tp], K.attended_t(t), ACT.Copy) \
                    .then_inc(C.at_hi, 1)

            def queries_out(u, n):
                bank = full(u, f"Q{n}")
                chunks = PJ[bank][:].rearrange("p (i b s) -> p i b s", i=2, s=SEQ)
                for r in range(4):
                    rows = slice(DK * r, DK * r + DK)
                    last = nc.scalar.activation(
                        q_pad[rows, 2 * n:2 * n + 2, r // 2, 0:K.b, r % 2, :],
                        chunks[rows, :, 0:K.b, :], ACT.Copy)
                last.then_inc(C.pj_free[bank], 1)

            def exponentials(u, q):
                exponentials_of(e, C, lambda k: total(u, 4, q + k), q % 2, PAIRS // K.kt, c_s[q % 2],
                                c_p)

            def probs_t_out(u, q):
                wait(e, C.pt_full, total(u, 4, q + 1))
                wait(e, C.pv_done, total(u, 4, q))
                nc.scalar.activation(c_pt[:], PT[:], ACT.Copy).then_inc(C.pt_ready, 1)

            def split_ctx(v):
                wait(e, ctx_in[parity(v)], total_of_parity(v, 64, 64))
                nc.scalar.activation(ctx_hi[:, parity(v)].rearrange("p j c k -> p (j c k)"),
                                     ctx_raw[:, parity(v)].rearrange("p j c k -> p (j c k)"),
                                     ACT.Copy).then_inc(ctx_hi_ready, 1)

            def step(u, kind):
                more, ahead = kind != "last", kind == "full"
                v = later(u, 1)
                exponentials(u, 0)
                if more:
                    keys_out(u, v, 0)
                    keys_out(u, v, 1)
                probs_t_out(u, 0)
                exponentials(u, 1)
                if more:
                    keys_out(u, v, 2)
                    keys_out(u, v, 3)
                probs_t_out(u, 1)
                if more:
                    for t in range(K.nt):
                        x_hi(u, v, t)
                exponentials(u, 2)
                if K.nt == 2:
                    a_hi(u, 0)
                if not more:
                    self_w_hi(e, 0)
                probs_t_out(u, 2)
                exponentials(u, 3)
                if not more:
                    self_w_hi(e, 1)
                if ahead:
                    split_ctx(later(u, 2))
                if not more:
                    self_w_hi(e, 2)
                probs_t_out(u, 3)
                if more:
                    queries_out(u, 0)
                a_hi(u, K.nt - 1)
                if more:
                    queries_out(u, 1)

            first = Unit(0, 0)
            split_ctx(first)
            cross_w_hi(e, 1)
            keys_out(None, first, 0)
            keys_out(None, first, 1)
            cross_w_hi(e, 2)
            keys_out(None, first, 2)
            keys_out(None, first, 3)
            for t in range(K.nt):
                x_hi(None, first, t)
            e.wait_ge(pads_ready, 1)
            queries_out(None, 0)
            cross_w_hi(e, 3)
            queries_out(None, 1)
            split_ctx(later(first, 1))
            run_steps(e, K.units, step)

        def cross_dve(e, K):
            def full(u, name, kind="full"):
                bank, before = K.banks.at(u, name, kind)
                wait(e, C.pj_full[bank], before + 1)
                return bank

            def ln_statistics(v):
                wait(e, C.x_in[parity(v)], total_of_parity(v, 16 * K.nt, 16 * K.nt))
                for t in range(K.nt):
                    nc.vector.bn_stats(stats[0:K.tp, t, :], cx[0:K.tp, parity(v), t, :]) \
                        .then_inc(C.stats, 1)

            def ln_normalise(v):
                for t in range(K.nt):
                    nc.vector.bn_aggr(mean_var[0:K.tp, t, :], stats[0:K.tp, t, :]) \
                        .then_inc(C.agg, 1)
                for t in range(K.nt):
                    wait(e, C.rstd, total(v, K.nt, t + 1))
                    nc.vector.tensor_scalar(cxn[0:K.tp, t, :], cx[0:K.tp, parity(v), t, :],
                                            mean_var[0:K.tp, t, 0:1], rstd[0:K.tp, t, :],
                                            ALU.subtract, ALU.mult).then_inc(C.xn, 1)

            def x_lo(u, v, t):
                bank = full(u, f"X{t}")
                wait(e, C.xt_hi, total(v, K.nt, t + 1))
                nc.vector.tensor_tensor(
                    cxt_lo[:, :, t * P:t * P + K.tp],
                    PJ[bank][:].rearrange("p (c s) -> p c s", c=DC)[:, :, 0:K.tp],
                    cxt_hi[:, :, t * P:t * P + K.tp].bitcast(F32),
                    ALU.subtract).then_inc(C.pj_free[bank], 1)

            def a_lo(u, t):
                wait(e, C.at_hi, total(u, K.nt, t + 1))
                nc.vector.tensor_tensor(cat_lo[:, :, 0:K.tp], K.attended_t(t),
                                        cat_hi[:, :, 0:K.tp].bitcast(F32),
                                        ALU.subtract).then_inc(C.at_lo, 1)

            def values_out(u, v, j):
                bank = full(u, f"V{j}")
                nc.vector.tensor_copy(cv[:, parity(v), j, :], PJ[bank][:]) \
                    .then_inc(C.pj_free[bank], 1)

            groups, n_keys = PAIRS // K.kt, K.kt * P

            def maxima(u, q):
                rows = lambda a: a[:].rearrange("p (g k) -> p g k", g=groups)
                wait(e, C.s_full, total(u, 4, q + 1))
                nc.vector.tensor_tensor(
                    rows(c_s[q % 2]), rows(S),
                    mask_bias[:, KEYS - n_keys:KEYS].unsqueeze(1).to_broadcast([P, groups, n_keys]),
                    ALU.add).then_inc(C.s_free, 1)
                wait(e, C.s_free, total(u, 4, q + 1))
                row_bias(e, C, lambda k: total(u, 4, q + k), q % 2, groups, rows(c_s[q % 2]))

            def divide(u, q):
                divide_by_sums(e, C, lambda k: total(u, 4, q + k), groups, c_p)

            def residual(u, t, kind):
                bank = full(u, f"O{t}", kind)
                nc.vector.tensor_tensor(cx[0:K.tp, parity(u), t, :], PJ[bank][0:K.tp, :],
                                        cx[0:K.tp, parity(u), t, :], ALU.add) \
                    .then_inc(C.pj_free[bank], 1)

            def split_ctx(v):
                wait(e, ctx_hi_ready, total(v, 1, 1))
                flat = lambda a: a[:, parity(v)].rearrange("p j c k -> p (j c k)")
                nc.vector.tensor_tensor(flat(ctx_lo), flat(ctx_raw), flat(ctx_hi).bitcast(F32),
                                        ALU.subtract).then_inc(ctx_lo_ready, 1)

            def step(u, kind):
                more, ahead = kind != "last", kind == "full"
                v = later(u, 1)
                maxima(u, 0)
                if not is_unit(u, 0):
                    residual(later(u, -1), K.nt - 1, "last_but_one" if kind == "last" else "full")
                if not more:
                    maxima(u, 1)
                divide(u, 0)
                if more:
                    maxima(u, 1)
                    ln_statistics(v)
                    wait(e, C.stats, total(v, K.nt, K.nt))
                    nc.vector.tensor_copy(stats_seen[:], stats[0:1, 0, 0:1])
                    ln_normalise(v)
                else:
                    maxima(u, 2)
                divide(u, 1)
                if more:
                    maxima(u, 2)
                    for t in range(K.nt):
                        x_lo(u, v, t)
                else:
                    maxima(u, 3)
                divide(u, 2)
                if K.nt == 2:
                    a_lo(u, 0)
                if more:
                    values_out(u, v, 0)
                    maxima(u, 3)
                else:
                    self_w_lo(e, 0)
                if more:
                    values_out(u, v, 1)
                divide(u, 3)
                if more:
                    values_out(u, v, 2)
                else:
                    self_w_lo(e, 1)
                if K.nt == 2:
                    residual(u, 0, kind)
                if ahead:
                    split_ctx(later(u, 2))
                if not more:
                    self_ln_statistics(e, Unit(0, 0))
                    e.wait_ge(G.stats, NT)
                    self_ln_normalise(e, Unit(0, 0))
                a_lo(u, K.nt - 1)
                if more:
                    values_out(u, v, 3)
                else:
                    self_w_lo(e, 2)
                    residual(u, K.nt - 1, kind)

            first = Unit(0, 0)
            split_ctx(first)
            ln_statistics(first)
            e.wait_ge(C.stats, K.nt)
            cross_w_lo(e, 1)
            e.wait_ge(pads_ready, 2)
            ln_normalise(first)
            cross_w_lo(e, 2)
            for t in range(K.nt):
                x_lo(None, first, t)
            values_out(None, first, 0)
            values_out(None, first, 1)
            cross_w_lo(e, 3)
            values_out(None, first, 2)
            values_out(None, first, 3)
            split_ctx(later(first, 1))
            e.wait_ge(w_lo_ready, 4)
            run_steps(e, K.units, step)

        def rstd_of(e, agg, eps, done, v, per, rows):
            for t in range(per):
                wait(e, agg, total(v, per, t + 1))
                e.tensor_tensor(var_eps[0:rows, t, :], mean_var[0:rows, t, 1:2], ln_eps[0:rows, :],
                                ALU.add).then_inc(eps, 1)
                wait(e, eps, total(v, per, t + 1))
                e.tensor_tensor(rstd[0:rows, t, :], var_eps[0:rows, t, :], minus_half[0:rows, :],
                                ALU.pow).then_inc(done, 1)

        def cross_pool(e, K):
            def step(u, kind):
                more, ahead = kind != "last", kind == "full"
                if more:
                    rstd_of(e, C.agg, C.eps, C.rstd, later(u, 1), K.nt, K.tp)

            rstd_of(e, C.agg, C.eps, C.rstd, Unit(0, 0), K.nt, K.tp)
            run_steps(e, K.units, step)

        F_UNITS, FT, LEAD = TOKENS // (4 * P), 4, 2
        f_x2 = x2.rearrange("(u t p) d -> u t p d", t=FT, p=P)
        f_out = out.rearrange("(u t p) d -> u t p d", t=FT, p=P)
        W_SUMS = PV[:, 0, 0:2]
        flat_q = [t[:].rearrange("p a b -> p (a b)").rearrange("p (k n) -> p k n", n=512)
                  for t in (w1_q, w2_q)]

        def ff_ln_statistics(e, v):
            wait(e, fx_in[parity(v)], total_of_parity(v, 16 * FT, 16 * FT))
            for t in range(FT):
                nc.vector.bn_stats(stats[:, t, :], fx[:, parity(v), t, :]).then_inc(f_stats, 1)

        def ff_ln_aggregate(e):
            for t in range(FT):
                nc.vector.bn_aggr(mean_var[:, t, :], stats[:, t, :]).then_inc(f_agg, 1)

        def ff_ln_normalise(e, v, t):
            wait(e, f_rstd, total(v, FT, t + 1))
            wait(e, xb_full, total(v, FT, t - 1))
            nc.vector.tensor_scalar(fxn[:, t % 2, :], fx[:, parity(v), t, :],
                                    mean_var[:, t, 0:1], rstd[:, t, :],
                                    ALU.subtract, ALU.mult).then_inc(f_xn, 1)

        def ff_x_transpose(e, v, t):
            wait(e, xb_free, total(v, FT, t - 1))
            wait(e, f_xn, total(v, FT, t + 1))
            for c in range(DC):
                last = nc.tensor.transpose(XB[t % 2][:, c * P:c * P + P],
                                           fxn[:, t % 2, c * P:c * P + P], ident[:])
            last.then_inc(xb_full, 1)

        def ff_x_hi(e, v, t):
            wait(e, xb_full, total(v, FT, t + 1))
            nc.scalar.activation(fxt_hi[parity(v)][:, :, t * P:t * P + P],
                                 XB[t % 2].rearrange("p (c s) -> p c s", c=DC),
                                 ACT.Copy).then_inc(fxt_hi_ready, 1)

        def ff_x_lo(e, v, t):
            wait(e, fxt_hi_ready, total(v, FT, t + 1))
            nc.vector.tensor_tensor(fxt_lo[parity(v)][:, :, t * P:t * P + P],
                                    XB[t % 2].rearrange("p (c s) -> p c s", c=DC),
                                    fxt_hi[parity(v)][:, :, t * P:t * P + P].bitcast(F32),
                                    ALU.subtract).then_inc(xb_free, 1)

        LAST_TILE, ALL_TILES = Cross(1), Cross(KEY_TILES)

        block = outer.enter_context(nc.Block())

        s_full_uses = ["Q0", "Q1", "K0", "K1", "V0", "V1", "X0", "O0", "X1", "O1"]
        SB = Banks(["X0", "X1", "Q0", "Q1", "K0", "K1", "V0", "V1", "Y0", "Y1"], s_full_uses,
                   [n for n in s_full_uses if n[0] != "X"], [n for n in s_full_uses if n[0] == "O"])
        by_batch = lambda a: a[:].rearrange("p c (b s) -> p b c s", s=SEQ)
        s_attended_t = lambda t: (PV[:, :, 256 * t:256 * t + 256]
                                  .rearrange("p b (c s) -> p b c s", s=SEQ))
        SLOT = [(pair % 2) * 4 + pair // 2 for pair in range(PAIRS)]

        def self_sync(e):
            def step(u, kind):
                if kind == "full":
                    load_self_x(e, later(u, 2))
                elif kind == "last":
                    bank, before = SB.at(later(u, -1), "V1", "last_but_one")
                    wait(e, G.pj_free[bank], before + 1)
                    for i in range(2):
                        e.wait_ge(G.stored[i], 16 * NT * (S_UNITS // 2 - 1))
                    e.dma_start(b2_sb[:], b2.unsqueeze(0).to_broadcast([P, D])) \
                        .then_inc(ff_bias_in, 16)
                    for n in range(2):
                        for t in range(FT):
                            e.dma_start(fx[:, n, t, :], f_x2[n, t]).then_inc(fx_in[n], 16)
                if not is_unit(u, 0):
                    store(later(u, -1), 1, "last_but_one" if kind == "last" else "full")
                store(u, 0, kind)
                if kind == "last":
                    store(u, 1, kind)

            def store(u, t, kind):
                bank, before = SB.at(u, f"O{t}", kind)
                wait(e, G.pj_free[bank], before + 1)
                e.dma_start(s_x2[number(u), t], sres[:, parity(u), t, :]) \
                    .then_inc(G.stored[parity(u)], 16)

            for n, src in enumerate((w1, w2)):
                e.dma_start(w_raw[:, n].rearrange("p k n -> p (k n)"), src).then_inc(fw_in[n], 16)
            run_steps(e, S_UNITS, step)
            for i in range(2):
                e.wait_ge(G.stored[i], 16 * NT * S_UNITS // 2)

        def self_pe(e):
            def begin(u, name, kind="full"):
                bank, before = SB.at(u, name, kind)
                wait(e, G.pj_free[bank], before)
                return bank

            def x_transpose(u, v, t, name=None):
                bank = begin(u, name or f"X{t}")
                wait(e, G.xn, total(v, NT, t + 1))
                for c in range(DC):
                    last = nc.tensor.transpose(PJ[bank][:, c * P:c * P + P],
                                               sxn[:, t, c * P:c * P + P], ident[:])
                last.then_inc(G.pj_full[bank], 1)

            def qk_proj(u, name, w, kind="full", before_last=None):
                bank = begin(u, name, kind)
                n = int(name[1])
                for i in range(2):
                    cols = slice((2 * n + i) * P, (2 * n + i + 1) * P)
                    last = split_products(e, PJ[bank][:, 256 * i:256 * i + 256], [
                        (sw_hi[:, w, c, cols], sw_lo[:, w, c, cols], sxt_hi[:, c, :], sxt_lo[:, c, :])
                        for c in range(DC)], before_last if i else None)
                last.then_inc(G.pj_full[bank], 1)

            def v_proj(u, t, kind="full", before_last=None):
                bank = begin(u, f"V{t}", kind)
                rows = slice(t * P, t * P + P)
                split_products(e, PJ[bank][:], [
                    (sxt_hi[:, c, rows], sxt_lo[:, c, rows], sw_hi[:, 2, c, :], sw_lo[:, 2, c, :])
                    for c in range(DC)], before_last).then_inc(G.pj_full[bank], 1)

            def scores(u, t):
                wait(e, G.p_ready, total(u, NT, t))
                for r in (0, 2, 1, 3):
                    rows, half = slice(DK * r, DK * r + DK), SEQ * (r % 2)
                    for c in range(DC):
                        slot = SLOT[2 * c + r // 2]
                        for b in range(2):
                            col = slot * P + b * SEQ
                            last = nc.tensor.matmul(S[half:half + SEQ, col:col + SEQ],
                                                    sq_t[rows, parity(u), c, 2 * t + b, :],
                                                    sk_t[rows, parity(u), c, 2 * t + b, :],
                                                    start=True, stop=True)
                last.then_inc(G.s_full, 1)

            def transposes(u, t):
                wait(e, G.pt_ready, total(u, NT, t))
                wait(e, G.p_norm, total(u, NT, t + 1))
                for i in range(8):
                    last = nc.tensor.transpose(PT[:, i * P:i * P + P], s_p[:, i * P:i * P + P],
                                               ident[:])
                last.then_inc(G.pt_full, 1)

            def attend_waits(u, t):
                wait(e, G.at_lo, total(u, NT, t - 1))
                wait(e, G.pt_ready, total(u, NT, t + 1))

            def attend(u, t):
                for b in range(2):
                    keys = slice(SEQ * b, SEQ * b + SEQ)
                    for head in range(HEADS):
                        rows = slice(DK * (head % 4), DK * (head % 4) + DK)
                        col = (t * DC + head // 4) * SEQ
                        at = SLOT[head // 2] * P + SEQ * (head % 2)
                        last = nc.tensor.matmul(
                            PV[rows, b, col:col + SEQ],
                            sv[keys, parity(u), t, DK * head:DK * head + DK],
                            s_pt[keys, at:at + SEQ], start=True, stop=True)
                last.then_inc(G.pv_done, 1)

            def o_proj(u, t, kind):
                bank = begin(u, f"O{t}", kind)
                wait(e, G.at_lo, total(u, NT, t + 1))
                split_products(e, PJ[bank][:], [
                    (sat_hi[:, c, :], sat_lo[:, c, :], sw_hi[:, 3, c, :], sw_lo[:, 3, c, :])
                    for c in range(DC)]).then_inc(G.pj_full[bank], 1)

            def step(u, kind):
                more = kind != "last"
                scores(u, 0)
                if is_unit(u, 0):
                    e.wait_ge(sw_lo_ready, 4)
                    for bank in range(2):
                        e.wait_ge(G.pj_free[bank], SB.drained(bank))
                else:
                    o_proj(later(u, -1), 1, "last_but_one" if kind == "last" else "full")
                if more:
                    qk_proj(u, "Q0", 0, kind)
                    qk_proj(u, "Q1", 0, kind)
                scores(u, 1)
                transposes(u, 0)
                if more:
                    qk_proj(u, "K0", 1, kind, lambda: attend_waits(u, 0))
                else:
                    attend_waits(u, 0)
                attend(u, 0)
                if more:
                    qk_proj(u, "K1", 1, kind)
                    v_proj(u, 0, kind)
                transposes(u, 1)
                if more:
                    v_proj(u, 1, kind, lambda: attend_waits(u, 1))
                    if kind == "full":
                        x_transpose(u, later(u, 2), 0)
                    attend(u, 1)
                    o_proj(u, 0, kind)
                    if kind == "full":
                        x_transpose(u, later(u, 2), 1)
                else:
                    o_proj(u, 0, kind)
                    attend_waits(u, 1)
                    attend(u, 1)
                if is_unit(u, 1):
                    e.wait_ge(fw_abs, 1)
                    nc.tensor.matmul(W_SUMS, ones[:], abs_total[:], start=True, stop=True) \
                        .then_inc(fw_total, 1)
                    e.wait_ge(fw_thresh, 1)
                if kind == "last":
                    e.wait_ge(G.at_lo, NT * S_UNITS)
                    for t in range(2):
                        ff_x_transpose(e, Unit(0, 0), t)
                    o_proj(u, 1, kind)

            for t in range(NT):
                x_transpose(None, Unit(0, 0), t)
            e.wait_ge(sw_lo_ready, 3)
            for bank in range(2):
                e.wait_ge(G.pj_free[bank], 1)
            for n in range(2):
                qk_proj(None, f"Q{n}", 0)
            for n in range(2):
                qk_proj(None, f"K{n}", 1)
            for t in range(NT):
                v_proj(None, t)
            for t in range(NT):
                x_transpose(None, Unit(0, 1), t, f"Y{t}")
            run_steps(e, S_UNITS, step)

        def self_act(e):
            def full(u, name, kind="full"):
                bank, before = SB.at(u, name, kind)
                wait(e, G.pj_full[bank], before + 1)
                return bank

            def x_hi(u, v, t, name=None):
                bank = full(u, name or f"X{t}")
                nc.scalar.activation(sxt_hi[:, :, t * P:t * P + P],
                                     PJ[bank][:].rearrange("p (c s) -> p c s", c=DC),
                                     ACT.Copy).then_inc(G.xt_hi, 1)

            def a_hi(u, kind):
                full(u, "O0", kind)
                wait(e, G.pv_done, total(u, NT, NT))
                nc.scalar.activation(by_batch(sat_hi), s_attended_t(1), ACT.Copy) \
                    .then_inc(G.at_hi, 1)

            def qk_out(u, v, name, kind="full"):
                bank = full(u, name, kind)
                n = int(name[1])
                dst, bias = (sq_t, bq_sb) if name[0] == "Q" else (sk_t, bk_sb)
                for i in range(2):
                    last = nc.scalar.activation(
                        dst[:, parity(v), 2 * n + i, :, :].rearrange("p b s -> p (b s)"),
                        PJ[bank][:, 256 * i:256 * i + 256], ACT.Identity,
                        bias=bias[:, 2 * n + i:2 * n + i + 1])
                last.then_inc(G.pj_free[bank], 1)

            def exponentials(u, t):
                exponentials_of(e, G, lambda k: total(u, NT, t + k), t, HEADS, S, s_p)

            def probs_t_out(u, t):
                wait(e, G.pt_full, total(u, NT, t + 1))
                wait(e, G.pv_done, total(u, NT, t))
                nc.scalar.activation(s_pt[:], PT[:], ACT.Copy).then_inc(G.pt_ready, 1)

            def magnitudes(u, first, last):
                if not (is_unit(u, 0) or is_unit(u, 1)):
                    return
                w = u.off
                if first == 0:
                    e.wait_ge(fw_in[w], 16)
                for n in range(first, last):
                    wait(e, fw_summed, w * FC + n)
                    nc.scalar.activation(f_scratch[:], w_raw[:, w, n, :], ACT.Abs,
                                         accum_out=abs_sum[:, w, n:n + 1]).then_inc(fw_summed, 1)

            def step(u, kind):
                v, more = later(u, 1), kind != "last"
                exponentials(u, 0)
                magnitudes(u, 0, 3)
                if more:
                    qk_out(u, v, "Q0", kind)
                    qk_out(u, v, "Q1", kind)
                magnitudes(u, 3, 6)
                probs_t_out(u, 0)
                exponentials(u, 1)
                if more:
                    qk_out(u, v, "K0", kind)
                magnitudes(u, 6, 9)
                magnitudes(u, 9, 12)
                probs_t_out(u, 1)
                magnitudes(u, 12, 16)
                if kind == "full":
                    x_hi(u, later(u, 2), 0)
                a_hi(u, kind)
                if kind == "full":
                    x_hi(u, later(u, 2), 1)
                if kind == "last":
                    for t in range(2):
                        ff_x_hi(e, Unit(0, 0), t)

            e.wait_ge(self_bias_in, 80)
            e.wait_ge(sw_lo_ready, 3)
            for t in range(NT):
                x_hi(None, Unit(0, 0), t)
            qk_out(None, Unit(0, 0), "Q0")
            e.wait_ge(cross_w_used, 1)
            self_w_hi(e, 3)
            for name in ("Q1", "K0"):
                qk_out(None, Unit(0, 0), name)
            for t in range(NT):
                x_hi(None, Unit(0, 1), t, f"Y{t}")
            run_steps(e, S_UNITS, step)

        def self_dve(e):
            def full(u, name, kind="full"):
                bank, before = SB.at(u, name, kind)
                wait(e, G.pj_full[bank], before + 1)
                return bank

            def x_lo(u, v, t, name=None):
                bank = full(u, name or f"X{t}")
                wait(e, G.xt_hi, total(v, NT, t + 1))
                nc.vector.tensor_tensor(sxt_lo[:, :, t * P:t * P + P],
                                        PJ[bank][:].rearrange("p (c s) -> p c s", c=DC),
                                        sxt_hi[:, :, t * P:t * P + P].bitcast(F32),
                                        ALU.subtract).then_inc(G.pj_free[bank], 1)

            def a_hi(u):
                wait(e, G.pv_done, total(u, NT, 1))
                nc.vector.tensor_copy(by_batch(sat_hi), s_attended_t(0)).then_inc(G.at_hi, 1)

            def a_lo(u, t):
                wait(e, G.at_hi, total(u, NT, t + 1))
                nc.vector.tensor_tensor(by_batch(sat_lo), s_attended_t(t),
                                        by_batch(sat_hi).bitcast(F32), ALU.subtract) \
                    .then_inc(G.at_lo, 1)

            def keys_out(u, v, kind="full"):
                bank = full(u, "K1", kind)
                for i in range(2):
                    last = nc.vector.tensor_scalar(
                        sk_t[:, parity(v), 2 + i, :, :].rearrange("p b s -> p (b s)"),
                        PJ[bank][:, 256 * i:256 * i + 256], bk_sb[:, 2 + i:3 + i], None, ALU.add)
                last.then_inc(G.pj_free[bank], 1)

            def values_out(u, v, t, kind="full"):
                bank = full(u, f"V{t}", kind)
                nc.vector.tensor_tensor(sv[:, parity(v), t, :], PJ[bank][:], bv_sb[:],
                                        ALU.add).then_inc(G.pj_free[bank], 1)

            def maxima(u, t):
                wait(e, G.s_full, total(u, NT, t + 1))
                row_bias(e, G, lambda k: total(u, NT, t + k), t, HEADS,
                         S[:].rearrange("p (g k) -> p g k", g=HEADS))

            def divide(u, t):
                divide_by_sums(e, G, lambda k: total(u, NT, t + k), HEADS, s_p[:])

            def residual(u, t, kind):
                bank = full(u, f"O{t}", kind)
                if t == 0:
                    wait(e, G.res, total(u, NT, NT))
                nc.vector.tensor_tensor(sres[:, parity(u), t, :], PJ[bank][:],
                                        sres[:, parity(u), t, :], ALU.add) \
                    .then_inc(G.pj_free[bank], 1)

            def ternary(k, waits):
                for w in range(2):
                    wait(e, fw_ready, waits(w))
                    nc.vector.tensor_scalar(f_scratch[:], w_raw[:, w, k, :], thresh[:, 1, w:w + 1],
                                            None, ALU.is_lt).then_inc(fw_neg, 1)
                    wait(e, fw_neg, waits(w + 1))
                    nc.vector.scalar_tensor_tensor(flat_q[w][:, k, :], w_raw[:, w, k, :],
                                                   thresh[:, 0, w:w + 1],
                                                   f_scratch[:], ALU.is_gt, ALU.subtract) \
                        .then_inc(fw_ready, 1)

            def make_ternary(k):
                ternary(k, lambda n: 2 * k + n)

            def step(u, kind):
                v, more, w = later(u, 1), kind != "last", later(u, 2)
                maxima(u, 0)
                if not is_unit(u, 0):
                    residual(later(u, -1), 1, "last_but_one" if kind == "last" else "full")
                if kind == "full":
                    self_ln_statistics(e, w)
                    wait(e, G.stats, total(w, NT, NT))
                elif kind == "last_but_one":
                    make_ternary(S_UNITS - 4)
                    make_ternary(S_UNITS - 3)
                elif kind == "last":
                    ff_ln_statistics(e, Unit(0, 0))
                    e.wait_ge(f_stats, FT)
                    ff_ln_aggregate(e)
                divide(u, 0)
                if kind == "full":
                    self_ln_normalise(e, w)
                maxima(u, 1)
                if kind == "last_but_one":
                    make_ternary(S_UNITS - 2)
                a_hi(u)
                a_lo(u, 0)
                divide(u, 1)
                if more:
                    keys_out(u, v, kind)
                    values_out(u, v, 0, kind)
                    values_out(u, v, 1, kind)
                if kind == "full":
                    x_lo(u, w, 0)
                if kind == "full" and not (isinstance(u.half, int)):
                    ternary(number(u) - 2, lambda n: total(u, 2, n - 4))
                if kind == "last_but_one":
                    make_ternary(S_UNITS - 1)
                if kind == "last":
                    for t in range(2):
                        ff_ln_normalise(e, Unit(0, 0), t)
                residual(u, 0, kind)
                a_lo(u, 1)
                if kind == "full":
                    x_lo(u, w, 1)
                if is_unit(u, 1):
                    e.wait_ge(fw_summed, 2 * FC)
                    nc.vector.reduce_sum(abs_total[:], abs_sum[:], AXIS.X).then_inc(fw_abs, 1)
                    e.wait_ge(fw_total, 1)
                    nc.vector.tensor_scalar(thresh[:, 0, :], W_SUMS, 0.5 / (D * FF),
                                            0.5 * QUANT_EPS, ALU.mult, ALU.add) \
                        .then_inc(fw_thresh, 1)
                    e.wait_ge(fw_thresh, 1)
                    nc.vector.tensor_scalar(thresh[:, 1, :], thresh[:, 0, :], -1.0, None, ALU.mult) \
                        .then_inc(fw_thresh, 1)
                    e.wait_ge(fw_thresh, 2)
                if kind == "last":
                    for t in range(2):
                        ff_ln_normalise(e, Unit(0, 0), t + 2)
                        ff_x_lo(e, Unit(0, 0), t)
                    residual(u, 1, kind)

            for t in range(NT):
                x_lo(None, Unit(0, 0), t)
            self_ln_statistics(e, Unit(0, 1))
            e.wait_ge(G.stats, 2 * NT)
            self_ln_normalise(e, Unit(0, 1))
            self_w_lo(e, 3)
            e.wait_ge(self_bias_in, 80)
            keys_out(None, Unit(0, 0))
            for t in range(NT):
                values_out(None, Unit(0, 0), t)
            for t in range(NT):
                x_lo(None, Unit(0, 1), t, f"Y{t}")
            run_steps(e, S_UNITS, step)

        def self_pool(e):
            def residuals(v):
                wait(e, G.x_in[parity(v)], total_of_parity(v, 16 * NT, 16 * NT))
                wait(e, G.stored[parity(v)], total_of_parity(v, 16 * NT))
                for t in range(NT):
                    e.tensor_tensor(sres[:, parity(v), t, :], sx[:, parity(v), t, :], bo_sb[:],
                                    ALU.add).then_inc(G.res, 1)

            def step(u, kind):
                if kind != "last":
                    residuals(later(u, 1))
                if kind == "full":
                    rstd_of(e, G.agg, G.eps, G.rstd, later(u, 2), NT, P)

            rstd_of(e, G.agg, G.eps, G.rstd, Unit(0, 0), NT, P)
            rstd_of(e, G.agg, G.eps, G.rstd, Unit(0, 1), NT, P)
            e.wait_ge(self_bias_in, 80)
            e.wait_ge(sw_lo_ready, 4)
            residuals(Unit(0, 0))
            run_steps(e, S_UNITS, step)


        def ff_sync(e):
            def step(u, kind):
                if kind == "full":
                    w = later(u, 2)
                    wait(e, f_xn, total(u, FT, FT))
                    wait(e, f_res, total(u, FT, FT))
                    for t in range(FT):
                        e.dma_start(fx[:, parity(w), t, :], f_x2[number(w), t]) \
                            .then_inc(fx_in[parity(w)], 16)
                for t in range(FT):
                    wait(e, y_new[t], total(u, 1, 1))
                    e.dma_start(f_out[number(u), t], fres[:, parity(u), t, :]) \
                        .then_inc(f_stored[parity(u)], 16)

            run_steps(e, F_UNITS, step)
            for i in range(2):
                e.wait_ge(f_stored[i], 16 * FT * F_UNITS // 2)

        def ff_pe(e):
            def hidden(v, m):
                wait(e, h_relu, total(v, FC, m - 1))
                if m == 0:
                    wait(e, xb_free, total(v, FT, FT))
                cols = slice(m * P, m * P + P)
                for c in range(DC):
                    for x_t in (fxt_hi, fxt_lo):
                        last = nc.tensor.matmul(PJ[m % 2][:], w1_q[:, c, cols],
                                                x_t[parity(v)][:, c, :],
                                                start=(c == 0 and x_t is fxt_hi),
                                                stop=(c == DC - 1 and x_t is fxt_lo))
                last.then_inc(h_full, 1)

            def contract(u, m):
                wait(e, h_lo_ready, total(u, FC, m + 1))
                for t in range(FT):
                    if m == 0:
                        wait(e, y_new[t], total(u, 1))
                    rows = slice(t * P, t * P + P)
                    nc.tensor.matmul(YB[t], h_hi[:, m % 4, rows], w2_q[:, m, :],
                                     start=(m == 0), stop=False)
                    last = nc.tensor.matmul(YB[t], h_lo[:, m % 4, rows], w2_q[:, m, :],
                                            start=False, stop=(m == FC - 1))
                    if m == FC - 1:
                        last.then_inc(y_full[t], 1)
                    elif t == FT - 1:
                        last.then_inc(y_m, 1)

            def step(u, kind):
                v, more = later(u, 1), kind != "last"
                for m in range(FC):
                    if m + LEAD < FC:
                        hidden(u, m + LEAD)
                    elif more:
                        hidden(v, m + LEAD - FC)
                    contract(u, m)
                    if more and m in (3, 5, 7, 9):
                        ff_x_transpose(e, v, (m - 3) // 2)

            for t in range(2, FT):
                ff_x_transpose(e, Unit(0, 0), t)
            e.wait_ge(fw_ready, 2 * FC)
            bank, before = SB.at(Unit(S_UNITS // 2 - 1, 1), "O1", "last")
            e.wait_ge(G.pj_free[bank], before + 1)
            for m in range(LEAD):
                hidden(Unit(0, 0), m)
            run_steps(e, F_UNITS, step)

        def ff_act(e):
            def relu(v, m):
                wait(e, h_full, total(v, FC, m + 1))
                wait(e, h_lo_ready, total(v, FC, m - 1))
                nc.scalar.activation(h_raw[:, m % 2, :], PJ[m % 2][:], ACT.Relu,
                                     bias=b1_sb[:, m:m + 1]).then_inc(h_relu, 1)

            def step(u, kind):
                v, more = later(u, 1), kind != "last"
                for m in range(FC):
                    if m + LEAD < FC:
                        relu(u, m + LEAD)
                    elif more:
                        relu(v, m + LEAD - FC)
                    if more and m in (3, 5, 7, 9):
                        ff_x_hi(e, v, (m - 3) // 2)

            for t in range(2, FT):
                ff_x_hi(e, Unit(0, 0), t)
            for m in range(LEAD):
                relu(Unit(0, 0), m)
            for i in range(2):
                e.wait_ge(G.stored[i], 16 * NT * S_UNITS // 2)
            run_steps(e, F_UNITS, step)

        def ff_dve(e):
            def split_hidden(v, m):
                wait(e, h_relu, total(v, FC, m + 1))
                nc.vector.tensor_copy(h_hi[:, m % 4, :], h_raw[:, m % 2, :]).then_inc(h_hi_ready, 1)
                wait(e, h_hi_ready, total(v, FC, m + 1))
                nc.vector.tensor_tensor(h_lo[:, m % 4, :], h_raw[:, m % 2, :],
                                        h_hi[:, m % 4, :].bitcast(F32),
                                        ALU.subtract).then_inc(h_lo_ready, 1)

            def step(u, kind):
                v, more = later(u, 1), kind != "last"
                for m in range(FC):
                    if more and m == 1:
                        wait(e, f_stats, total(v, FT, FT))
                    if m + LEAD < FC:
                        split_hidden(u, m + LEAD)
                    elif more:
                        split_hidden(v, m + LEAD - FC)
                    if more:
                        if m == 0:
                            ff_ln_statistics(e, v)
                        if m == 1:
                            ff_ln_aggregate(e)
                        if m in (2, 4, 6, 8):
                            ff_ln_normalise(e, v, (m - 2) // 2)
                        if m in (3, 5, 7, 9):
                            ff_x_lo(e, v, (m - 3) // 2)
                for t in range(FT):
                    wait(e, y_full[t], total(u, 1, 1))
                    if t == 0:
                        wait(e, f_res, total(u, FT, FT))
                    nc.vector.tensor_tensor(fres[:, parity(u), t, :], YB[t],
                                            fres[:, parity(u), t, :], ALU.add) \
                        .then_inc(y_new[t], 1)

            first = Unit(0, 0)
            for t in range(2, FT):
                ff_x_lo(e, first, t)
            for m in range(LEAD):
                split_hidden(first, m)
            run_steps(e, F_UNITS, step)

        def ff_pool(e):
            def residuals(v):
                wait(e, fx_in[parity(v)], total_of_parity(v, 16 * FT, 16 * FT))
                wait(e, f_stored[parity(v)], total_of_parity(v, 16 * FT))
                for t in range(FT):
                    e.tensor_tensor(fres[:, parity(v), t, :], fx[:, parity(v), t, :], b2_sb[:],
                                    ALU.add).then_inc(f_res, 1)

            def step(u, kind):
                if kind != "last":
                    rstd_of(e, f_agg, f_eps, f_rstd, later(u, 1), FT, P)
                    residuals(later(u, 1))

            rstd_of(e, f_agg, f_eps, f_rstd, Unit(0, 0), FT, P)
            e.wait_ge(ff_bias_in, 16)
            residuals(Unit(0, 0))
            run_steps(e, F_UNITS, step)

        def choose(e, program):
            e.wait_ge(flag_ready, 1)
            only_last = e.value_load(flag_i[0:1, 0:1], min_val=0, max_val=1)
            with e.If(only_last):
                program(e, LAST_TILE)
                e.nop()
            with e.Else():
                program(e, ALL_TILES)
                e.nop()

        @block.sync
        def _(e):
            m = mask.rearrange("a b s k -> (a b s) k")
            for half in range(2):
                e.dma_start(mask_u8[SEQ * half:SEQ * half + SEQ, :], m).then_inc(mask_in, 16)
            load_cross_w(e, 0)
            choose(e, cross_sync)
            self_sync(e)
            ff_sync(e)

        @block.gpsimd
        def _(e):
            e.memset(ident[:], 0.0).then_inc(const_ready, 1)
            e.memset(ones[:], 1.0).then_inc(const_ready, 1)
            e.memset(minus_half[:], -0.5).then_inc(const_ready, 1)
            e.memset(ln_eps[:], LN_EPS).then_inc(const_ready, 1)
            e.wait_ge(const_ready, 4)
            e.affine_select(out=ident[:], in_=ident[:], compare_op=ALU.not_equal, fill=1.0, base=0,
                            pattern=[[-1, P]], channel_multiplier=1).then_inc(const_ready, 1)
            e.memset(q_pad[:].rearrange("p c a b h s -> p (c a b h s)"), 0.0).then_inc(pads_ready, 1)
            e.memset(cxn[:].rearrange("p t d -> p (t d)"), 0.0).then_inc(pads_ready, 1)
            choose(e, cross_pool)
            self_pool(e)
            ff_pool(e)

        @block.scalar
        def _(e):
            cross_w_hi(e, 0)
            choose(e, cross_act)
            self_act(e)
            ff_act(e)

        @block.vector
        def _(e):
            e.wait_ge(mask_in, 32)
            nc.vector.tensor_copy(mask_f, mask_u8[:]).then_inc(mask_step, 1)
            e.wait_ge(mask_step, 1)
            nc.vector.reduce_sum(counts[:, 0:1], mask_f, AXIS.X)
            nc.vector.reduce_sum(counts[:, 1:2], mask_f[:, 0:KEYS - P], AXIS.X).then_inc(mask_step, 1)
            e.wait_ge(mask_step, 2)
            nc.vector.tensor_scalar(counts[:, 2:3], counts[:, 0:1], -1.0, float(KEYS),
                                    ALU.mult, ALU.add).then_inc(mask_step, 1)
            e.wait_ge(mask_step, 3)
            nc.vector.reciprocal(counts[:, 3:4], counts[:, 2:3]).then_inc(mask_step, 1)
            e.wait_ge(mask_step, 4)
            nc.vector.tensor_scalar(counts[:, 2:3], counts[:, 3:4], 0.0, None, ALU.mult) \
                .then_inc(mask_step, 1)
            e.wait_ge(mask_step, 5)
            nc.vector.tensor_scalar(mask_bias[:], mask_f, MASKED, counts[:, 2:3],
                                    ALU.mult, ALU.add).then_inc(mask_step, 1)
            e.wait_ge(mask_counted, 1)
            nc.vector.tensor_scalar(flag_i[0:1, 0:1], S[0:1, 0:1], float(P * (KEYS - P)), None,
                                    ALU.is_ge).then_inc(flag_ready, 1)
            cross_w_lo(e, 0)
            e.wait_ge(mask_step, 6)
            choose(e, cross_dve)
            self_dve(e)
            ff_dve(e)

        @block.tensor
        def _(e):
            e.wait_ge(const_ready, 5)
            e.wait_ge(mask_step, 2)
            nc.tensor.matmul(S[0:1, 0:2], counts[:, 1:2], ones[:, 0:2], start=True, stop=True) \
                .then_inc(mask_counted, 1)
            e.wait_ge(flag_ready, 1)
            choose(e, cross_pe)
            self_pe(e)
            ff_pe(e)


def tiled(w):
    import numpy as np
    t = np.ascontiguousarray(w.T)
    return np.ascontiguousarray(t.reshape(t.shape[0] // 128, 128, t.shape[1]).transpose(1, 0, 2)) \
        .reshape(128, -1)


def kernel(x, ctx_1024, mask_1x1xSxS2_bk1, L0_xattn_W_Q, L0_xattn_W_K, L0_xattn_W_V, L0_xattn_W_O,
           L0_attn_Wq, L0_attn_bq, L0_attn_Wk, L0_attn_bk, L0_attn_Wv, L0_attn_bv, L0_attn_Wo,
           L0_attn_bo, L0_ffn_W1, L0_ffn_b1, L0_ffn_W2, L0_ffn_b2):
    import numpy as np
    import concourse.bacc as bacc
    from concourse.bass_utils import run_bass_kernel_spmd

    a = np.asarray
    ctx = np.ascontiguousarray(a(ctx_1024).reshape(BATCHES, KEY_TILES, P, DC, P)
                               .transpose(0, 1, 4, 3, 2)).reshape(BATCHES, KEY_TILES, P, DC * P)
    arrays = {
        "x": a(x).reshape(TOKENS, D),
        "ctx": ctx,
        "mask": a(mask_1x1xSxS2_bk1),
        "w_cross": np.stack([tiled(a(w)) for w in
                             (L0_xattn_W_Q, L0_xattn_W_K, L0_xattn_W_V, L0_xattn_W_O)]),
        "w_self": np.stack([tiled(a(w)) for w in
                            (L0_attn_Wq, L0_attn_Wk, L0_attn_Wv, L0_attn_Wo)]),
        "bq": np.ascontiguousarray(a(L0_attn_bq).reshape(DC, P).T),
        "bk": np.ascontiguousarray(a(L0_attn_bk).reshape(DC, P).T),
        "bv": a(L0_attn_bv),
        "bo": a(L0_attn_bo),
        "w1": tiled(a(L0_ffn_W1)),
        "b1": np.ascontiguousarray(a(L0_ffn_b1).reshape(FC, P).T),
        "w2": tiled(a(L0_ffn_W2)),
        "b2": a(L0_ffn_b2),
    }
    nc = bacc.Bacc("TRN2", target_bir_lowering=False, num_devices=1)
    args = [nc.dram_tensor(f"in_{n}", v.shape, mybir.dt.from_np(v.dtype), kind="ExternalInput").ap()
            for n, v in arrays.items()]
    out = nc.dram_tensor("out", (TOKENS, D), F32, kind="ExternalOutput").ap()
    build(nc, *args, out)
    result = run_bass_kernel_spmd(nc, [{f"in_{n}": v for n, v in arrays.items()}], core_ids=[0])
    return np.asarray(result.results[0]["out"]).reshape(BATCHES, SEQ, D)
```
